# Optimizing a Trainium2 kernel written in Bass

```python
import numpy as np
import jax
import jax.numpy as jnp

def _softmax(x, axis=-1):
    return jax.nn.softmax(x, axis=axis)

def _gelu(x):
    return jax.nn.gelu(x, approximate=True)

def _silu(x):
    return jax.nn.silu(x)

def _sigmoid(x):
    return jax.nn.sigmoid(x)

def _layernorm(x, axis=-1, eps=1e-05):
    m = jnp.mean(x, axis=axis, keepdims=True)
    v = jnp.var(x, axis=axis, keepdims=True)
    return (x - m) / jnp.sqrt(v + eps)

def _scatter_add(tgt, idx, src, axis=0):
    return tgt.at[idx].add(src)

def _segment_sum(src, seg, n):
    return jax.ops.segment_sum(src, seg, n)
kernel_name = 'mk_gps_d1_gnn_r8_930cc9'

def setup_inputs(seed: int=0):
    np.random.seed(seed)
    _w = jnp.asarray

    def _rec_inputs():
        import jax
        import jax.numpy as jnp
        _gk = jax.random.key(seed)
        x = -7.329e-05 + 0.9999 * jax.random.normal(jax.random.fold_in(_gk, 1), (1250, 512), jnp.float32)
        _s = jax.random.randint(jax.random.fold_in(_gk, 2), (20000,), 0, 1250, jnp.int32)
        _d = jax.random.randint(jax.random.fold_in(_gk, 3), (20000,), 0, 1250, jnp.int32)
        _loop = jnp.arange(1250, dtype=jnp.int32)
        src = jnp.concatenate([_s, _d, _loop])
        dst = jnp.concatenate([_d, _s, _loop])
        _o = jnp.argsort(dst, stable=True)
        src = src[_o]
        dst = dst[_o]
        edge_weight = jax.random.uniform(jax.random.fold_in(_gk, 12), (41250,), jnp.float32, 0.0, 0.999998)
        return (x, src, dst, edge_weight)
    x, src, dst, edge_weight = _rec_inputs()

    def _L0_gnn_setup():
        import jax, jax.numpy as jnp
        import numpy as np
        N_NODES = 12500
        N_EDGES = 50000
        IN_FT = 512
        OUT_FT = 512
        key = jax.random.key(seed)
        k_feat, k_ei, k_ew, k_w, k_a = jax.random.split(key, 5)
        feat = jax.random.normal(k_feat, (N_NODES, IN_FT), dtype=jnp.float32)
        edge_index = jax.random.randint(k_ei, (2, N_EDGES), 0, N_NODES, dtype=jnp.int64)
        edge_weight = jax.random.uniform(k_ew, (N_EDGES,), dtype=jnp.float32)
        bound = float(np.sqrt(6.0 / (IN_FT + OUT_FT)))
        W = jax.random.uniform(k_w, (OUT_FT, IN_FT), dtype=jnp.float32, minval=-bound, maxval=bound)
        alpha = jnp.array(0.25, dtype=jnp.float32)
        return {'feat': feat, 'edge_index': edge_index, 'edge_weight': edge_weight, 'num_nodes': N_NODES, 'W': W, 'alpha': alpha}
    _L0_gnn_all = _L0_gnn_setup()
    _L0_gnn_in = {k: v for k, v in _L0_gnn_all.items() if k in ('W', 'alpha')}
    del _L0_gnn_all

    def _L0_mix_setup():
        import jax, jax.numpy as jnp
        import numpy as np
        B, S, H = (4, 1024, 512)
        NH, HD = (8, 64)
        FD = HD // 2
        key = jax.random.key(seed)
        k1, k2, k3, k4 = jax.random.split(key, 4)
        x = jax.random.normal(k1, (B, S, H), dtype=jnp.float32)
        W_qkv = jax.random.normal(k2, (H, 3 * H), dtype=jnp.float32) * (1.0 / np.sqrt(H))
        random_matrix = jax.random.normal(k3, (HD, FD), dtype=jnp.float32) * (1.0 / np.sqrt(HD))
        W_out = jax.random.normal(k4, (H, H), dtype=jnp.float32) * (1.0 / np.sqrt(H))
        b_out = jnp.zeros((H,), dtype=jnp.float32)
        return {'x': x, 'W_qkv': W_qkv, 'random_matrix': random_matrix, 'W_out': W_out, 'b_out': b_out}
    _L0_mix_all = _L0_mix_setup()
    _L0_mix_in = {k: v for k, v in _L0_mix_all.items() if k in ('W_qkv', 'random_matrix', 'W_out', 'b_out')}
    del _L0_mix_all

    def _L0_ffn_setup():
        import jax, jax.numpy as jnp
        import numpy as np
        DIM = 512
        NE = 8
        TOPK = 2
        CF = 1.2
        HID = 4 * DIM
        B, S = (8, 512)
        key = jax.random.key(seed)
        ks = jax.random.split(key, 4)
        s = 0.02
        return {'x': jax.random.normal(ks[0], (B, S, DIM), jnp.float32), 'gate_w': jax.random.normal(ks[1], (NE, DIM), jnp.float32) * s, 'gate_b': jnp.zeros((NE,), jnp.float32), 'w1': jax.random.normal(ks[2], (NE, DIM, HID), jnp.float32) * s, 'b1': jnp.zeros((NE, HID), jnp.float32), 'w2': jax.random.normal(ks[3], (NE, HID, DIM), jnp.float32) * s, 'b2': jnp.zeros((NE, DIM), jnp.float32)}
    _L0_ffn_all = _L0_ffn_setup()
    _L0_ffn_in = {k: v for k, v in _L0_ffn_all.items() if k in ('gate_w', 'gate_b', 'w1', 'b1', 'w2', 'b2')}
    del _L0_ffn_all
    return {'x': x, 'src': src, 'dst': dst, 'edge_weight': edge_weight, 'L0_gnn_W': _L0_gnn_in['W'], 'L0_gnn_alpha': _L0_gnn_in['alpha'], 'L0_mix_W_qkv': _L0_mix_in['W_qkv'], 'L0_mix_random_matrix': _L0_mix_in['random_matrix'], 'L0_mix_W_out': _L0_mix_in['W_out'], 'L0_mix_b_out': _L0_mix_in['b_out'], 'L0_ffn_gate_w': _L0_ffn_in['gate_w'], 'L0_ffn_gate_b': _L0_ffn_in['gate_b'], 'L0_ffn_w1': _L0_ffn_in['w1'], 'L0_ffn_b1': _L0_ffn_in['b1'], 'L0_ffn_w2': _L0_ffn_in['w2'], 'L0_ffn_b2': _L0_ffn_in['b2']}

def reference(x, src, dst, edge_weight, L0_gnn_W, L0_gnn_alpha, L0_mix_W_qkv, L0_mix_random_matrix, L0_mix_W_out, L0_mix_b_out, L0_ffn_gate_w, L0_ffn_gate_b, L0_ffn_w1, L0_ffn_b1, L0_ffn_w2, L0_ffn_b2):
    import jax
    import jax.numpy as jnp

    def _L0_gnn_ref(feat, edge_index, edge_weight, num_nodes, W, alpha):
        import jax, jax.numpy as jnp
        import numpy as np
        N_NODES = 12500
        N_EDGES = 50000
        IN_FT = 512
        OUT_FT = 512
        h = jnp.einsum('ni,oi->no', feat, W)
        row, col = (edge_index[0], edge_index[1])
        msgs = h[row] * edge_weight[:, None]
        out = jax.ops.segment_sum(msgs, col, num_segments=num_nodes)
        return jnp.where(out >= 0, out, alpha * out)

    def _L0_mix_ref(x, W_qkv, random_matrix, W_out, b_out):
        import jax, jax.numpy as jnp
        import numpy as np
        B, S, H = (4, 1024, 512)
        NH, HD = (8, 64)
        FD = HD // 2
        b, s, h = x.shape
        qkv = (x @ W_qkv).reshape(b, s, 3, NH, HD)
        q, k, v = (qkv[:, :, 0], qkv[:, :, 1], qkv[:, :, 2])
        q_prime = jax.nn.elu(q @ random_matrix) + 1.0
        k_prime = jax.nn.elu(k @ random_matrix) + 1.0
        kv = jnp.einsum('bshd,bshf->bhdf', k_prime, v)
        z = jnp.einsum('bshd,bhdf->bshf', q_prime, kv)
        normalizer = jnp.einsum('bshd,bhd->bsh', q_prime, k_prime.sum(axis=1))
        z = z / (normalizer[..., None] + 1e-06)
        z = z.reshape(b, s, h)
        return z @ W_out + b_out

    def _L0_ffn_ref(x, gate_w, gate_b, w1, b1, w2, b2):
        import jax, jax.numpy as jnp
        import numpy as np
        DIM = 512
        NE = 8
        TOPK = 2
        CF = 1.2
        HID = 4 * DIM
        B, S = (8, 512)
        Bq, Sq, D = x.shape
        T = Bq * Sq
        cap = int(CF * T / NE)
        xf = x.reshape(T, D)
        probs = jax.nn.softmax(xf @ gate_w.T + gate_b, axis=-1)
        topw, topi = jax.lax.top_k(probs, TOPK)
        onehot = jax.nn.one_hot(topi, NE, dtype=topw.dtype)
        w_te = jnp.einsum('tk,tke->te', topw, onehot)
        routed = onehot.sum(axis=1) > 0
        wm = jnp.where(routed, w_te, -1.0)
        sel_w, sel_idx = jax.lax.top_k(wm.T, cap)
        sel_w = jnp.maximum(sel_w, 0.0)
        xg = xf[sel_idx]
        h = jax.nn.gelu(jnp.einsum('ecd,edh->ech', xg, w1) + b1[:, None, :], approximate=False)
        out = jnp.einsum('ech,ehd->ecd', h, w2) + b2[:, None, :]
        weighted = out * sel_w[..., None]
        of = jnp.zeros((T, D), x.dtype).at[sel_idx.reshape(-1)].add(weighted.reshape(-1, D))
        return of.reshape(Bq, Sq, D)
    edge_index = jnp.stack([src, dst])
    xn = _layernorm(x, axis=-1)
    x = x + _L0_gnn_ref(xn, edge_index, edge_weight, 1250, L0_gnn_W, L0_gnn_alpha) + _L0_mix_ref(xn[None], L0_mix_W_qkv, L0_mix_random_matrix, L0_mix_W_out, L0_mix_b_out)[0]
    x = x + _L0_ffn_ref(_layernorm(x, axis=-1)[None], L0_ffn_gate_w, L0_ffn_gate_b, L0_ffn_w1, L0_ffn_b1, L0_ffn_w2, L0_ffn_b2)[0]
    return x

_drawn_inputs = setup_inputs


def setup_inputs(seed=0):
    import zlib

    import numpy as np

    out = dict(_drawn_inputs(seed))
    spreads = {'L0_mix_b_out': (0.0, 0.1),
     'L0_ffn_gate_b': (0.0, 0.8),
     'L0_ffn_b1': (0.0, 0.8),
     'L0_ffn_b2': (0.0, 0.8)}
    factors = {'L0_mix_W_qkv': 5.422, 'L0_mix_random_matrix': 8.0, 'L0_mix_W_out': 4.92}
    for name, (base, spread) in spreads.items():
        noise = np.random.default_rng([zlib.crc32(name.encode()), seed]).standard_normal(out[name].shape)
        drawn = base * np.exp(spread * noise) if base else spread * noise
        out[name] = jnp.asarray(drawn.astype(out[name].dtype))
    for name, factor in factors.items():
        out[name] = (out[name] * factor).astype(out[name].dtype)
    return out
```

```python
from contextlib import ExitStack

import concourse.bass as bass
from concourse import mybir

ALU = mybir.AluOpType
ACT = mybir.ActivationFunctionType
AX_X = mybir.AxisListType.X
F32 = mybir.dt.float32
F32R = mybir.dt.float32r
BF16 = mybir.dt.bfloat16
I32 = mybir.dt.int32
U32 = mybir.dt.uint32
P = 128


class Chain:

    def __init__(self, eng, sem):
        self.eng, self.sem, self.n = eng, sem, 0

    def __call__(self, ins):
        ins.then_inc(self.sem, 1)
        self.n += 1
        self.eng.wait_ge(self.sem, self.n)


class Region:

    def __init__(self, nc, start):
        self.nc, self.at = nc, -(-start // 32) * 32

    def __call__(self, name, shape, dt=F32):
        t = self.nc.alloc_sbuf_tensor_at(name, shape, dt, offset=self.at)
        size = mybir.dt.size(dt)
        for n in shape[1:]:
            size *= n
        self.at += -(-size // 32) * 32
        assert self.at <= self.nc.sbuf_usable_end, (name, self.at, self.nc.sbuf_usable_end)
        return t


def ds(start, size):
    return bass.ds(start, size)


def gps_layer(nc, x, src, dst, edge_weight, gnn_W, gnn_alpha, W_qkv, R_feat, W_out, b_out,
              gate_w, gate_b, w1, b1, w2, b2, out):
    N, D = x.shape
    E = src.shape[0]
    HD, FD = R_feat.shape
    NH = D // HD
    NE, _, HID = w1.shape
    TOPK = 2
    CAP = int(1.2 * N / NE)
    EPS = 1e-5

    TP = 125
    T = N // TP
    KD = D // P
    NF = NH * FD
    assert T * TP == N and TOPK == 2

    GC, WIN = 3, 16
    GE = GC * P
    G = -(-E // GE)
    TAIL = E - (G - 1) * GE
    KEYS = T * WIN
    RING = 3
    GPI = 9
    TURNS = G // GPI
    assert TURNS * GPI == G and GPI % RING == 0 and TURNS > T
    NWIN = -(-N // WIN)
    AW = NWIN * WIN + WIN

    SLOTS = 188
    SB2 = SLOTS // 2
    TRASH = (NE + 1) * SLOTS
    HT = HID // P
    CH = 4
    NCH = HT // CH
    assert SLOTS >= CAP and CH == KD

    xg_rows = nc.dram_tensor("xg_rows", (TRASH + TOPK * N, D), F32, kind="Internal").ap()
    y_rows = nc.dram_tensor("y_rows", (NE * SLOTS, D), F32, kind="Internal").ap()


    ctx = ExitStack()
    with ctx:
        def sem(name):
            return ctx.enter_context(nc.semaphore(name))

        bank = [ctx.enter_context(nc.psum_tensor(f"bank{i}", [P, 512], F32)) for i in range(8)]

        keep = Region(nc, nc.sbuf_base)
        X = keep("X", [TP, T, D])
        ident = keep("ident", [P, P])
        ones_f = keep("ones_f", [P, 1])
        ones_b = keep("ones_b", [TP, TP], BF16)
        tri_b = keep("tri_b", [TP, TP], BF16)
        b1T = keep("b1T", [P, NE * HT])
        b2T = keep("b2T", [P, NE * KD])
        gwT = keep("gwT", [P, KD, NE])
        gate_b_all = keep("gate_b_all", [TP, NE])
        stats = keep("stats", [TP, 2, 6])
        mv = keep("mv", [TP, T, 2])
        sd = keep("sd", [TP, T])
        rstd = keep("rstd", [TP, T])
        eps_c = keep("eps_c", [TP, 1])
        scat_idx = keep("scat_idx", [TP, TOPK * T], U32)
        gath_idx = keep("gath_idx", [TP, TOPK * T], U32)
        comb_w = keep("comb_w", [TP, TOPK * T])

        graph = Region(nc, keep.at)
        A = graph("A", [TP, T, AW])
        Wcat = graph("Wcat", [P, KD, 2 * D + NF])
        Mq = graph("Mq", [P, KD, NF])
        Wo = graph("Wo", [P, KD, D])
        alpha_neg = graph("alpha_neg", [TP, 1])
        bo_all = graph("bo_all", [TP, D])
        iota_r = graph("iota_r", [P, P])
        iota_k = graph("iota_k", [P, KEYS])
        col_r = graph("col_r", [P, G, GC])
        col_key = graph("col_key", [P, G, GC])
        col_w = graph("col_w", [P, G, GC, 2])
        col_blk = graph("col_blk", [P, G, GC])
        col_dst = graph("col_dst", [P, G, GC])
        first_dst = graph("first_dst", [1, G], I32)
        flag = graph("flag", [1, 1], I32)
        KV = graph("KV", [P, 2, 260])

        shared = graph.at
        H = graph("H", [TP, T, D])
        QT = graph("QT", [P, 2, N])
        xnT = graph("xnT", [P, KD, TP])
        V = graph("V", [TP, D])
        Kf = graph("Kf", [TP, NF])
        k_min = graph("k_min", [TP, NF])
        k_exp = graph("k_exp", [TP, NF])
        q_min = graph("q_min", [P, 2 * TP])
        q_exp = graph("q_exp", [P, 2 * TP])
        late = max(graph.at, shared + 4 * (KD * 2 * D * 2 + KD * D))
        graph = Region(nc, late)
        xn = graph("xn", [TP, D])
        lo1h = graph("lo1h", [P, RING, GC, P], F32R)
        key1h = graph("key1h", [P, RING, GC, 2 * KEYS], F32R)
        win_lo = graph("win_lo", [P, 1])
        gen_rel = graph("gen_rel", [P, GC])
        gen_in = graph("gen_in", [P, GC])
        gen_key = graph("gen_key", [P, GC])

        first = Region(nc, shared)
        raw_qk = first("raw_qk", [P, KD, 2 * D])
        qkT = first("qkT", [P, 2 * KD, D])
        raw_g = first("raw_g", [P, KD, D])
        assert first.at <= late
        first = Region(nc, late)
        gw_row = first("gw_row", [NE, D])
        Rbd = first("Rbd", [P, 2 * FD])
        row_src = first("row_src", [G, GE], I32)
        row_dst = first("row_dst", [G, GE], I32)
        row_w = first("row_w", [G, GE])
        valid = first("valid", [G, GE])
        src_f = first("src_f", [G, GE])
        dst_f = first("dst_f", [G, GE])
        blk_i = first("blk_i", [G, GE], I32)
        blk_f = first("blk_f", [G, GE])
        r_f = first("r_f", [G, GE])
        rel = first("rel", [G, GE])
        inside = first("inside", [G, GE])
        key_f = first("key_f", [G, GE])
        w_hi = first("w_hi", [G, GE], F32R)
        w_lo = first("w_lo", [G, GE])
        n_in = first("n_in", [G, 1])
        b1_row = first("b1_row", [NE * HT, P])
        b2_row = first("b2_row", [NE * KD, P])
        zero_rows = first("zero_rows", [SB2, D])

        second = Region(nc, late)
        Qt = second("Qt", [P, 2, TP])
        At = second("At", [TP, T, TP])
        zn = second("zn", [TP, D])
        zrec = second("zrec", [TP, 2, NH])
        znT = second("znT", [P, KD, TP])
        agg_pos = second("agg_pos", [TP, D])
        agg_neg = second("agg_neg", [TP, D])

        moe = Region(nc, keep.at)
        raw = moe("raw", [P, 4, CH, 512])
        whi = moe("whi", [P, 4, CH, 512], F32R)
        wlo = moe("wlo", [P, 4, CH, 512], F32R)
        over_ = moe.at
        xn2 = moe("xn2", [TP, T, D])
        xn2T = moe("xn2T", [P, 2, KD, TP])
        shp = [TP, T, NE]
        flat = [TP, T * NE]
        lg = moe("lg", shp)
        mx = moe("mx", [TP, T])
        ex = moe("ex", shp)
        sm = moe("sm", [TP, 2, T])
        pr = moe("pr", shp)
        cmp_gt = moe("cmp_gt", [TP, T * NE, NE])
        cmp_eq = moe("cmp_eq", [TP, T * NE, NE])
        lower_e = moe("lower_e", [TP, NE, NE])
        rank = moe("rank", flat)
        is_k = moe("is_k", [TP, TOPK, T * NE])
        routed = moe("routed", flat)
        wm = moe("wm", flat)
        bits = moe("bits", [TP, 3, NE], I32)
        thr = moe("thr", [TP, NE], I32)
        cand = moe("cand", [TP, 3, NE], I32)
        over = moe("over", [TP, 3, T * NE], BF16)
        n_over = moe("n_over", [TP, 3, NE])
        grown = moe("grown", [TP, 3, NE])
        more = moe("more", [TP, NE], I32)
        above = moe("above", flat, BF16)
        tied = moe("tied", flat, BF16)
        room = moe("room", [TP, 2, NE])
        fits = moe("fits", [TP, 2, T * NE])
        sel = moe("sel", flat, BF16)
        first_row = moe("first_row", flat)
        slot = moe("slot", [TP, 2, T * NE])
        p_sel = moe("p_sel", flat)
        trash = moe("trash", [TP, TOPK * T])
        pick = moe("pick", [TP, 3, TOPK, T * NE])
        sel_k = moe("sel_k", [TP, 2, TOPK * T])
        slot_k = moe("slot_k", [TP, TOPK * T])
        scat_f = moe("scat_f", [TP, 2, TOPK * T])
        em = Region(nc, over_)
        xg = em("xg", [SB2, 2, D])
        xgT_hi = em("xgT_hi", [P, KD, SLOTS], F32R)
        xgT_lo = em("xgT_lo", [P, KD, SLOTS], F32R)
        yT = em("yT", [P, KD, SLOTS])
        y = em("y", [SB2, 2, D])
        hg = em("hg", [P, 2, SLOTS])
        h_hi = em("h_hi", [P, HT, SLOTS], F32R)
        h_lo = em("h_lo", [P, HT, SLOTS], F32R)
        cm = Region(nc, keep.at)
        got = cm("got", [TP, 4, TOPK, D])
        part = cm("part", [TP, 4, D])
        res = cm("res", [TP, 4, D])

        rows_zeroed = sem("rows_zeroed"); edges_in = sem("edges_in"); x_in = sem("x_in")
        qk_in = sem("qk_in"); r_in = sem("r_in"); g_in = sem("g_in"); v_in = sem("v_in")
        small_in = sem("small_in"); wo_in = sem("wo_in"); bo_in = sem("bo_in")
        ident_made = sem("ident_made"); consts_made = sem("consts_made"); A_step = sem("A_step")
        xg_zeroed = sem("xg_zeroed")
        edge_step = sem("edge_step"); ln_step = sem("ln_step"); std_done = sem("std_done")
        pe_setup = sem("pe_setup"); act_setup = sem("act_setup")
        xn_ready = sem("xn_ready"); xnT_out = sem("xnT_out"); xnT_ready = sem("xnT_ready")
        h_out = sem("h_out"); h_ready = sem("h_ready"); v_out = sem("v_out"); v_ready = sem("v_ready")
        k_out = sem("k_out"); kmin_ready = sem("kmin_ready"); kexp_ready = sem("kexp_ready")
        kf_ready = sem("kf_ready"); q_out = sem("q_out"); qmin_ready = sem("qmin_ready")
        qexp_ready = sem("qexp_ready"); qt_ready = sem("qt_ready"); kv_out = sem("kv_out")
        key_ready = sem("key_ready"); grp_out = sem("grp_out")
        gen_step = sem("gen_step"); gen_w = sem("gen_w"); waited_apart = sem("waited_apart"); gen_out = sem("gen_out"); A_final = sem("A_final")
        kv_ready = sem("kv_ready")
        qt_c = sem("qt_c"); at_c = sem("at_c"); z_out = sem("z_out"); zrec_step = sem("zrec_step")
        zn_ready = sem("zn_ready"); znT_out = sem("znT_out"); znT_ready = sem("znT_ready")
        agg_out = sem("agg_out"); agg_parts = sem("agg_parts"); mix_out = sem("mix_out"); x2_step = sem("x2_step")
        x2_ready = sem("x2_ready")
        ln2_step = sem("ln2_step"); std2_done = sem("std2_done"); xn2_ready = sem("xn2_ready")
        xn2T_out = sem("xn2T_out"); xn2T_ready = sem("xn2T_ready"); gate_out = sem("gate_out")
        route_consts = sem("route_consts"); route_step = sem("route_step"); exp_ready = sem("exp_ready")
        over_ready = sem("over_ready"); over_out = sem("over_out"); srch_step = sem("srch_step")
        mask_ready = sem("mask_ready"); rank_out = sem("rank_out"); idx_ready = sem("idx_ready")
        scattered = sem("scattered")
        raw_in = [sem(f"raw_in{i}") for i in range(4)]
        hi_ready = sem("hi_ready"); wlo_ready = sem("wlo_ready"); piece_out = sem("piece_out")
        xg_in = sem("xg_in"); xgT_out = sem("xgT_out"); xgT_hi_ready = sem("xgT_hi_ready")
        xgT_lo_ready = sem("xgT_lo_ready"); hid_out = sem("hid_out"); gelu_done = sem("gelu_done")
        hhi_ready = sem("hhi_ready"); hlo_ready = sem("hlo_ready"); yT_ready = sem("yT_ready")
        y_out = sem("y_out"); y_half = sem("y_half"); y_ready = sem("y_ready"); y_stored = sem("y_stored")
        got_in = [sem(f"got_in{i}") for i in range(4)]
        part_ready = sem("part_ready"); res_ready = sem("res_ready")
        stored = [sem(f"stored{i}") for i in range(4)]

        EDGE_STEPS, EXP_AT, GEN_STEPS, SRCH, ROUNDS = 8, 3, 8, 5, 15
        S_EDGE, S_SMALL, S_QKT, S_MAP, S_GT = 6, 8, 8, 16, 20
        N_SETUP = 24
        block = ctx.enter_context(nc.Block())

        def bc(ap, shape):
            return ap.to_broadcast(shape)

        def row3(t):
            return t[:, :].rearrange("g (c p) -> g c p", c=GC)

        @block.sync
        def _(sp):
            sp.wait_ge(rows_zeroed, 1)
            for row, vec in ((row_src, src), (row_dst, dst), (row_w, edge_weight)):
                sp.dma_start(row[0:G - 1, :], vec[0:(G - 1) * GE].rearrange("(g e) -> g e", e=GE)).then_inc(edges_in, 16)
                sp.dma_start(row[G - 1:G, 0:TAIL], vec[(G - 1) * GE:E].rearrange("(a e) -> a e", a=1)).then_inc(edges_in, 16)
            sp.dma_start(raw_qk[:], W_qkv[:, 0:2 * D].rearrange("(k p) n -> p k n", p=P)).then_inc(qk_in, 16)
            sp.wait_ge(consts_made, 1)
            for j in range(2):
                sp.dma_start(Rbd[j * HD:(j + 1) * HD, j * FD:(j + 1) * FD], R_feat).then_inc(r_in, 16)
            sp.dma_start(X[:], x.rearrange("(t p) d -> p t d", p=TP)).then_inc(x_in, 16)
            sp.dma_start(raw_g[:], gnn_W.rearrange("(k p) n -> p k n", p=P)).then_inc(g_in, 16)
            sp.dma_start(Wcat[:, :, D:2 * D], W_qkv[:, 2 * D:3 * D].rearrange("(k p) n -> p k n", p=P)).then_inc(v_in, 16)
            sp.dma_start(Wo[:], W_out.rearrange("(k p) n -> p k n", p=P)).then_inc(wo_in, 16)
            sp.dma_start(bo_all[:], b_out.partition_broadcast(TP)).then_inc(bo_in, 16)
            sp.dma_start(xg_rows[0:TRASH, :].rearrange("(b p) d -> p b d", p=SB2),
                         bc(zero_rows[:, :].unsqueeze(1), [SB2, TRASH // SB2, D])).then_inc(xg_zeroed, 16)
            sp.wait_ge(x2_ready, T)

            def load_piece(e, c, free):
                if free is not None:
                    sp.wait_ge(wlo_ready, free)
                if c < NCH:
                    part = w1[ds(e, 1), :, c * 512:(c + 1) * 512].rearrange("e (k p) h -> p (e k) h", p=P)
                else:
                    part = w2[ds(e, 1), (c - NCH) * 512:(c - NCH + 1) * 512, :].rearrange("e (j p) d -> p (e j) d", p=P)
                sp.dma_start(raw[:, c % 4], part).then_inc(raw_in[c % 4], 16)

            def load_xg(e):
                sp.dma_start(xg[:], xg_rows[ds(e * SLOTS, SLOTS), :].rearrange("(c p) d -> p c d", p=SB2)).then_inc(xg_in, 16)

            for c in range(4):
                load_piece(0, c, None)
            sp.wait_ge(scattered, 16 * TOPK * T)
            sp.wait_ge(xg_zeroed, 16)
            load_xg(0)
            for c in range(4, 8):
                load_piece(0, c, c - 3)

            def store_y(e):
                sp.wait_ge(y_ready, 2 * e + 4)
                sp.dma_start(y_rows[ds(e * SLOTS, SLOTS), :].rearrange("(c p) d -> p c d", p=SB2), y[:]).then_inc(y_stored, 16)

            with sp.Fori(0, NE - 1) as e:
                sp.wait_ge(xgT_out, e * 2 + 2)
                load_xg(e + 1)
                for c in range(8):
                    load_piece(e + 1, c, e * 8 + c + 5)
                store_y(e)
            store_y(NE - 1)
            for t in range(T):
                sp.wait_ge(res_ready, t + 1)
                sp.dma_start(out[t * TP:(t + 1) * TP, :], res[:, t % 4, :]).then_inc(stored[t % 4], 16)
            for i in range(4):
                sp.wait_ge(stored[i], 16 * len(range(i, T, 4)))

        @block.gpsimd
        def _(pool):
            g = nc.gpsimd
            for row in (row_src, row_dst, row_w):
                last = g.memset(row[:], 0)
            last.then_inc(rows_zeroed, 1)
            g.memset(ident[:], 0.0).then_inc(ident_made, 1)
            g.memset(valid[:], 1.0)
            g.memset(zero_rows[:], 0.0)
            g.memset(ones_f[:], 1.0)
            g.memset(Rbd[:], 0.0).then_inc(consts_made, 1)
            pool.wait_ge(consts_made, 1)
            g.affine_select(out=ident[:], in_=ident[:], compare_op=ALU.not_equal, fill=1.0, base=0,
                            pattern=[[-1, P]], channel_multiplier=1).then_inc(ident_made, 1)
            g.affine_select(out=valid[:], in_=valid[:], compare_op=ALU.is_gt, fill=0.0, base=E,
                            pattern=[[-1, GE]], channel_multiplier=-GE).then_inc(consts_made, 1)
            g.iota(iota_r[:], [[1, P]], base=0, channel_multiplier=0, allow_small_or_imprecise_dtypes=True)
            g.iota(iota_k[:], [[1, KEYS]], base=0, channel_multiplier=0, allow_small_or_imprecise_dtypes=True)
            g.memset(eps_c[:], EPS)
            g.memset(KV[:], 0.0)
            g.memset(ones_b[:], 1.0)
            g.memset(tri_b[:], 1.0).then_inc(consts_made, 1)
            pool.wait_ge(consts_made, 3)
            g.affine_select(out=tri_b[:], in_=tri_b[:], compare_op=ALU.is_gt, fill=0.0, base=0,
                            pattern=[[1, TP]], channel_multiplier=-1).then_inc(consts_made, 1)
            g.memset(A[:], 0.0).then_inc(A_step, 1)
            g.dma_start(b1_row[:], b1.rearrange("e (j p) -> (e j) p", p=P)).then_inc(small_in, 16)
            g.dma_start(b2_row[:], b2.rearrange("e (j p) -> (e j) p", p=P)).then_inc(small_in, 16)
            g.dma_start(gw_row[:], gate_w).then_inc(small_in, 16)
            g.dma_start(gate_b_all[:], gate_b.partition_broadcast(TP)).then_inc(small_in, 16)
            g.dma_start(alpha_neg[:], gnn_alpha.partition_broadcast(TP)).then_inc(small_in, 16)

            pool.wait_ge(x2_ready, T)
            g.memset(lower_e[:], 1.0).then_inc(route_consts, 1)
            pool.wait_ge(route_consts, 1)
            g.affine_select(out=lower_e[:], in_=lower_e[:], compare_op=ALU.is_gt, fill=0.0, base=0,
                            pattern=[[1, NE], [-1, NE]], channel_multiplier=0).then_inc(route_consts, 1)
            g.iota(first_row[:], [[0, T], [SLOTS, NE]], base=0, channel_multiplier=0, allow_small_or_imprecise_dtypes=True)
            g.iota(trash[:], [[N, TOPK], [TP, T]], base=TRASH, channel_multiplier=1,
                   allow_small_or_imprecise_dtypes=True).then_inc(route_consts, 1)
            pool.wait_ge(idx_ready, 1)
            pool.wait_ge(xg_zeroed, 16)
            for t in range(T):
                for k in range(TOPK):
                    g.indirect_dma_start(out=xg_rows, out_offset=bass.IndirectOffsetOnAxis(ap=scat_idx[:, k * T + t:k * T + t + 1], axis=0),
                                         in_=xn2[:, t, :], in_offset=None).then_inc(scattered, 16)
            pool.wait_ge(y_stored, 16 * (NE + 1))
            for t in range(T):
                if t >= 4:
                    pool.wait_ge(res_ready, t - 3)
                for k in range(TOPK):
                    g.indirect_dma_start(out=got[:, t % 4, k, :], out_offset=None, in_=y_rows,
                                         in_offset=bass.IndirectOffsetOnAxis(ap=gath_idx[:, k * T + t:k * T + t + 1], axis=0)
                                         ).then_inc(got_in[t % 4], 16)

        @block.tensor
        def _(pe):
            mm, tr = nc.tensor.matmul, nc.tensor.transpose

            def begin(k):
                if k >= 8:
                    pe.wait_ge(act_setup, k - 7)
                return bank[k % 8]

            pe.wait_ge(ident_made, 2)
            pe.wait_ge(consts_made, 1)
            pe.wait_ge(edge_step, EDGE_STEPS)
            for k, row in enumerate((r_f, key_f, w_hi, w_lo, blk_f, dst_f)):
                ps = begin(k)
                for j in range(GC):
                    part = row[:, j * P:(j + 1) * P]
                    last = tr(ps[:, j * G:(j + 1) * G], part.bitcast(F32) if row is w_hi else part, ident[0:G, 0:G])
                last.then_inc(pe_setup, 1)
            ps = begin(S_EDGE)
            tr(ps[0:1, 0:G], dst_f[:, 0:1], ident[0:G, 0:G])
            mm(ps[0:1, 128:129], n_in[:], ones_f[0:G, :], start=True, stop=True).then_inc(pe_setup, 1)
            pe.wait_ge(small_in, 80)
            ps = begin(S_EDGE + 1)
            tr(ps[:, 0:NE * HT], b1_row[:], ident[:])
            tr(ps[:, 128:128 + NE * KD], b2_row[:], ident[0:NE * KD, 0:NE * KD])
            for k in range(KD):
                last = tr(ps[:, 160 + k * NE:160 + (k + 1) * NE], gw_row[:, k * P:(k + 1) * P], ident[0:NE, 0:NE])
            last.then_inc(pe_setup, 1)
            pe.wait_ge(qk_in, 16)
            for s in range(2 * KD):
                ps = begin(S_QKT + s)
                for d in range(KD):
                    last = tr(ps[:, d * P:(d + 1) * P], raw_qk[:, d, s * P:(s + 1) * P], ident[:])
                last.then_inc(pe_setup, 1)
            pe.wait_ge(r_in, 32)
            for s in range(4):
                ps = begin(S_MAP + s)
                pe.wait_ge(act_setup, S_MAP)
                for d in range(2):
                    for f in range(KD):
                        row = (s % 2) * 2 + d
                        last = mm(ps[:, d * NF + f * 2 * FD:d * NF + (f + 1) * 2 * FD],
                                  qkT[:, (s // 2) * KD + f, row * P:(row + 1) * P], Rbd[:], start=True, stop=True)
                last.then_inc(pe_setup, 1)
            pe.wait_ge(g_in, 16)
            for s in range(KD):
                ps = begin(S_GT + s)
                for o in range(KD):
                    last = tr(ps[:, o * P:(o + 1) * P], raw_g[:, o, s * P:(s + 1) * P], ident[:])
                last.then_inc(pe_setup, 1)
            pe.wait_ge(act_setup, N_SETUP)
            pe.wait_ge(v_in, 16)

            PT, PA, PB, PKV, PKS = bank[3], bank[4], bank[5], bank[6], bank[7]

            def group(gi, s):
                pe.wait_ge(key_ready, gi + 1)
                for j in range(GC):
                    for part in range(2):
                        last = mm(bank[s % RING][:, 0:KEYS], lo1h[:, s % RING, j, :],
                                  key1h[:, s % RING, j, part * KEYS:(part + 1) * KEYS],
                                  start=(j == 0 and part == 0), stop=(j == GC - 1 and part == 1))
                last.then_inc(grp_out, 1)

            def tile_work(i, first):
                G_ = lambda s: group(i * GPI + s, s)
                pe.wait_ge(xn_ready, i + 1)
                for k in range(KD):
                    last = tr(PT[:, k * TP:(k + 1) * TP], xn[:, k * P:(k + 1) * P], ident[0:TP, 0:TP])
                last.then_inc(xnT_out, 1)
                G_(0)
                pe.wait_ge(xnT_ready, i + 1)
                for k in range(KD):
                    last = mm(PA[0:TP, :], xnT[:, k, :], Wcat[:, k, 0:D], start=(k == 0), stop=(k == KD - 1))
                last.then_inc(h_out, 1)
                G_(1)
                for k in range(KD):
                    last = mm(PB[0:TP, :], xnT[:, k, :], Wcat[:, k, D:2 * D], start=(k == 0), stop=(k == KD - 1))
                last.then_inc(v_out, 1)
                G_(2)
                pe.wait_ge(h_ready, i + 1)
                for k in range(KD):
                    last = mm(PA[0:TP, 0:NF], xnT[:, k, :], Wcat[:, k, 2 * D:], start=(k == 0), stop=(k == KD - 1))
                last.then_inc(k_out, 1)
                G_(3)
                pe.wait_ge(v_ready, i + 1)
                for m in range(2):
                    for k in range(KD):
                        last = mm(PB[:, m * TP:(m + 1) * TP], Mq[:, k, m * P:(m + 1) * P], xnT[:, k, :],
                                  start=(k == 0), stop=(k == KD - 1))
                last.then_inc(q_out, 1)
                G_(4)
                G_(5)
                pe.wait_ge(kf_ready, i + 1)
                for m in range(2):
                    mm(PKV[:, m * 256:(m + 1) * 256], Kf[:, m * P:(m + 1) * P], V[:, m * 256:(m + 1) * 256],
                       start=(first and m == 0), stop=False, skip_group_check=True)
                    last = mm(PKS[:, m:m + 1], Kf[:, m * P:(m + 1) * P], ones_f[0:TP, :],
                              start=(first and m == 0), stop=False, skip_group_check=True)
                last.then_inc(kv_out, 1)
                for s in range(6, GPI):
                    G_(s)

            tile_work(0, True)
            with pe.Fori(1, T) as i:
                tile_work(i, False)
            with pe.Fori(T, TURNS) as i:
                for s in range(GPI):
                    group(i * GPI + s, s)

            some = pe.value_load(flag[0:1, 0:1], min_val=0, max_val=1)
            with pe.If(some):
                pe.nop().then_inc(gen_out, 1)
                with pe.Fori(0, NWIN * G) as n:
                    pe.wait_ge(gen_step, n * GEN_STEPS + 7)
                    for j in range(GC):
                        for part in range(2):
                            last = mm(bank[0][:, 0:KEYS], lo1h[:, 0, j, :], key1h[:, 0, j, part * KEYS:(part + 1) * KEYS],
                                      start=(j == 0 and part == 0), stop=(j == GC - 1 and part == 1))
                    last.then_inc(gen_out, 1)

            PZ, PN, PG, PM = bank[4], bank[5], bank[0], bank[1]
            pe.wait_ge(kv_ready, 1)
            pe.wait_ge(A_final, 1)
            pe.wait_ge(wo_in, 16)
            with pe.Fori(0, T) as t:
                pe.wait_ge(qt_c, t + 1)
                for m in range(2):
                    mm(PZ[0:TP, m * 256:(m + 1) * 256], Qt[:, m, :], KV[:, m, 0:256], start=True, stop=True)
                    last = mm(PN[0:TP, m * 4:(m + 1) * 4], Qt[:, m, :], KV[:, m, 256:260], start=True, stop=True)
                last.then_inc(z_out, 1)
                pe.wait_ge(at_c, t + 1)
                for b in range(T):
                    last = mm(PG[0:TP, :], At[:, b, :], H[:, b, :], start=(b == 0), stop=(b == T - 1))
                last.then_inc(agg_out, 1)
                pe.wait_ge(zn_ready, t + 1)
                for k in range(KD):
                    last = tr(PT[:, k * TP:(k + 1) * TP], zn[:, k * P:(k + 1) * P], ident[0:TP, 0:TP])
                last.then_inc(znT_out, 1)
                pe.wait_ge(znT_ready, t + 1)
                for k in range(KD):
                    last = mm(PM[0:TP, :], znT[:, k, :], Wo[:, k, :], start=(k == 0), stop=(k == KD - 1))
                last.then_inc(mix_out, 1)

            PL = bank[7]
            pe.wait_ge(x2_ready, T)
            for i in range(T // 2):
                for u in range(2):
                    pe.wait_ge(xn2_ready, 2 * i + u + 1)
                    for k in range(KD):
                        last = tr(bank[3 + u][:, k * TP:(k + 1) * TP], xn2[:, 2 * i + u, k * P:(k + 1) * P], ident[0:TP, 0:TP])
                    last.then_inc(xn2T_out, 1)
                for u in range(2):
                    t = 2 * i + u
                    pe.wait_ge(xn2T_ready, t + 1)
                    for k in range(KD):
                        last = mm(PL[0:TP, t * NE:(t + 1) * NE], xn2T[:, u, k, :], gwT[:, k, :], start=(k == 0), stop=(k == KD - 1))
                    last.then_inc(gate_out, 1)

            pe.wait_ge(consts_made, 4)
            with pe.Fori(0, ROUNDS) as n:
                pe.wait_ge(over_ready, n + 1)
                mm(bank[0][0:TP, 0:3 * T * NE], ones_b[:], over[:, :, :].rearrange("p j f -> p (j f)"),
                   start=True, stop=True).then_inc(over_out, 1)

            def ranks(ps, mask):
                mm(ps[0:TP, 0:T * NE], tri_b[:], mask[:], start=True, stop=False, skip_group_check=True)
                for s in range(1, T):
                    last = mm(ps[0:TP, s * NE:T * NE], ones_b[:], mask[:, 0:(T - s) * NE], start=False,
                              stop=(s == T - 1), skip_group_check=True)
                last.then_inc(rank_out, 1)

            pe.wait_ge(mask_ready, 2)
            mm(bank[1][0:TP, 0:T * NE], ones_b[:], above[:], start=True, stop=True).then_inc(rank_out, 1)
            ranks(bank[2], tied)
            pe.wait_ge(mask_ready, 3)
            ranks(bank[3], sel)

            PH, PX, PO = (bank[0], bank[1]), (bank[2], bank[3]), bank[4:8]

            def turn_in(e):
                pe.wait_ge(xg_in, (e + 1) * 16)
                for h in range(2):
                    for k in range(2):
                        for c in range(2):
                            o = k * SLOTS + c * SB2
                            last = tr(PX[h][:, o:o + SB2], xg[:, c, (2 * h + k) * P:(2 * h + k + 1) * P], ident[0:SB2, 0:SB2])
                    last.then_inc(xgT_out, 1)

            def three(ps, a_hi, a_lo, whs, wls, start, stop):
                mm(ps, whs, a_hi, start=start, stop=False)
                mm(ps, whs, a_lo, start=False, stop=False)
                return mm(ps, wls, a_hi, start=False, stop=stop)

            def expert(e, last_one):
                pe.wait_ge(xgT_lo_ready, e * 2 + 2)
                pe.wait_ge(xgT_hi_ready, e * 2 + 2)
                pe.wait_ge(y_ready, e * 2 + 2)
                for c in range(NCH):
                    pe.wait_ge(wlo_ready, e * 8 + c + 1)
                    for j in range(CH):
                        q = CH * c + j
                        pe.wait_ge(gelu_done, e * HT + q + 1)
                        for k in range(KD):
                            last = three(PH[q % 2][:, 0:SLOTS], xgT_hi[:, k, :], xgT_lo[:, k, :],
                                         whi[:, c % 4, k, j * P:(j + 1) * P], wlo[:, c % 4, k, j * P:(j + 1) * P],
                                         k == 0, k == KD - 1)
                        last.then_inc(hid_out, 1)
                for c in range(NCH, 2 * NCH):
                    pe.wait_ge(wlo_ready, e * 8 + c + 1)
                    for j in range(CH):
                        q = CH * (c - NCH) + j
                        pe.wait_ge(hlo_ready, e * HT + q + 3)
                        for d in range(KD):
                            last = three(PO[d][:, 0:SLOTS], h_hi[:, q, :], h_lo[:, q, :],
                                         whi[:, c % 4, j, d * P:(d + 1) * P], wlo[:, c % 4, j, d * P:(d + 1) * P],
                                         q == 0, q == HT - 1)
                    last.then_inc(piece_out, 1)
                if not last_one:
                    turn_in(e + 1)
                pe.wait_ge(yT_ready, e + 1)
                for c in range(2):
                    for d in range(KD):
                        last = tr(PH[c][0:SB2, d * P:(d + 1) * P], yT[:, d, c * SB2:(c + 1) * SB2], ident[:])
                    last.then_inc(y_out, 1)

            pe.nop().then_inc(piece_out, NCH)
            turn_in(0)
            with pe.Fori(0, NE - 1) as e:
                expert(e, False)
            expert(NE - 1, True)

        @block.scalar
        def _(act):
            av = nc.scalar.activation

            def take(k):
                act.wait_ge(pe_setup, k + 1)
                return bank[k % 8]

            for k, col in enumerate((col_r[:], col_key[:], col_w[:, :, :, 0], col_w[:, :, :, 1], col_blk[:], col_dst[:])):
                ps = take(k)
                av(col, ps[:, 0:GC * G].rearrange("p (c g) -> p g c", c=GC), ACT.Copy).then_inc(act_setup, 1)
            ps = take(S_EDGE)
            av(first_dst[:], ps[0:1, 0:G], ACT.Copy)
            av(flag[:], ps[0:1, 128:129], ACT.Relu, bias=float(G * GE), scale=-1.0).then_inc(act_setup, 1)
            ps = take(S_EDGE + 1)
            av(b1T[:], ps[:, 0:NE * HT], ACT.Copy)
            av(b2T[:], ps[:, 128:128 + NE * KD], ACT.Copy)
            av(gwT[:, :, :], ps[:, 160:160 + KD * NE].rearrange("p (k e) -> p k e", k=KD), ACT.Copy).then_inc(act_setup, 1)
            for s in range(2 * KD):
                ps = take(S_QKT + s)
                av(qkT[:, s, :], ps[:], ACT.Copy).then_inc(act_setup, 1)
            for s in range(4):
                ps = take(S_MAP + s)
                half = slice((s % 2) * 2, (s % 2) * 2 + 2)
                to = Mq[:, half, :] if s < 2 else Wcat[:, half, 2 * D:]
                av(to, ps[:].rearrange("p (d n) -> p d n", d=2), ACT.Copy).then_inc(act_setup, 1)
            for s in range(KD):
                ps = take(S_GT + s)
                av(Wcat[:, s, 0:D], ps[:], ACT.Copy).then_inc(act_setup, 1)
            act.wait_ge(ln_step, 2 * T)
            act.wait_ge(consts_made, 3)
            av(sd[:], mv[:, :, 1], ACT.Sqrt, bias=eps_c[:]).then_inc(std_done, 1)

            PT, PA, PB, PKV, PKS = bank[3], bank[4], bank[5], bank[6], bank[7]
            with act.Fori(0, T) as i:
                act.wait_ge(xnT_out, i + 1)
                av(xnT[:], PT[:, 0:KD * TP].rearrange("p (k t) -> p k t", k=KD), ACT.Copy).then_inc(xnT_ready, 1)
                act.wait_ge(h_out, i + 1)
                av(H[:, ds(i, 1), :].rearrange("p a d -> p (a d)"), PA[0:TP, :], ACT.Copy).then_inc(h_ready, 1)
                act.wait_ge(v_out, i + 1)
                av(V[:], PB[0:TP, :], ACT.Copy).then_inc(v_ready, 1)
                act.wait_ge(kmin_ready, i + 1)
                av(k_exp[:], k_min[:], ACT.Exp).then_inc(kexp_ready, 1)
                act.wait_ge(qmin_ready, i + 1)
                av(q_exp[:], q_min[:], ACT.Exp).then_inc(qexp_ready, 1)

            act.wait_ge(kv_out, T)
            for m in range(2):
                for h in range(4):
                    p = slice(h * FD, (h + 1) * FD)
                    av(KV[p, m, h * HD:(h + 1) * HD], PKV[p, m * 256 + h * HD:m * 256 + (h + 1) * HD], ACT.Copy)
                    last = av(KV[p, m, 256 + h:257 + h], PKS[p, m:m + 1], ACT.Copy)
            last.then_inc(kv_ready, 1)

            PG = bank[0]
            act.wait_ge(A_final, 1)
            act.wait_ge(qt_ready, T)
            with act.Fori(0, T) as t:
                av(Qt[:], QT[:, :, ds(t * TP, TP)], ACT.Copy).then_inc(qt_c, 1)
                av(At[:], A[:, :, ds(t * TP, TP)], ACT.Copy).then_inc(at_c, 1)
                act.wait_ge(znT_out, t + 1)
                av(znT[:], PT[:, 0:KD * TP].rearrange("p (k t) -> p k t", k=KD), ACT.Copy).then_inc(znT_ready, 1)
                av(agg_pos[:], PG[0:TP, :], ACT.Relu)
                av(agg_neg[:], PG[0:TP, :], ACT.Relu, scale=-1.0).then_inc(agg_parts, 1)

            act.wait_ge(x2_ready, T)
            av(sd[:], mv[:, :, 1], ACT.Sqrt, bias=eps_c[:]).then_inc(std2_done, 1)
            for t in range(T):
                act.wait_ge(xn2T_out, t + 1)
                av(xn2T[:, t % 2], bank[3 + t % 2][:, 0:KD * TP].rearrange("p (k t) -> p k t", k=KD), ACT.Copy).then_inc(xn2T_ready, 1)
            act.wait_ge(route_step, EXP_AT)
            av(ex[:], lg[:], ACT.Exp).then_inc(exp_ready, 1)

            PH, PX, PO = (bank[0], bank[1]), (bank[2], bank[3]), bank[4:8]

            def high(e, c):
                act.wait_ge(raw_in[c % 4], (e * 2 + (c // 4 + 1)) * 16)
                av(whi[:, c % 4], raw[:, c % 4], ACT.Copy).then_inc(hi_ready, 1)

            def xg_high(e):
                for h in range(2):
                    act.wait_ge(xgT_out, e * 2 + (h + 1))
                    av(xgT_hi[:, 2 * h:2 * h + 2, :], PX[h][:, 0:2 * SLOTS].rearrange("p (k c) -> p k c", k=2), ACT.Copy).then_inc(xgT_hi_ready, 1)

            def expert(e, last_one):
                for c in range(NCH):
                    if c == 0:
                        act.wait_ge(piece_out, e * NCH + NCH)
                    high(e, c + 3)
                    for j in range(CH):
                        q = CH * c + j
                        act.wait_ge(hid_out, e * HT + (q + 1))
                        act.wait_ge(hlo_ready, e * HT + (q + 1))
                        av(hg[:, q % 2, :], PH[q % 2][:, 0:SLOTS], ACT.Gelu, bias=b1T[:, ds(e * HT + q, 1)]).then_inc(gelu_done, 1)
                        act.wait_ge(gelu_done, e * HT + (q + 3))
                        av(h_hi[:, q, :], hg[:, q % 2, :], ACT.Copy).then_inc(hhi_ready, 1)
                for c in range(NCH, 2 * NCH):
                    if c + 3 < 8 or not last_one:
                        if c > NCH:
                            act.wait_ge(piece_out, e * NCH + c)
                        high(e, c + 3)
                act.wait_ge(piece_out, e * NCH + 2 * NCH)
                for d in range(KD):
                    last = av(yT[:, d, :], PO[d][:, 0:SLOTS], ACT.Identity, bias=b2T[:, ds(e * KD + d, 1)])
                last.then_inc(yT_ready, 1)
                if not last_one:
                    xg_high(e + 1)
                act.wait_ge(y_out, e * 2 + 1)
                act.wait_ge(y_stored, (e + 1) * 16)
                av(y[:, 0, :], PH[0][0:SB2, :], ACT.Copy).then_inc(y_ready, 1)

            act.nop().then_inc(gelu_done, 2)
            act.nop().then_inc(y_ready, 2)
            act.nop().then_inc(y_stored, 16)
            for c in range(3):
                high(0, c)
            act.wait_ge(xg_in, 16)
            xg_high(0)
            with act.Fori(0, NE - 1) as e:
                expert(e, False)
            expert(NE - 1, True)

        @block.vector
        def _(dve):
            v = nc.vector

            step = Chain(dve, edge_step)
            dve.wait_ge(edges_in, 96)
            v.tensor_copy(w_hi[:], row_w[:])
            v.tensor_copy(src_f[:], row_src[:])
            step(v.tensor_copy(dst_f[:], row_dst[:]))
            v.tensor_tensor(w_lo[:], row_w[:], w_hi[:].bitcast(F32), ALU.subtract)
            v.tensor_scalar(blk_i[:], src_f[:], 1.0 / TP, -((TP - 1) / 2) / TP, ALU.mult, ALU.add)
            step(v.tensor_scalar(rel[:], dst_f[:], dst_f[:, 0:1], None, ALU.subtract))
            dve.wait_ge(consts_made, 2)
            v.tensor_copy(blk_f[:], blk_i[:])
            step(v.tensor_tensor(rel[:], rel[:], valid[:], ALU.mult))
            v.scalar_tensor_tensor(out=r_f[:], in0=blk_f[:], scalar=-float(TP), in1=src_f[:], op0=ALU.mult, op1=ALU.add)
            step(v.tensor_scalar(inside[:], rel[:], 0.0, None, ALU.is_ge))
            step(v.scalar_tensor_tensor(out=inside[:], in0=rel[:], scalar=float(WIN), in1=inside[:], op0=ALU.is_lt, op1=ALU.mult))
            v.tensor_reduce(n_in[:], inside[:], AX_X, ALU.add)
            step(v.scalar_tensor_tensor(out=key_f[:], in0=blk_f[:], scalar=float(WIN), in1=rel[:], op0=ALU.mult, op1=ALU.add))
            step(v.scalar_tensor_tensor(out=key_f[:], in0=key_f[:], scalar=1.0, in1=inside[:], op0=ALU.add, op1=ALU.mult))
            step(v.tensor_scalar(key_f[:], key_f[:], -1.0, None, ALU.add))
            assert step.n == EDGE_STEPS

            ln = Chain(dve, ln_step)
            dve.wait_ge(x_in, 16)
            for t in range(T):
                ln(v.bn_stats(stats[:, 0, :], X[:, t, :]))
                ln(v.bn_aggr(mv[:, t, :], stats[:, 0, :]))
            dve.wait_ge(std_done, 1)
            ln(v.reciprocal(rstd[:], sd[:]))
            dve.wait_ge(small_in, 80)
            ln(v.tensor_scalar(alpha_neg[:], alpha_neg[:], -1.0, None, ALU.mult))

            PT, PA, PB = bank[3], bank[4], bank[5]

            def wait_apart(sem, value):
                dve.wait_ge(sem, value)
                dve.sem_inc(waited_apart, 1)

            def keys(gi, s, key_col, n_sem, slot=None):
                slot = s % RING if slot is None else slot
                for j in range(GC):
                    last = v.scalar_tensor_tensor(
                        out=key1h[:, slot, j, :].rearrange("p (a k) -> p a k", a=2),
                        in0=bc(iota_k[:, :].unsqueeze(1), [P, 2, KEYS]),
                        scalar=key_col(j),
                        in1=bc(col_w[:, ds(gi, 1), j, :].rearrange("p a w -> p (a w)").unsqueeze(2), [P, 2, KEYS]),
                        op0=ALU.is_equal, op1=ALU.mult)
                last.then_inc(n_sem, 1)

            def places(gi, slot):
                return v.tensor_tensor(lo1h[:, slot], bc(iota_r[:, :].unsqueeze(1), [P, GC, P]),
                                       bc(col_r[:, ds(gi, 1), :].rearrange("p a c -> p (a c)").unsqueeze(2), [P, GC, P]),
                                       ALU.is_equal)

            def key_group(gi, s):
                places(gi, s % RING)
                keys(gi, s, lambda j: col_key[:, ds(gi, 1), j], key_ready)

            def add_group(gi, s):
                at = dve.value_load(first_dst[0:1, ds(gi, 1)], min_val=0, max_val=N - 1)
                dve.wait_ge(grp_out, gi + 1)
                dve.wait_ge(A_step, gi + 1)
                win = A[:, :, ds(at, WIN)]
                v.tensor_tensor(win, win, bank[s % RING][0:TP, 0:KEYS].rearrange("p (b w) -> p b w", b=T), ALU.add).then_inc(A_step, 1)

            dve.wait_ge(act_setup, S_QKT)
            key_group(0, 0)
            key_group(1, 1)
            dve.wait_ge(act_setup, N_SETUP)
            with dve.Fori(0, T) as i:
                xt = X[:, ds(i, 1), :].rearrange("p a d -> p (a d)")
                v.tensor_scalar(xn[:], xt, mv[:, ds(i, 1), 0], rstd[:, ds(i, 1)], ALU.subtract, ALU.mult).then_inc(xn_ready, 1)
                for s in range(GPI):
                    key_group(i * GPI + (s + 2), s + 2)
                    add_group(i * GPI + s, s)
                    if s == 4:
                        dve.wait_ge(k_out, i + 1)
                        v.tensor_scalar(k_min[:], PA[0:TP, 0:NF], 0.0, None, ALU.min).then_inc(kmin_ready, 1)
                    if s == 5:
                        dve.wait_ge(kexp_ready, i + 1)
                        v.scalar_tensor_tensor(out=Kf[:], in0=PA[0:TP, 0:NF], scalar=0.0, in1=k_exp[:],
                                               op0=ALU.max, op1=ALU.add).then_inc(kf_ready, 1)
                    if s == 6:
                        dve.wait_ge(q_out, i + 1)
                        v.tensor_scalar(q_min[:], PB[:, 0:2 * TP], 0.0, None, ALU.min).then_inc(qmin_ready, 1)
                    if s == 7:
                        dve.wait_ge(qexp_ready, i + 1)
                        v.scalar_tensor_tensor(out=QT[:, :, ds(i * TP, TP)], in0=PB[:, 0:2 * TP].rearrange("p (m t) -> p m t", m=2),
                                               scalar=0.0, in1=q_exp[:].rearrange("p (m t) -> p m t", m=2),
                                               op0=ALU.max, op1=ALU.add).then_inc(qt_ready, 1)
            with dve.Fori(T, TURNS - 1) as i:
                for s in range(GPI):
                    key_group(i * GPI + (s + 2), s + 2)
                    add_group(i * GPI + s, s)
            for s in range(GPI):
                if s + 2 < GPI:
                    key_group((TURNS - 1) * GPI + s + 2, s + 2)
                add_group((TURNS - 1) * GPI + s, s)
            dve.wait_ge(A_step, G + 1)

            some = dve.value_load(flag[0:1, 0:1], min_val=0, max_val=1)
            with dve.If(some):
                v.memset(A[:], 0.0)
                v.memset(win_lo[:], -float(WIN))
                v.nop().then_inc(gen_w, 1)
                with dve.Fori(0, NWIN) as w:
                    dve.wait_ge(gen_w, w + 1)
                    v.tensor_scalar(win_lo[:], win_lo[:], float(WIN), None, ALU.add).then_inc(gen_w, 1)
                    wait_apart(gen_w, w + 2)
                    with dve.Fori(0, G) as gi:
                        n = w * G + gi
                        k = [0]

                        def link(ins):
                            k[0] += 1
                            ins.then_inc(gen_step, 1)
                            dve.wait_ge(gen_step, n * GEN_STEPS + k[0])

                        dcol = col_dst[:, ds(gi, 1), :].rearrange("p a c -> p (a c)")
                        bcol = col_blk[:, ds(gi, 1), :].rearrange("p a c -> p (a c)")
                        link(v.tensor_scalar(gen_rel[:], dcol, win_lo[:, 0:1], None, ALU.subtract))
                        link(v.tensor_scalar(gen_in[:], gen_rel[:], 0.0, None, ALU.is_ge))
                        link(v.scalar_tensor_tensor(out=gen_in[:], in0=gen_rel[:], scalar=float(WIN), in1=gen_in[:], op0=ALU.is_lt, op1=ALU.mult))
                        link(v.scalar_tensor_tensor(out=gen_key[:], in0=bcol, scalar=float(WIN), in1=gen_rel[:], op0=ALU.mult, op1=ALU.add))
                        link(v.scalar_tensor_tensor(out=gen_key[:], in0=gen_key[:], scalar=1.0, in1=gen_in[:], op0=ALU.add, op1=ALU.mult))
                        link(v.tensor_scalar(gen_key[:], gen_key[:], -1.0, None, ALU.add))
                        dve.wait_ge(gen_out, n + 1)
                        places(gi, 0)
                        keys(gi, 0, lambda j: gen_key[:, j:j + 1], gen_step, slot=0)
                        dve.wait_ge(gen_out, n + 2)
                        win = A[:, :, ds(w * WIN, WIN)]
                        v.tensor_tensor(win, win, bank[0][0:TP, 0:KEYS].rearrange("p (b w) -> p b w", b=T), ALU.add).then_inc(gen_step, 1)
                        dve.wait_ge(gen_step, n * GEN_STEPS + 8)
            v.nop().then_inc(A_final, 1)

            PZ, PN, PM = bank[4], bank[5], bank[1]
            dve.wait_ge(kv_ready, 1)
            with dve.Fori(0, T) as t:
                xt = X[:, ds(t, 1), :].rearrange("p a d -> p (a d)")
                dve.wait_ge(z_out, t + 1)
                v.tensor_scalar(zrec[:, 0, :], PN[0:TP, 0:NH], 1e-6, None, ALU.add).then_inc(zrec_step, 1)
                dve.wait_ge(zrec_step, t * 2 + 1)
                v.reciprocal(zrec[:, 1, :], zrec[:, 0, :]).then_inc(zrec_step, 1)
                dve.wait_ge(zrec_step, t * 2 + 2)
                v.tensor_tensor(zn[:, :].rearrange("p (h f) -> p h f", h=NH), PZ[0:TP, :].rearrange("p (h f) -> p h f", h=NH),
                                bc(zrec[:, 1, :].unsqueeze(2), [TP, NH, HD]), ALU.mult).then_inc(zn_ready, 1)
                dve.wait_ge(agg_parts, t + 1)
                v.scalar_tensor_tensor(out=xt, in0=agg_neg[:], scalar=alpha_neg[:, 0:1], in1=xt, op0=ALU.mult, op1=ALU.add).then_inc(x2_step, 1)
                dve.wait_ge(x2_step, t * 6 + 1)
                v.tensor_tensor(xt, xt, agg_pos[:], ALU.add).then_inc(x2_step, 1)
                dve.wait_ge(x2_step, t * 6 + 2)
                dve.wait_ge(bo_in, 16)
                v.tensor_tensor(xt, xt, bo_all[:], ALU.add).then_inc(x2_step, 1)
                dve.wait_ge(x2_step, t * 6 + 3)
                dve.wait_ge(mix_out, t + 1)
                v.tensor_tensor(xt, xt, PM[0:TP, :], ALU.add).then_inc(x2_step, 1)
                wait_apart(x2_step, t * 6 + 4)
                v.bn_stats(stats[:, 0, :], xt).then_inc(x2_step, 1)
                wait_apart(x2_step, t * 6 + 5)
                v.bn_aggr(stats[:, 1, 0:2], stats[:, 0, :]).then_inc(x2_step, 1)
                dve.wait_ge(x2_step, t * 6 + 6)
                v.tensor_copy(mv[:, ds(t, 1), :].rearrange("p a s -> p (a s)"), stats[:, 1, 0:2]).then_inc(x2_ready, 1)

            dve.wait_ge(std2_done, 1)
            v.reciprocal(rstd[:], sd[:]).then_inc(ln2_step, 1)
            dve.wait_ge(ln2_step, 1)
            for t in range(T):
                v.tensor_scalar(xn2[:, t, :], X[:, t, :], mv[:, t, 0:1], rstd[:, t:t + 1], ALU.subtract, ALU.mult).then_inc(xn2_ready, 1)

            st = Chain(dve, route_step)
            PL = bank[7]

            def tv(ap):
                return ap.rearrange("p (t e) -> p t e", e=NE)

            dve.wait_ge(gate_out, T)
            st(v.tensor_tensor(lg[:], tv(PL[0:TP, 0:T * NE]), bc(gate_b_all[:, :].unsqueeze(1), shp), ALU.add))
            st(v.tensor_reduce(mx[:], lg[:], AX_X, ALU.max))
            st(v.tensor_tensor(lg[:], lg[:], bc(mx[:, :].unsqueeze(2), shp), ALU.subtract))
            assert st.n == EXP_AT
            dve.wait_ge(exp_ready, 1)
            st(v.tensor_reduce(sm[:, 0, :], ex[:], AX_X, ALU.add))
            st(v.reciprocal(sm[:, 1, :], sm[:, 0, :]))
            st(v.tensor_tensor(pr[:], ex[:], bc(sm[:, 1, :].unsqueeze(2), shp), ALU.mult))
            prf = pr[:, :, :].rearrange("p t e -> p (t e)")
            others = bc(pr[:, :, :].unsqueeze(2), [TP, T, NE, NE])
            mine = bc(pr[:, :, :].unsqueeze(3), [TP, T, NE, NE])
            c4 = lambda m: m[:, :, :].rearrange("p (t e) f -> p t e f", e=NE)
            v.tensor_tensor(c4(cmp_gt), others, mine, ALU.is_gt)
            st(v.tensor_tensor(c4(cmp_eq), others, mine, ALU.is_equal))
            dve.wait_ge(route_consts, 3)
            st(v.tensor_tensor(c4(cmp_eq), c4(cmp_eq), bc(lower_e[:, :, :].unsqueeze(1), [TP, T, NE, NE]), ALU.mult))
            st(v.tensor_tensor(cmp_gt[:], cmp_gt[:], cmp_eq[:], ALU.add))
            st(v.tensor_reduce(rank[:], cmp_gt[:], AX_X, ALU.add))
            v.tensor_scalar(is_k[:, 0, :], rank[:], 0.0, None, ALU.is_equal)
            v.tensor_scalar(is_k[:, 1, :], rank[:], 1.0, None, ALU.is_equal)
            st(v.tensor_scalar(routed[:], rank[:], float(TOPK), None, ALU.is_lt))
            st(v.tensor_tensor(wm[:], routed[:], prf, ALU.mult))
            st(v.scalar_tensor_tensor(out=wm[:], in0=routed[:], scalar=-1.0, in1=wm[:], op0=ALU.add, op1=ALU.add))

            v.memset(thr[:], 0)
            for j in range(3):
                last = v.memset(bits[:, j, :], (j + 1) << (2 * ROUNDS - 2))
            st(last)
            st(v.tensor_copy(cand[:], bits[:]))
            with dve.Fori(0, ROUNDS) as n:
                k = [0]

                def link(ins):
                    k[0] += 1
                    ins.then_inc(srch_step, 1)
                    dve.wait_ge(srch_step, n * SRCH + k[0])

                v.tensor_tensor(over[:, :, :].rearrange("p j (t e) -> p j t e", e=NE), bc(tv(wm[:, :]).unsqueeze(1), [TP, 3, T, NE]),
                                bc(cand[:, :, :].bitcast(F32).unsqueeze(2), [TP, 3, T, NE]), ALU.is_ge).then_inc(over_ready, 1)
                dve.wait_ge(over_out, n + 1)
                link(v.tensor_reduce(n_over[:], bank[0][0:TP, 0:3 * T * NE].rearrange("p (j t e) -> p j e t", j=3, t=T), AX_X, ALU.add))
                link(v.scalar_tensor_tensor(out=grown[:], in0=n_over[:], scalar=CAP - 0.5, in1=bc(bits[:, 0:1, :], [TP, 3, NE]),
                                            op0=ALU.is_ge, op1=ALU.mult))
                with nc.allow_low_precision(reason="up to three times a power of two: exact as an integer"):
                    link(v.tensor_reduce(more[:], grown[:, :, :].rearrange("p j e -> p e j"), AX_X, ALU.add))
                v.tensor_scalar(bits[:], bits[:], 2, None, ALU.logical_shift_right)
                link(v.tensor_tensor(thr[:], thr[:], more[:], ALU.bitwise_or))
                link(v.tensor_tensor(cand[:], bits[:], bc(thr[:, :].unsqueeze(1), [TP, 3, NE]), ALU.bitwise_or))

            thr_b = bc(thr[:, :].bitcast(F32).unsqueeze(1), shp)
            v.tensor_tensor(tv(above[:, :]), tv(wm[:, :]), thr_b, ALU.is_gt).then_inc(mask_ready, 1)
            v.tensor_tensor(tv(tied[:, :]), tv(wm[:, :]), thr_b, ALU.is_equal).then_inc(mask_ready, 1)
            dve.wait_ge(rank_out, 1)
            st(v.tensor_reduce(room[:, 0, :], bank[1][0:TP, 0:T * NE].rearrange("p (t e) -> p e t", t=T), AX_X, ALU.add))
            st(v.tensor_scalar(room[:, 1, :], room[:, 0, :], -1.0, float(CAP), ALU.mult, ALU.add))
            dve.wait_ge(rank_out, 2)
            st(v.tensor_tensor(tv(fits[:, 0, :]), tv(bank[2][0:TP, 0:T * NE]), bc(room[:, 1, :].unsqueeze(1), shp), ALU.is_lt))
            st(v.tensor_tensor(fits[:, 1, :], fits[:, 0, :], tied[:], ALU.mult))
            v.tensor_tensor(sel[:], fits[:, 1, :], above[:], ALU.add).then_inc(mask_ready, 1)
            dve.wait_ge(mask_ready, 3)
            v.tensor_tensor(p_sel[:], prf, sel[:], ALU.mult)
            dve.wait_ge(rank_out, 3)
            st(v.tensor_tensor(slot[:, 0, :], bank[3][0:TP, 0:T * NE], first_row[:], ALU.add))
            st(v.tensor_tensor(slot[:, 1, :], slot[:, 0, :], sel[:], ALU.mult))
            kf = [TP, TOPK, T * NE]
            v.tensor_tensor(pick[:, 0], is_k[:], bc(slot[:, 1:2, :], kf), ALU.mult)
            v.tensor_tensor(pick[:, 1], is_k[:], bc(sel[:, :].unsqueeze(1), kf), ALU.mult)
            st(v.tensor_tensor(pick[:, 2], is_k[:], bc(p_sel[:, :].unsqueeze(1), kf), ALU.mult))
            pk = lambda i: pick[:, i].rearrange("p k (t e) -> p (k t) e", e=NE)
            v.tensor_reduce(slot_k[:], pk(0), AX_X, ALU.add)
            v.tensor_reduce(comb_w[:], pk(2), AX_X, ALU.add)
            st(v.tensor_reduce(sel_k[:, 0, :], pk(1), AX_X, ALU.add))
            v.tensor_copy(gath_idx[:], slot_k[:])
            st(v.tensor_scalar(sel_k[:, 1, :], sel_k[:, 0, :], -1.0, 1.0, ALU.mult, ALU.add))
            st(v.tensor_tensor(scat_f[:, 0, :], sel_k[:, 1, :], trash[:], ALU.mult))
            st(v.tensor_tensor(scat_f[:, 1, :], scat_f[:, 0, :], slot_k[:], ALU.add))
            v.tensor_copy(scat_idx[:], scat_f[:, 1, :]).then_inc(idx_ready, 1)

            PH, PX = (bank[0], bank[1]), (bank[2], bank[3])

            def low(e, c):
                dve.wait_ge(hi_ready, e * 8 + (c + 1))
                v.tensor_tensor(wlo[:, c % 4], raw[:, c % 4], whi[:, c % 4].bitcast(F32), ALU.subtract).then_inc(wlo_ready, 1)

            def xg_low(e):
                for h in range(2):
                    dve.wait_ge(xgT_hi_ready, e * 2 + (h + 1))
                    v.tensor_tensor(xgT_lo[:, 2 * h:2 * h + 2, :], PX[h][:, 0:2 * SLOTS].rearrange("p (k c) -> p k c", k=2),
                                    xgT_hi[:, 2 * h:2 * h + 2, :].bitcast(F32), ALU.subtract).then_inc(xgT_lo_ready, 1)

            def expert(e, last_one):
                for c in range(2 * NCH):
                    if c + 3 < 8 or not last_one:
                        low(e, c + 3)
                    if c < NCH:
                        for q in range(CH * c, CH * c + CH):
                            dve.wait_ge(hhi_ready, e * HT + (q + 1))
                            v.tensor_tensor(h_lo[:, q, :], hg[:, q % 2, :], h_hi[:, q, :].bitcast(F32), ALU.subtract).then_inc(hlo_ready, 1)
                if not last_one:
                    xg_low(e + 1)
                dve.wait_ge(y_out, e * 2 + 2)
                dve.wait_ge(y_stored, (e + 1) * 16)
                v.tensor_copy(y[:, 1, :], PH[1][0:SB2, :]).then_inc(y_ready, 1)

            v.nop().then_inc(hlo_ready, 2)
            for c in range(3):
                low(0, c)
            xg_low(0)
            with dve.Fori(0, NE - 1) as e:
                expert(e, False)
            expert(NE - 1, True)

            for t in range(T):
                dve.wait_ge(got_in[t % 4], 32 * (t // 4 + 1))
                if t >= 4:
                    dve.wait_ge(stored[t % 4], 16 * (t // 4))
                v.scalar_tensor_tensor(out=part[:, t % 4, :], in0=got[:, t % 4, 0, :], scalar=comb_w[:, t:t + 1], in1=X[:, t, :],
                                       op0=ALU.mult, op1=ALU.add).then_inc(part_ready, 1)
                dve.wait_ge(part_ready, t + 1)
                v.scalar_tensor_tensor(out=res[:, t % 4, :], in0=got[:, t % 4, 1, :], scalar=comb_w[:, T + t:T + t + 1],
                                       in1=part[:, t % 4, :], op0=ALU.mult, op1=ALU.add).then_inc(res_ready, 1)


_INS = ['x', 'src', 'dst', 'edge_weight', 'L0_gnn_W', 'L0_gnn_alpha', 'L0_mix_W_qkv', 'L0_mix_random_matrix',
        'L0_mix_W_out', 'L0_mix_b_out', 'L0_ffn_gate_w', 'L0_ffn_gate_b', 'L0_ffn_w1', 'L0_ffn_b1', 'L0_ffn_w2',
        'L0_ffn_b2']
_OUTS = [((1250, 512), 'float32')]


def kernel(**inputs):
    import numpy as _np
    import concourse.bacc as _bacc
    from concourse import mybir as _mybir
    from concourse.bass_utils import run_bass_kernel_spmd as _run

    nc = _bacc.Bacc("TRN2", target_bir_lowering=False, num_devices=1)
    arrays, args = {}, []
    for name in _INS:
        a = _np.ascontiguousarray(inputs[name])
        if a.ndim == 0:
            a = a.reshape(1)
        arrays[f"in_{name}_dram"] = a
        args.append(nc.dram_tensor(f"in_{name}_dram", a.shape, _mybir.dt.from_np(a.dtype), kind="ExternalInput").ap())
    for i, (shape, dtype) in enumerate(_OUTS):
        dt = _mybir.dt.from_np(_np.dtype(dtype))
        args.append(nc.dram_tensor(f"out_{i}_dram", shape, dt, kind="ExternalOutput").ap())
    gps_layer(nc, *args)
    r = _run(nc, [arrays], core_ids=[0])
    got = tuple(r.results[0][f"out_{i}_dram"] for i in range(len(_OUTS)))
    return got[0]
```

```python
from contextlib import ExitStack

import concourse.bass as bass
from concourse import mybir

ALU = mybir.AluOpType
ACT = mybir.ActivationFunctionType
AX_X = mybir.AxisListType.X
F32 = mybir.dt.float32
F32R = mybir.dt.float32r
BF16 = mybir.dt.bfloat16
I32 = mybir.dt.int32
U32 = mybir.dt.uint32
P = 128


class Chain:

    def __init__(self, eng, sem):
        self.eng, self.sem, self.n = eng, sem, 0

    def __call__(self, ins):
        ins.then_inc(self.sem, 1)
        self.n += 1
        self.eng.wait_ge(self.sem, self.n)


class Region:

    def __init__(self, nc, start):
        self.nc, self.at = nc, -(-start // 32) * 32

    def __call__(self, name, shape, dt=F32):
        t = self.nc.alloc_sbuf_tensor_at(name, shape, dt, offset=self.at)
        size = mybir.dt.size(dt)
        for n in shape[1:]:
            size *= n
        self.at += -(-size // 32) * 32
        assert self.at <= self.nc.sbuf_usable_end, (name, self.at, self.nc.sbuf_usable_end)
        return t


def ds(start, size):
    return bass.ds(start, size)


def gps_layer(nc, x, src, dst, edge_weight, gnn_W, gnn_alpha, W_qkv, R_feat, W_out, b_out,
              gate_w, gate_b, w1, b1, w2, b2, out):
    N, D = x.shape
    E = src.shape[0]
    HD, FD = R_feat.shape
    NH = D // HD
    NE, _, HID = w1.shape
    TOPK = 2
    CAP = int(1.2 * N / NE)
    EPS = 1e-5

    TP = 125
    T = N // TP
    KD = D // P
    NF = NH * FD
    assert T * TP == N and TOPK == 2

    GC, WIN = 5, 26
    GE = GC * P
    FULL = E // GE
    TAIL = E - FULL * GE
    KEYS = T * WIN
    RING = 2
    PSR = 3
    GPI = 6
    TURNS = -(-E // (GE * GPI))
    G = TURNS * GPI
    assert GPI % RING == 0 and GPI % PSR == 0 and TURNS == T + 1 and 0 < TAIL and FULL < G
    NWIN = -(-N // WIN)
    AW = NWIN * WIN + WIN

    SLOTS = 188
    SB2 = SLOTS // 2
    TRASH = (NE + 1) * SLOTS
    HT = HID // P
    CH = 4
    NCH = HT // CH
    assert SLOTS >= CAP and CH == KD

    xg_rows = nc.dram_tensor("xg_rows", (TRASH + TOPK * N, D), F32, kind="Internal").ap()
    y_rows = nc.dram_tensor("y_rows", (NE * SLOTS, D), F32, kind="Internal").ap()


    ctx = ExitStack()
    with ctx:
        def sem(name):
            return ctx.enter_context(nc.semaphore(name))

        bank = [ctx.enter_context(nc.psum_tensor(f"bank{i}", [P, 512], F32)) for i in range(8)]

        keep = Region(nc, nc.sbuf_base)
        X = keep("X", [TP, T + 1, D])
        ident = keep("ident", [P, P])
        ones_f = keep("ones_f", [P, 1])
        ones_b = keep("ones_b", [TP, TP], BF16)
        tri_b = keep("tri_b", [TP, TP], BF16)
        b1T = keep("b1T", [P, NE * HT])
        b2T = keep("b2T", [P, NE * KD])
        gwT = keep("gwT", [P, KD, NE])
        gate_b_all = keep("gate_b_all", [TP, NE])
        stats = keep("stats", [TP, 2, 6])
        mv = keep("mv", [TP, T + 1, 2])
        sd = keep("sd", [TP, T])
        rstd = keep("rstd", [TP, T + 1])
        eps_c = keep("eps_c", [TP, 1])
        scat_idx = keep("scat_idx", [TP, TOPK * T], U32)
        gath_idx = keep("gath_idx", [TP, TOPK * T], U32)
        comb_w = keep("comb_w", [TP, TOPK * T])

        graph = Region(nc, keep.at)
        A = graph("A", [TP, T, AW])
        Wcat = graph("Wcat", [P, KD, 2 * D + NF])
        Mq = graph("Mq", [P, KD, NF])
        Wo = graph("Wo", [P, KD, D])
        alpha_neg = graph("alpha_neg", [TP, 1])
        bo_all = graph("bo_all", [TP, D])
        iota_r = graph("iota_r", [P, P])
        iota_k = graph("iota_k", [P, KEYS])
        col_r = graph("col_r", [P, G, GC])
        col_key = graph("col_key", [P, G, GC])
        col_w = graph("col_w", [P, G, GC, 2])
        col_blk = graph("col_blk", [P, G, GC])
        col_dst = graph("col_dst", [P, G, GC])
        first_dst = graph("first_dst", [1, G], I32)
        flag = graph("flag", [1, 1], I32)
        KV = graph("KV", [P, 2, 260])

        shared = graph.at
        H = graph("H", [TP, T, D])
        QT = graph("QT", [P, 2, N])
        xnT = graph("xnT", [P, KD, TP])
        V = graph("V", [TP, D])
        Kf = graph("Kf", [TP, NF])
        k_min = graph("k_min", [TP, NF])
        k_exp = graph("k_exp", [TP, NF])
        q_min = graph("q_min", [P, 2 * TP])
        q_exp = graph("q_exp", [P, 2 * TP])
        late = max(graph.at, shared + 4 * (KD * 2 * D * 2 + KD * D))
        graph = Region(nc, late)
        xn = graph("xn", [TP, D])
        src_w = graph("src_w", [P, RING, GC, 2 * P], F32R)
        key1h = graph("key1h", [P, RING, GC, KEYS], F32R)
        away = graph("away", [P, RING, GC, KEYS])
        win_lo = graph("win_lo", [P, 1])
        gen_rel = graph("gen_rel", [P, GC])
        gen_in = graph("gen_in", [P, GC])
        gen_key = graph("gen_key", [P, GC])

        first = Region(nc, shared)
        raw_qk = first("raw_qk", [P, KD, 2 * D])
        qkT = first("qkT", [P, 2 * KD, D])
        raw_g = first("raw_g", [P, KD, D])
        assert first.at <= late
        first = Region(nc, late)
        gw_row = first("gw_row", [NE, D])
        Rbd = first("Rbd", [P, 2 * FD])
        row_src = first("row_src", [G, GE], I32)
        row_dst = first("row_dst", [G, GE], I32)
        row_w = first("row_w", [G, GE])
        valid = first("valid", [G, GE])
        src_f = first("src_f", [G, GE])
        dst_f = first("dst_f", [G, GE])
        blk_i = first("blk_i", [G, GE], I32)
        blk_f = first("blk_f", [G, GE])
        r_f = first("r_f", [G, GE])
        rel = first("rel", [G, GE])
        inside = first("inside", [G, GE])
        key_f = first("key_f", [G, GE])
        w_hi = first("w_hi", [G, GE], F32R)
        w_lo = first("w_lo", [G, GE])
        n_in = first("n_in", [G, 1])
        b1_row = first("b1_row", [NE * HT, P])
        b2_row = first("b2_row", [NE * KD, P])
        zero_rows = first("zero_rows", [SB2, D])

        second = Region(nc, late)
        Qt = second("Qt", [P, 2, TP])
        At = second("At", [TP, T, TP])
        zn = second("zn", [TP, D])
        zrec = second("zrec", [TP, 2, NH])
        znT = second("znT", [P, KD, TP])
        agg_pos = second("agg_pos", [TP, D])
        agg_neg = second("agg_neg", [TP, D])

        moe = Region(nc, keep.at)
        raw = moe("raw", [P, 2 * NCH, CH, 512])
        over_ = moe.at
        xn2 = moe("xn2", [TP, T, D])
        xn2T = moe("xn2T", [P, 2, KD, TP])
        shp = [TP, T, NE]
        flat = [TP, T * NE]
        lg = moe("lg", shp)
        mx = moe("mx", [TP, T])
        ex = moe("ex", shp)
        sm = moe("sm", [TP, 2, T])
        pr = moe("pr", shp)
        cmp_gt = moe("cmp_gt", [TP, T * NE, NE])
        cmp_eq = moe("cmp_eq", [TP, T * NE, NE])
        lower_e = moe("lower_e", [TP, NE, NE])
        rank = moe("rank", flat)
        is_k = moe("is_k", [TP, TOPK, T * NE])
        routed = moe("routed", flat)
        wm = moe("wm", flat)
        bits = moe("bits", [TP, 3, NE], I32)
        thr = moe("thr", [TP, NE], I32)
        cand = moe("cand", [TP, 3, NE], I32)
        over = moe("over", [TP, 3, T * NE], BF16)
        n_over = moe("n_over", [TP, 3, NE])
        grown = moe("grown", [TP, 3, NE])
        more = moe("more", [TP, NE], I32)
        above = moe("above", flat, BF16)
        tied = moe("tied", flat, BF16)
        room = moe("room", [TP, 2, NE])
        fits = moe("fits", [TP, 2, T * NE])
        sel = moe("sel", flat, BF16)
        first_row = moe("first_row", flat)
        slot = moe("slot", [TP, 2, T * NE])
        p_sel = moe("p_sel", flat)
        trash = moe("trash", [TP, TOPK * T])
        pick = moe("pick", [TP, 3, TOPK, T * NE])
        sel_k = moe("sel_k", [TP, 2, TOPK * T])
        slot_k = moe("slot_k", [TP, TOPK * T])
        scat_f = moe("scat_f", [TP, 2, TOPK * T])
        em = Region(nc, over_)
        xg = em("xg", [SB2, 2, D])
        xgT = em("xgT", [P, KD, SLOTS])
        yT = em("yT", [P, KD, SLOTS])
        y = em("y", [SB2, 2, D])
        hid = em("hid", [P, HT, SLOTS])
        cm = Region(nc, keep.at)
        got = cm("got", [TP, 4, TOPK, D])
        part = cm("part", [TP, 4, D])
        res = cm("res", [TP, 4, D])

        rows_zeroed = sem("rows_zeroed"); edges_in = sem("edges_in"); x_in = sem("x_in")
        qk_in = sem("qk_in"); r_in = sem("r_in"); g_in = sem("g_in"); v_in = sem("v_in")
        small_in = sem("small_in"); wo_in = sem("wo_in"); bo_in = sem("bo_in")
        ident_made = sem("ident_made"); consts_made = sem("consts_made"); A_step = sem("A_step")
        xg_zeroed = sem("xg_zeroed")
        edge_step = sem("edge_step"); ln_step = sem("ln_step"); std_done = sem("std_done")
        pe_setup = sem("pe_setup"); act_setup = sem("act_setup")
        xn_ready = sem("xn_ready"); xnT_out = sem("xnT_out"); xnT_ready = sem("xnT_ready")
        h_out = sem("h_out"); h_ready = sem("h_ready"); v_out = sem("v_out"); v_ready = sem("v_ready")
        k_out = sem("k_out"); kmin_ready = sem("kmin_ready"); kexp_ready = sem("kexp_ready")
        kf_ready = sem("kf_ready"); q_out = sem("q_out"); qmin_ready = sem("qmin_ready")
        qexp_ready = sem("qexp_ready"); qt_ready = sem("qt_ready"); kv_out = sem("kv_out")
        away_ready = sem("away_ready"); square_ready = sem("square_ready")
        key_ready = sem("key_ready"); src_ready = sem("src_ready"); grp_out = sem("grp_out")
        gen_step = sem("gen_step"); gen_w = sem("gen_w"); waited_apart = sem("waited_apart"); gen_out = sem("gen_out"); A_final = sem("A_final")
        kv_ready = sem("kv_ready")
        qt_c = sem("qt_c"); at_c = sem("at_c"); z_out = sem("z_out"); zrec_step = sem("zrec_step")
        zn_ready = sem("zn_ready"); znT_out = sem("znT_out"); znT_ready = sem("znT_ready")
        agg_out = sem("agg_out"); agg_parts = sem("agg_parts"); mix_out = sem("mix_out"); x2_step = sem("x2_step")
        x2_ready = sem("x2_ready")
        ln2_step = sem("ln2_step"); std2_done = sem("std2_done"); xn2_ready = sem("xn2_ready")
        xn2T_out = sem("xn2T_out"); xn2T_ready = sem("xn2T_ready"); gate_out = sem("gate_out")
        route_consts = sem("route_consts"); route_step = sem("route_step"); exp_ready = sem("exp_ready")
        over_ready = sem("over_ready"); over_out = sem("over_out"); srch_step = sem("srch_step")
        mask_ready = sem("mask_ready"); rank_out = sem("rank_out"); idx_ready = sem("idx_ready")
        scattered = sem("scattered")
        raw_in = [sem(f"raw_in{i}") for i in range(2 * NCH)]
        piece_out = sem("piece_out")
        xg_in = sem("xg_in"); xgT_out = sem("xgT_out"); xgT_ready = sem("xgT_ready")
        hid_out = sem("hid_out"); gelu_done = sem("gelu_done"); yT_ready = sem("yT_ready")
        y_out = sem("y_out"); y_half = sem("y_half"); y_ready = sem("y_ready"); y_stored = sem("y_stored")
        got_in = [sem(f"got_in{i}") for i in range(4)]
        part_ready = sem("part_ready"); res_ready = sem("res_ready")
        stored = [sem(f"stored{i}") for i in range(4)]

        EDGE_STEPS, EXP_AT, GEN_STEPS, SRCH, ROUNDS = 8, 3, 8, 5, 15
        S_EDGE, S_SMALL, S_QKT, S_MAP, S_GT = 6, 8, 8, 16, 20
        N_SETUP = 24
        block = ctx.enter_context(nc.Block())

        def bc(ap, shape):
            return ap.to_broadcast(shape)

        def row3(t):
            return t[:, :].rearrange("g (c p) -> g c p", c=GC)

        @block.sync
        def _(sp):
            sp.wait_ge(rows_zeroed, 1)
            for row, vec in ((row_src, src), (row_dst, dst), (row_w, edge_weight)):
                sp.dma_start(row[0:FULL, :], vec[0:FULL * GE].rearrange("(g e) -> g e", e=GE)).then_inc(edges_in, 16)
                sp.dma_start(row[FULL:FULL + 1, 0:TAIL], vec[FULL * GE:E].rearrange("(a e) -> a e", a=1)).then_inc(edges_in, 16)
            sp.dma_start(raw_qk[:], W_qkv[:, 0:2 * D].rearrange("(k p) n -> p k n", p=P)).then_inc(qk_in, 16)
            sp.wait_ge(consts_made, 1)
            for j in range(2):
                sp.dma_start(Rbd[j * HD:(j + 1) * HD, j * FD:(j + 1) * FD], R_feat).then_inc(r_in, 16)
            sp.dma_start(X[:, 0:T, :], x.rearrange("(t p) d -> p t d", p=TP)).then_inc(x_in, 16)
            sp.dma_start(raw_g[:], gnn_W.rearrange("(k p) n -> p k n", p=P)).then_inc(g_in, 16)
            sp.dma_start(Wcat[:, :, D:2 * D], W_qkv[:, 2 * D:3 * D].rearrange("(k p) n -> p k n", p=P)).then_inc(v_in, 16)
            sp.dma_start(Wo[:], W_out.rearrange("(k p) n -> p k n", p=P)).then_inc(wo_in, 16)
            sp.dma_start(bo_all[:], b_out.partition_broadcast(TP)).then_inc(bo_in, 16)
            sp.dma_start(xg_rows[0:TRASH, :].rearrange("(b p) d -> p b d", p=SB2),
                         bc(zero_rows[:, :].unsqueeze(1), [SB2, TRASH // SB2, D])).then_inc(xg_zeroed, 16)
            sp.wait_ge(x2_ready, T)

            def load_piece(e, c):
                if c < NCH:
                    part = w1[ds(e, 1), :, c * 512:(c + 1) * 512].rearrange("e (k p) h -> p (e k) h", p=P)
                else:
                    part = w2[ds(e, 1), (c - NCH) * 512:(c - NCH + 1) * 512, :].rearrange("e (j p) d -> p (e j) d", p=P)
                sp.dma_start(raw[:, c], part).then_inc(raw_in[c], 16)

            def load_xg(e):
                sp.dma_start(xg[:], xg_rows[ds(e * SLOTS, SLOTS), :].rearrange("(c p) d -> p c d", p=SB2)).then_inc(xg_in, 16)

            for c in range(2 * NCH):
                load_piece(0, c)
            sp.wait_ge(scattered, 16 * TOPK * T)
            sp.wait_ge(xg_zeroed, 16)
            load_xg(0)

            def store_y(e):
                sp.wait_ge(y_ready, 2 * e + 4)
                sp.dma_start(y_rows[ds(e * SLOTS, SLOTS), :].rearrange("(c p) d -> p c d", p=SB2), y[:]).then_inc(y_stored, 16)

            with sp.Fori(0, NE - 1) as e:
                sp.wait_ge(xgT_out, e * 2 + 2)
                load_xg(e + 1)
                for c in range(2 * NCH):
                    if c < NCH:
                        sp.wait_ge(hid_out, e * HT + CH * (c + 1))
                    else:
                        sp.wait_ge(piece_out, e * NCH + (c - NCH + 1))
                    load_piece(e + 1, c)
                store_y(e)
            store_y(NE - 1)
            for t in range(T):
                sp.wait_ge(res_ready, t + 1)
                sp.dma_start(out[t * TP:(t + 1) * TP, :], res[:, t % 4, :]).then_inc(stored[t % 4], 16)
            for i in range(4):
                sp.wait_ge(stored[i], 16 * len(range(i, T, 4)))

        @block.gpsimd
        def _(pool):
            g = nc.gpsimd
            for row in (row_src, row_dst, row_w):
                last = g.memset(row[:], 0)
            last.then_inc(rows_zeroed, 1)
            g.memset(ident[:], 0.0).then_inc(ident_made, 1)
            g.memset(valid[:], 1.0)
            g.memset(zero_rows[:], 0.0)
            g.memset(ones_f[:], 1.0)
            g.memset(Rbd[:], 0.0).then_inc(consts_made, 1)
            pool.wait_ge(consts_made, 1)
            g.affine_select(out=ident[:], in_=ident[:], compare_op=ALU.not_equal, fill=1.0, base=0,
                            pattern=[[-1, P]], channel_multiplier=1).then_inc(ident_made, 1)
            g.affine_select(out=valid[:], in_=valid[:], compare_op=ALU.is_gt, fill=0.0, base=E,
                            pattern=[[-1, GE]], channel_multiplier=-GE).then_inc(consts_made, 1)
            g.iota(iota_r[:], [[1, P]], base=0, channel_multiplier=0, allow_small_or_imprecise_dtypes=True)
            g.iota(iota_k[:], [[1, KEYS]], base=0, channel_multiplier=0, allow_small_or_imprecise_dtypes=True)
            g.memset(eps_c[:], EPS)
            g.memset(X[:, T, :], 0.0)
            g.memset(mv[:, T, :], 0.0)
            g.memset(rstd[:, T:T + 1], 0.0)
            g.memset(KV[:], 0.0)
            g.memset(ones_b[:], 1.0)
            g.memset(tri_b[:], 1.0).then_inc(consts_made, 1)
            pool.wait_ge(consts_made, 3)
            g.affine_select(out=tri_b[:], in_=tri_b[:], compare_op=ALU.is_gt, fill=0.0, base=0,
                            pattern=[[1, TP]], channel_multiplier=-1).then_inc(consts_made, 1)
            g.memset(A[:], 0.0).then_inc(A_step, 1)
            g.dma_start(b1_row[:], b1.rearrange("e (j p) -> (e j) p", p=P)).then_inc(small_in, 16)
            g.dma_start(b2_row[:], b2.rearrange("e (j p) -> (e j) p", p=P)).then_inc(small_in, 16)
            g.dma_start(gw_row[:], gate_w).then_inc(small_in, 16)
            g.dma_start(gate_b_all[:], gate_b.partition_broadcast(TP)).then_inc(small_in, 16)
            g.dma_start(alpha_neg[:], gnn_alpha.partition_broadcast(TP)).then_inc(small_in, 16)

            def distances(gi, s):
                g.tensor_tensor(away[:, s], bc(iota_k[:, :].unsqueeze(1), [P, GC, KEYS]),
                                bc(col_key[:, ds(gi, 1), :].rearrange("p a c -> p (a c)").unsqueeze(2), [P, GC, KEYS]),
                                ALU.subtract).then_inc(away_ready, 1)

            pool.wait_ge(act_setup, N_SETUP)
            for s in range(RING):
                distances(s, s)
            with pool.Fori(1, G // RING) as n:
                for s in range(RING):
                    pool.wait_ge(key_ready, n * RING + (s + 1 - RING))
                    distances(n * RING + s, s)

            pool.wait_ge(x2_ready, T)
            g.memset(lower_e[:], 1.0).then_inc(route_consts, 1)
            pool.wait_ge(route_consts, 1)
            g.affine_select(out=lower_e[:], in_=lower_e[:], compare_op=ALU.is_gt, fill=0.0, base=0,
                            pattern=[[1, NE], [-1, NE]], channel_multiplier=0).then_inc(route_consts, 1)
            g.iota(first_row[:], [[0, T], [SLOTS, NE]], base=0, channel_multiplier=0, allow_small_or_imprecise_dtypes=True)
            g.iota(trash[:], [[N, TOPK], [TP, T]], base=TRASH, channel_multiplier=1,
                   allow_small_or_imprecise_dtypes=True).then_inc(route_consts, 1)
            pool.wait_ge(idx_ready, 1)
            pool.wait_ge(xg_zeroed, 16)
            for t in range(T):
                for k in range(TOPK):
                    g.indirect_dma_start(out=xg_rows, out_offset=bass.IndirectOffsetOnAxis(ap=scat_idx[:, k * T + t:k * T + t + 1], axis=0),
                                         in_=xn2[:, t, :], in_offset=None).then_inc(scattered, 16)
            pool.wait_ge(y_stored, 16 * (NE + 1))
            for t in range(T):
                if t >= 4:
                    pool.wait_ge(res_ready, t - 3)
                for k in range(TOPK):
                    g.indirect_dma_start(out=got[:, t % 4, k, :], out_offset=None, in_=y_rows,
                                         in_offset=bass.IndirectOffsetOnAxis(ap=gath_idx[:, k * T + t:k * T + t + 1], axis=0)
                                         ).then_inc(got_in[t % 4], 16)

        @block.tensor
        def _(pe):
            mm, tr = nc.tensor.matmul, nc.tensor.transpose

            def begin(k):
                if k >= 8:
                    pe.wait_ge(act_setup, k - 7)
                return bank[k % 8]

            pe.wait_ge(ident_made, 2)
            pe.wait_ge(consts_made, 1)
            pe.wait_ge(edge_step, EDGE_STEPS)
            for k, row in enumerate((r_f, key_f, w_hi, w_lo, blk_f, dst_f)):
                ps = begin(k)
                for j in range(GC):
                    part = row[:, j * P:(j + 1) * P]
                    last = tr(ps[:, j * G:(j + 1) * G], part.bitcast(F32) if row is w_hi else part, ident[0:G, 0:G])
                last.then_inc(pe_setup, 1)
            ps = begin(S_EDGE)
            tr(ps[0:1, 0:G], dst_f[:, 0:1], ident[0:G, 0:G])
            mm(ps[0:1, 128:129], n_in[:], ones_f[0:G, :], start=True, stop=True).then_inc(pe_setup, 1)
            pe.wait_ge(small_in, 80)
            ps = begin(S_EDGE + 1)
            tr(ps[:, 0:NE * HT], b1_row[:], ident[:])
            tr(ps[:, 128:128 + NE * KD], b2_row[:], ident[0:NE * KD, 0:NE * KD])
            for k in range(KD):
                last = tr(ps[:, 160 + k * NE:160 + (k + 1) * NE], gw_row[:, k * P:(k + 1) * P], ident[0:NE, 0:NE])
            last.then_inc(pe_setup, 1)
            pe.wait_ge(qk_in, 16)
            for s in range(2 * KD):
                ps = begin(S_QKT + s)
                for d in range(KD):
                    last = tr(ps[:, d * P:(d + 1) * P], raw_qk[:, d, s * P:(s + 1) * P], ident[:])
                last.then_inc(pe_setup, 1)
            pe.wait_ge(r_in, 32)
            for s in range(4):
                ps = begin(S_MAP + s)
                pe.wait_ge(act_setup, S_MAP)
                for d in range(2):
                    for f in range(KD):
                        row = (s % 2) * 2 + d
                        last = mm(ps[:, d * NF + f * 2 * FD:d * NF + (f + 1) * 2 * FD],
                                  qkT[:, (s // 2) * KD + f, row * P:(row + 1) * P], Rbd[:], start=True, stop=True)
                last.then_inc(pe_setup, 1)
            pe.wait_ge(g_in, 16)
            for s in range(KD):
                ps = begin(S_GT + s)
                for o in range(KD):
                    last = tr(ps[:, o * P:(o + 1) * P], raw_g[:, o, s * P:(s + 1) * P], ident[:])
                last.then_inc(pe_setup, 1)
            pe.wait_ge(act_setup, N_SETUP)
            pe.wait_ge(v_in, 16)

            PT, PA, PB, PKV, PKS = bank[3], bank[4], bank[5], bank[6], bank[7]

            def products(ps, slot):
                for j in range(GC):
                    for part in range(2):
                        last = mm(ps[:, 0:KEYS], src_w[:, slot, j, part * P:(part + 1) * P], key1h[:, slot, j, :],
                                  start=(j == 0 and part == 0), stop=(j == GC - 1 and part == 1))
                return last

            def group(gi, s):
                pe.wait_ge(src_ready, gi + 1)
                pe.wait_ge(key_ready, gi + 1)
                products(bank[s % PSR], s % RING).then_inc(grp_out, 1)

            def tile_work(i, first):
                G_ = lambda s: group(i * GPI + s, s)
                pe.wait_ge(xn_ready, i + 1)
                for k in range(KD):
                    last = tr(PT[:, k * TP:(k + 1) * TP], xn[:, k * P:(k + 1) * P], ident[0:TP, 0:TP])
                last.then_inc(xnT_out, 1)
                G_(0)
                pe.wait_ge(xnT_ready, i + 1)
                for k in range(KD):
                    last = mm(PA[0:TP, :], xnT[:, k, :], Wcat[:, k, 0:D], start=(k == 0), stop=(k == KD - 1))
                last.then_inc(h_out, 1)
                G_(1)
                for k in range(KD):
                    last = mm(PB[0:TP, :], xnT[:, k, :], Wcat[:, k, D:2 * D], start=(k == 0), stop=(k == KD - 1))
                last.then_inc(v_out, 1)
                G_(2)
                pe.wait_ge(h_ready, i + 1)
                for k in range(KD):
                    last = mm(PA[0:TP, 0:NF], xnT[:, k, :], Wcat[:, k, 2 * D:], start=(k == 0), stop=(k == KD - 1))
                last.then_inc(k_out, 1)
                G_(3)
                pe.wait_ge(v_ready, i + 1)
                for m in range(2):
                    for k in range(KD):
                        last = mm(PB[:, m * TP:(m + 1) * TP], Mq[:, k, m * P:(m + 1) * P], xnT[:, k, :],
                                  start=(k == 0), stop=(k == KD - 1))
                last.then_inc(q_out, 1)
                G_(4)
                pe.wait_ge(kf_ready, i + 1)
                for m in range(2):
                    mm(PKV[:, m * 256:(m + 1) * 256], Kf[:, m * P:(m + 1) * P], V[:, m * 256:(m + 1) * 256],
                       start=(first and m == 0), stop=False, skip_group_check=True)
                    last = mm(PKS[:, m:m + 1], Kf[:, m * P:(m + 1) * P], ones_f[0:TP, :],
                              start=(first and m == 0), stop=False, skip_group_check=True)
                last.then_inc(kv_out, 1)
                G_(5)

            pe.nop().then_inc(grp_out, 1)
            tile_work(0, True)
            with pe.Fori(1, T) as i:
                tile_work(i, False)
            with pe.Fori(T, TURNS) as i:
                for s in range(GPI):
                    group(i * GPI + s, s)

            some = pe.value_load(flag[0:1, 0:1], min_val=0, max_val=G * GE)
            with pe.If(some):
                pe.nop().then_inc(gen_out, 1)
                with pe.Fori(0, NWIN * G) as n:
                    pe.wait_ge(gen_step, n * GEN_STEPS + 7)
                    products(bank[0], 0).then_inc(gen_out, 1)

            PZ, PN, PG, PM = bank[4], bank[5], bank[0], bank[1]
            pe.wait_ge(kv_ready, 1)
            pe.wait_ge(A_final, 1)
            pe.wait_ge(wo_in, 16)
            with pe.Fori(0, T) as t:
                pe.wait_ge(qt_c, t + 1)
                for m in range(2):
                    mm(PZ[0:TP, m * 256:(m + 1) * 256], Qt[:, m, :], KV[:, m, 0:256], start=True, stop=True)
                    last = mm(PN[0:TP, m * 4:(m + 1) * 4], Qt[:, m, :], KV[:, m, 256:260], start=True, stop=True)
                last.then_inc(z_out, 1)
                pe.wait_ge(at_c, t + 1)
                for b in range(T):
                    last = mm(PG[0:TP, :], At[:, b, :], H[:, b, :], start=(b == 0), stop=(b == T - 1))
                last.then_inc(agg_out, 1)
                pe.wait_ge(zn_ready, t + 1)
                for k in range(KD):
                    last = tr(PT[:, k * TP:(k + 1) * TP], zn[:, k * P:(k + 1) * P], ident[0:TP, 0:TP])
                last.then_inc(znT_out, 1)
                pe.wait_ge(znT_ready, t + 1)
                for k in range(KD):
                    last = mm(PM[0:TP, :], znT[:, k, :], Wo[:, k, :], start=(k == 0), stop=(k == KD - 1))
                last.then_inc(mix_out, 1)

            PL = bank[7]
            pe.wait_ge(x2_ready, T)
            for i in range(T // 2):
                for u in range(2):
                    pe.wait_ge(xn2_ready, 2 * i + u + 1)
                    for k in range(KD):
                        last = tr(bank[3 + u][:, k * TP:(k + 1) * TP], xn2[:, 2 * i + u, k * P:(k + 1) * P], ident[0:TP, 0:TP])
                    last.then_inc(xn2T_out, 1)
                for u in range(2):
                    t = 2 * i + u
                    pe.wait_ge(xn2T_ready, t + 1)
                    for k in range(KD):
                        last = mm(PL[0:TP, t * NE:(t + 1) * NE], xn2T[:, u, k, :], gwT[:, k, :], start=(k == 0), stop=(k == KD - 1))
                    last.then_inc(gate_out, 1)

            pe.wait_ge(consts_made, 4)
            with pe.Fori(0, ROUNDS) as n:
                pe.wait_ge(over_ready, n + 1)
                mm(bank[0][0:TP, 0:3 * T * NE], ones_b[:], over[:, :, :].rearrange("p j f -> p (j f)"),
                   start=True, stop=True).then_inc(over_out, 1)

            def ranks(ps, mask):
                mm(ps[0:TP, 0:T * NE], tri_b[:], mask[:], start=True, stop=False, skip_group_check=True)
                for s in range(1, T):
                    last = mm(ps[0:TP, s * NE:T * NE], ones_b[:], mask[:, 0:(T - s) * NE], start=False,
                              stop=(s == T - 1), skip_group_check=True)
                last.then_inc(rank_out, 1)

            pe.wait_ge(mask_ready, 2)
            mm(bank[1][0:TP, 0:T * NE], ones_b[:], above[:], start=True, stop=True).then_inc(rank_out, 1)
            ranks(bank[2], tied)
            pe.wait_ge(mask_ready, 3)
            ranks(bank[3], sel)

            PH, PX, PO = (bank[0], bank[1]), (bank[2], bank[3]), bank[4:8]

            def turn_in(e):
                pe.wait_ge(xg_in, (e + 1) * 16)
                for h in range(2):
                    for k in range(2):
                        for c in range(2):
                            o = k * SLOTS + c * SB2
                            last = tr(PX[h][:, o:o + SB2], xg[:, c, (2 * h + k) * P:(2 * h + k + 1) * P], ident[0:SB2, 0:SB2])
                    last.then_inc(xgT_out, 1)

            def expert(e, last_one):
                pe.wait_ge(xgT_ready, e * 2 + 2)
                pe.wait_ge(y_ready, e * 2 + 2)
                for c in range(NCH):
                    pe.wait_ge(raw_in[c], (e + 1) * 16)
                    for q in range(CH * c, CH * c + CH):
                        pe.wait_ge(gelu_done, e * HT + (q + 1))
                        for k in range(KD):
                            last = mm(PH[q % 2][:, 0:SLOTS], raw[:, c, k, (q % CH) * P:(q % CH + 1) * P], xgT[:, k, :],
                                      start=(k == 0), stop=(k == KD - 1))
                        last.then_inc(hid_out, 1)
                for c in range(NCH, 2 * NCH):
                    pe.wait_ge(raw_in[c], (e + 1) * 16)
                    for j in range(CH):
                        q = CH * (c - NCH) + j
                        pe.wait_ge(gelu_done, e * HT + (q + 3))
                        for d in range(KD):
                            last = mm(PO[d][:, 0:SLOTS], raw[:, c, j, d * P:(d + 1) * P], hid[:, q, :],
                                      start=(q == 0), stop=(q == HT - 1))
                    last.then_inc(piece_out, 1)
                if not last_one:
                    turn_in(e + 1)
                pe.wait_ge(yT_ready, e + 1)
                for c in range(2):
                    for d in range(KD):
                        last = tr(PH[c][0:SB2, d * P:(d + 1) * P], yT[:, d, c * SB2:(c + 1) * SB2], ident[:])
                    last.then_inc(y_out, 1)

            turn_in(0)
            with pe.Fori(0, NE - 1) as e:
                expert(e, False)
            expert(NE - 1, True)

        @block.scalar
        def _(act):
            av = nc.scalar.activation

            def take(k):
                act.wait_ge(pe_setup, k + 1)
                return bank[k % 8]

            for k, col in enumerate((col_r[:], col_key[:], col_w[:, :, :, 0], col_w[:, :, :, 1], col_blk[:], col_dst[:])):
                ps = take(k)
                av(col, ps[:, 0:GC * G].rearrange("p (c g) -> p g c", c=GC), ACT.Copy).then_inc(act_setup, 1)
            ps = take(S_EDGE)
            av(first_dst[:], ps[0:1, 0:G], ACT.Copy)
            av(flag[:], ps[0:1, 128:129], ACT.Relu, bias=float(G * GE), scale=-1.0).then_inc(act_setup, 1)
            ps = take(S_EDGE + 1)
            av(b1T[:], ps[:, 0:NE * HT], ACT.Copy)
            av(b2T[:], ps[:, 128:128 + NE * KD], ACT.Copy)
            av(gwT[:, :, :], ps[:, 160:160 + KD * NE].rearrange("p (k e) -> p k e", k=KD), ACT.Copy).then_inc(act_setup, 1)
            for s in range(2 * KD):
                ps = take(S_QKT + s)
                av(qkT[:, s, :], ps[:], ACT.Copy).then_inc(act_setup, 1)
            for s in range(4):
                ps = take(S_MAP + s)
                half = slice((s % 2) * 2, (s % 2) * 2 + 2)
                to = Mq[:, half, :] if s < 2 else Wcat[:, half, 2 * D:]
                av(to, ps[:].rearrange("p (d n) -> p d n", d=2), ACT.Copy).then_inc(act_setup, 1)
            for s in range(KD):
                ps = take(S_GT + s)
                av(Wcat[:, s, 0:D], ps[:], ACT.Copy).then_inc(act_setup, 1)
            act.wait_ge(ln_step, 2 * T)
            act.wait_ge(consts_made, 3)
            av(sd[:], mv[:, 0:T, 1], ACT.Sqrt, bias=eps_c[:]).then_inc(std_done, 1)

            PT, PA, PB, PKV, PKS = bank[3], bank[4], bank[5], bank[6], bank[7]
            def square(gi, s):
                act.wait_ge(away_ready, gi + 1)
                av(away[:, s % RING], away[:, s % RING], ACT.Square).then_inc(square_ready, 1)

            def one_hot(gi, s, free=None):
                act.wait_ge(square_ready, gi + 1)
                if free is not None:
                    act.wait_ge(grp_out, free)
                av(key1h[:, s % RING], away[:, s % RING], ACT.Relu, bias=1.0, scale=-1.0).then_inc(key_ready, 1)

            def ahead(i, s, last_turn=False):
                gi = i * GPI
                if not last_turn or s + 1 < GPI:
                    one_hot(gi + (s + 1), s + 1, gi + (s + 1))
                if not last_turn or s + 2 < GPI:
                    square(gi + (s + 2), s + 2)

            square(0, 0)
            square(1, 1)
            one_hot(0, 0)
            with act.Fori(0, T) as i:
                act.wait_ge(xnT_out, i + 1)
                av(xnT[:], PT[:, 0:KD * TP].rearrange("p (k t) -> p k t", k=KD), ACT.Copy).then_inc(xnT_ready, 1)
                ahead(i, 0)
                act.wait_ge(h_out, i + 1)
                av(H[:, ds(i, 1), :].rearrange("p a d -> p (a d)"), PA[0:TP, :], ACT.Copy).then_inc(h_ready, 1)
                ahead(i, 1)
                act.wait_ge(v_out, i + 1)
                av(V[:], PB[0:TP, :], ACT.Copy).then_inc(v_ready, 1)
                ahead(i, 2)
                act.wait_ge(kmin_ready, i + 1)
                av(k_exp[:], k_min[:], ACT.Exp).then_inc(kexp_ready, 1)
                ahead(i, 3)
                act.wait_ge(qmin_ready, i + 1)
                av(q_exp[:], q_min[:], ACT.Exp).then_inc(qexp_ready, 1)
                ahead(i, 4)
                ahead(i, 5)
            for s in range(GPI):
                ahead(TURNS - 1, s, last_turn=True)

            act.wait_ge(kv_out, T)
            for m in range(2):
                for h in range(4):
                    p = slice(h * FD, (h + 1) * FD)
                    av(KV[p, m, h * HD:(h + 1) * HD], PKV[p, m * 256 + h * HD:m * 256 + (h + 1) * HD], ACT.Copy)
                    last = av(KV[p, m, 256 + h:257 + h], PKS[p, m:m + 1], ACT.Copy)
            last.then_inc(kv_ready, 1)

            PG = bank[0]
            act.wait_ge(A_final, 1)
            act.wait_ge(qt_ready, T)
            with act.Fori(0, T) as t:
                av(Qt[:], QT[:, :, ds(t * TP, TP)], ACT.Copy).then_inc(qt_c, 1)
                av(At[:], A[:, :, ds(t * TP, TP)], ACT.Copy).then_inc(at_c, 1)
                act.wait_ge(znT_out, t + 1)
                av(znT[:], PT[:, 0:KD * TP].rearrange("p (k t) -> p k t", k=KD), ACT.Copy).then_inc(znT_ready, 1)
                av(agg_pos[:], PG[0:TP, :], ACT.Relu)
                av(agg_neg[:], PG[0:TP, :], ACT.Relu, scale=-1.0).then_inc(agg_parts, 1)

            act.wait_ge(x2_ready, T)
            av(sd[:], mv[:, 0:T, 1], ACT.Sqrt, bias=eps_c[:]).then_inc(std2_done, 1)
            for t in range(T):
                act.wait_ge(xn2T_out, t + 1)
                av(xn2T[:, t % 2], bank[3 + t % 2][:, 0:KD * TP].rearrange("p (k t) -> p k t", k=KD), ACT.Copy).then_inc(xn2T_ready, 1)
            act.wait_ge(route_step, EXP_AT)
            av(ex[:], lg[:], ACT.Exp).then_inc(exp_ready, 1)

            PH, PX = (bank[0], bank[1]), (bank[2], bank[3])

            def xg_take(e):
                for h in range(2):
                    act.wait_ge(xgT_out, e * 2 + (h + 1))
                    av(xgT[:, 2 * h:2 * h + 2, :], PX[h][:, 0:2 * SLOTS].rearrange("p (k c) -> p k c", k=2), ACT.Copy).then_inc(xgT_ready, 1)

            def expert(e, last_one):
                for q in range(HT):
                    act.wait_ge(hid_out, e * HT + (q + 1))
                    av(hid[:, q, :], PH[q % 2][:, 0:SLOTS], ACT.Gelu, bias=b1T[:, ds(e * HT + q, 1)]).then_inc(gelu_done, 1)
                if not last_one:
                    xg_take(e + 1)
                act.wait_ge(y_out, e * 2 + 1)
                act.wait_ge(y_stored, (e + 1) * 16)
                av(y[:, 0, :], PH[0][0:SB2, :], ACT.Copy).then_inc(y_ready, 1)

            act.nop().then_inc(gelu_done, 2)
            act.nop().then_inc(y_ready, 2)
            act.nop().then_inc(y_stored, 16)
            xg_take(0)
            with act.Fori(0, NE - 1) as e:
                expert(e, False)
            expert(NE - 1, True)

        @block.vector
        def _(dve):
            v = nc.vector

            step = Chain(dve, edge_step)
            dve.wait_ge(edges_in, 96)
            v.tensor_copy(w_hi[:], row_w[:])
            v.tensor_copy(src_f[:], row_src[:])
            step(v.tensor_copy(dst_f[:], row_dst[:]))
            v.tensor_tensor(w_lo[:], row_w[:], w_hi[:].bitcast(F32), ALU.subtract)
            v.tensor_scalar(blk_i[:], src_f[:], 1.0 / TP, -((TP - 1) / 2) / TP, ALU.mult, ALU.add)
            step(v.tensor_scalar(rel[:], dst_f[:], dst_f[:, 0:1], None, ALU.subtract))
            dve.wait_ge(consts_made, 2)
            v.tensor_copy(blk_f[:], blk_i[:])
            step(v.tensor_tensor(rel[:], rel[:], valid[:], ALU.mult))
            v.scalar_tensor_tensor(out=r_f[:], in0=blk_f[:], scalar=-float(TP), in1=src_f[:], op0=ALU.mult, op1=ALU.add)
            step(v.tensor_scalar(inside[:], rel[:], 0.0, None, ALU.is_ge))
            step(v.scalar_tensor_tensor(out=inside[:], in0=rel[:], scalar=float(WIN), in1=inside[:], op0=ALU.is_lt, op1=ALU.mult))
            v.tensor_reduce(n_in[:], inside[:], AX_X, ALU.add)
            step(v.scalar_tensor_tensor(out=key_f[:], in0=blk_f[:], scalar=float(WIN), in1=rel[:], op0=ALU.mult, op1=ALU.add))
            step(v.scalar_tensor_tensor(out=key_f[:], in0=key_f[:], scalar=1.0, in1=inside[:], op0=ALU.add, op1=ALU.mult))
            step(v.tensor_scalar(key_f[:], key_f[:], -1.0, None, ALU.add))
            assert step.n == EDGE_STEPS

            ln = Chain(dve, ln_step)
            dve.wait_ge(x_in, 16)
            for t in range(T):
                ln(v.bn_stats(stats[:, 0, :], X[:, t, :]))
                ln(v.bn_aggr(mv[:, t, :], stats[:, 0, :]))
            dve.wait_ge(std_done, 1)
            dve.wait_ge(consts_made, 3)
            ln(v.reciprocal(rstd[:, 0:T], sd[:]))
            dve.wait_ge(small_in, 80)
            ln(v.tensor_scalar(alpha_neg[:], alpha_neg[:], -1.0, None, ALU.mult))

            PT, PA, PB = bank[3], bank[4], bank[5]

            def wait_apart(sem, value):
                dve.wait_ge(sem, value)
                dve.sem_inc(waited_apart, 1)

            def sources(gi, slot):
                for j in range(GC):
                    last = v.scalar_tensor_tensor(
                        out=src_w[:, slot, j, :].rearrange("p (a k) -> p a k", a=2),
                        in0=bc(iota_r[:, :].unsqueeze(1), [P, 2, P]),
                        scalar=col_r[:, ds(gi, 1), j],
                        in1=bc(col_w[:, ds(gi, 1), j, :].rearrange("p a w -> p (a w)").unsqueeze(2), [P, 2, P]),
                        op0=ALU.is_equal, op1=ALU.mult)
                return last

            def add_group(gi, s):
                at = dve.value_load(first_dst[0:1, ds(gi, 1)], min_val=0, max_val=N - 1)
                dve.wait_ge(grp_out, gi + 2)
                dve.wait_ge(A_step, gi + 1)
                win = A[:, :, ds(at, WIN)]
                v.tensor_tensor(win, win, bank[s % PSR][0:TP, 0:KEYS].rearrange("p (b w) -> p b w", b=T), ALU.add).then_inc(A_step, 1)

            dve.wait_ge(act_setup, S_QKT)
            dve.wait_ge(edge_step, EDGE_STEPS)
            sources(0, 0).then_inc(src_ready, 1)
            dve.wait_ge(act_setup, N_SETUP)

            def norm_tile(i):
                v.tensor_scalar(xn[:], X[:, ds(i, 1), :].rearrange("p a d -> p (a d)"), mv[:, ds(i, 1), 0], rstd[:, ds(i, 1)],
                                ALU.subtract, ALU.mult).then_inc(xn_ready, 1)

            norm_tile(0)
            with dve.Fori(0, T) as i:
                for s in range(GPI):
                    sources(i * GPI + (s + 1), (s + 1) % RING).then_inc(src_ready, 1)
                    if s == 3:
                        dve.wait_ge(k_out, i + 1)
                        v.tensor_scalar(k_min[:], PA[0:TP, 0:NF], 0.0, None, ALU.min).then_inc(kmin_ready, 1)
                    if s == 4:
                        dve.wait_ge(kexp_ready, i + 1)
                        v.scalar_tensor_tensor(out=Kf[:], in0=PA[0:TP, 0:NF], scalar=0.0, in1=k_exp[:],
                                               op0=ALU.max, op1=ALU.add).then_inc(kf_ready, 1)
                        dve.wait_ge(q_out, i + 1)
                        v.tensor_scalar(q_min[:], PB[:, 0:2 * TP], 0.0, None, ALU.min).then_inc(qmin_ready, 1)
                    if s == 5:
                        dve.wait_ge(qexp_ready, i + 1)
                        v.scalar_tensor_tensor(out=QT[:, :, ds(i * TP, TP)], in0=PB[:, 0:2 * TP].rearrange("p (m t) -> p m t", m=2),
                                               scalar=0.0, in1=q_exp[:].rearrange("p (m t) -> p m t", m=2),
                                               op0=ALU.max, op1=ALU.add).then_inc(qt_ready, 1)
                        norm_tile(i + 1)
                    add_group(i * GPI + s, s)
            for s in range(GPI):
                if s + 1 < GPI:
                    sources((TURNS - 1) * GPI + s + 1, (s + 1) % RING).then_inc(src_ready, 1)
                add_group((TURNS - 1) * GPI + s, s)
            dve.wait_ge(A_step, G + 1)

            some = dve.value_load(flag[0:1, 0:1], min_val=0, max_val=G * GE)
            with dve.If(some):
                v.memset(A[:], 0.0)
                v.memset(win_lo[:], -float(WIN)).then_inc(gen_w, 1)
                with dve.Fori(0, NWIN) as w:
                    dve.wait_ge(gen_w, w + 1)
                    v.tensor_scalar(win_lo[:], win_lo[:], float(WIN), None, ALU.add).then_inc(gen_w, 1)
                    wait_apart(gen_w, w + 2)
                    with dve.Fori(0, G) as gi:
                        n = w * G + gi
                        k = [0]

                        def link(ins):
                            k[0] += 1
                            ins.then_inc(gen_step, 1)
                            dve.wait_ge(gen_step, n * GEN_STEPS + k[0])

                        dcol = col_dst[:, ds(gi, 1), :].rearrange("p a c -> p (a c)")
                        bcol = col_blk[:, ds(gi, 1), :].rearrange("p a c -> p (a c)")
                        link(v.tensor_scalar(gen_rel[:], dcol, win_lo[:, 0:1], None, ALU.subtract))
                        link(v.tensor_scalar(gen_in[:], gen_rel[:], 0.0, None, ALU.is_ge))
                        link(v.scalar_tensor_tensor(out=gen_in[:], in0=gen_rel[:], scalar=float(WIN), in1=gen_in[:], op0=ALU.is_lt, op1=ALU.mult))
                        link(v.scalar_tensor_tensor(out=gen_key[:], in0=bcol, scalar=float(WIN), in1=gen_rel[:], op0=ALU.mult, op1=ALU.add))
                        link(v.scalar_tensor_tensor(out=gen_key[:], in0=gen_key[:], scalar=1.0, in1=gen_in[:], op0=ALU.add, op1=ALU.mult))
                        link(v.tensor_scalar(gen_key[:], gen_key[:], -1.0, None, ALU.add))
                        dve.wait_ge(gen_out, n + 1)
                        sources(gi, 0)
                        v.tensor_tensor(key1h[:, 0], bc(iota_k[:, :].unsqueeze(1), [P, GC, KEYS]),
                                        bc(gen_key[:, :].unsqueeze(2), [P, GC, KEYS]), ALU.is_equal).then_inc(gen_step, 1)
                        dve.wait_ge(gen_out, n + 2)
                        win = A[:, :, ds(w * WIN, WIN)]
                        v.tensor_tensor(win, win, bank[0][0:TP, 0:KEYS].rearrange("p (b w) -> p b w", b=T), ALU.add).then_inc(gen_step, 1)
                        dve.wait_ge(gen_step, n * GEN_STEPS + 8)
            v.nop().then_inc(A_final, 1)

            PZ, PN, PM = bank[4], bank[5], bank[1]
            dve.wait_ge(kv_ready, 1)
            with dve.Fori(0, T) as t:
                xt = X[:, ds(t, 1), :].rearrange("p a d -> p (a d)")
                dve.wait_ge(z_out, t + 1)
                v.tensor_scalar(zrec[:, 0, :], PN[0:TP, 0:NH], 1e-6, None, ALU.add).then_inc(zrec_step, 1)
                dve.wait_ge(zrec_step, t * 2 + 1)
                v.reciprocal(zrec[:, 1, :], zrec[:, 0, :]).then_inc(zrec_step, 1)
                dve.wait_ge(zrec_step, t * 2 + 2)
                v.tensor_tensor(zn[:, :].rearrange("p (h f) -> p h f", h=NH), PZ[0:TP, :].rearrange("p (h f) -> p h f", h=NH),
                                bc(zrec[:, 1, :].unsqueeze(2), [TP, NH, HD]), ALU.mult).then_inc(zn_ready, 1)
                dve.wait_ge(agg_parts, t + 1)
                v.scalar_tensor_tensor(out=xt, in0=agg_neg[:], scalar=alpha_neg[:, 0:1], in1=xt, op0=ALU.mult, op1=ALU.add).then_inc(x2_step, 1)
                dve.wait_ge(x2_step, t * 6 + 1)
                v.tensor_tensor(xt, xt, agg_pos[:], ALU.add).then_inc(x2_step, 1)
                dve.wait_ge(x2_step, t * 6 + 2)
                dve.wait_ge(bo_in, 16)
                v.tensor_tensor(xt, xt, bo_all[:], ALU.add).then_inc(x2_step, 1)
                dve.wait_ge(x2_step, t * 6 + 3)
                dve.wait_ge(mix_out, t + 1)
                v.tensor_tensor(xt, xt, PM[0:TP, :], ALU.add).then_inc(x2_step, 1)
                wait_apart(x2_step, t * 6 + 4)
                v.bn_stats(stats[:, 0, :], xt).then_inc(x2_step, 1)
                wait_apart(x2_step, t * 6 + 5)
                v.bn_aggr(stats[:, 1, 0:2], stats[:, 0, :]).then_inc(x2_step, 1)
                dve.wait_ge(x2_step, t * 6 + 6)
                v.tensor_copy(mv[:, ds(t, 1), :].rearrange("p a s -> p (a s)"), stats[:, 1, 0:2]).then_inc(x2_ready, 1)

            dve.wait_ge(std2_done, 1)
            v.reciprocal(rstd[:, 0:T], sd[:]).then_inc(ln2_step, 1)
            dve.wait_ge(ln2_step, 1)
            for t in range(T):
                v.tensor_scalar(xn2[:, t, :], X[:, t, :], mv[:, t, 0:1], rstd[:, t:t + 1], ALU.subtract, ALU.mult).then_inc(xn2_ready, 1)

            st = Chain(dve, route_step)
            PL = bank[7]

            def tv(ap):
                return ap.rearrange("p (t e) -> p t e", e=NE)

            dve.wait_ge(gate_out, T)
            st(v.tensor_tensor(lg[:], tv(PL[0:TP, 0:T * NE]), bc(gate_b_all[:, :].unsqueeze(1), shp), ALU.add))
            st(v.tensor_reduce(mx[:], lg[:], AX_X, ALU.max))
            st(v.tensor_tensor(lg[:], lg[:], bc(mx[:, :].unsqueeze(2), shp), ALU.subtract))
            assert st.n == EXP_AT
            dve.wait_ge(exp_ready, 1)
            st(v.tensor_reduce(sm[:, 0, :], ex[:], AX_X, ALU.add))
            st(v.reciprocal(sm[:, 1, :], sm[:, 0, :]))
            st(v.tensor_tensor(pr[:], ex[:], bc(sm[:, 1, :].unsqueeze(2), shp), ALU.mult))
            prf = pr[:, :, :].rearrange("p t e -> p (t e)")
            others = bc(pr[:, :, :].unsqueeze(2), [TP, T, NE, NE])
            mine = bc(pr[:, :, :].unsqueeze(3), [TP, T, NE, NE])
            c4 = lambda m: m[:, :, :].rearrange("p (t e) f -> p t e f", e=NE)
            v.tensor_tensor(c4(cmp_gt), others, mine, ALU.is_gt)
            st(v.tensor_tensor(c4(cmp_eq), others, mine, ALU.is_equal))
            dve.wait_ge(route_consts, 3)
            st(v.tensor_tensor(c4(cmp_eq), c4(cmp_eq), bc(lower_e[:, :, :].unsqueeze(1), [TP, T, NE, NE]), ALU.mult))
            st(v.tensor_tensor(cmp_gt[:], cmp_gt[:], cmp_eq[:], ALU.add))
            st(v.tensor_reduce(rank[:], cmp_gt[:], AX_X, ALU.add))
            v.tensor_scalar(is_k[:, 0, :], rank[:], 0.0, None, ALU.is_equal)
            v.tensor_scalar(is_k[:, 1, :], rank[:], 1.0, None, ALU.is_equal)
            st(v.tensor_scalar(routed[:], rank[:], float(TOPK), None, ALU.is_lt))
            st(v.tensor_tensor(wm[:], routed[:], prf, ALU.mult))
            st(v.scalar_tensor_tensor(out=wm[:], in0=routed[:], scalar=-1.0, in1=wm[:], op0=ALU.add, op1=ALU.add))

            v.memset(thr[:], 0)
            for j in range(3):
                last = v.memset(bits[:, j, :], (j + 1) << (2 * ROUNDS - 2))
            st(last)
            st(v.tensor_copy(cand[:], bits[:]))
            with dve.Fori(0, ROUNDS) as n:
                k = [0]

                def link(ins):
                    k[0] += 1
                    ins.then_inc(srch_step, 1)
                    dve.wait_ge(srch_step, n * SRCH + k[0])

                v.tensor_tensor(over[:, :, :].rearrange("p j (t e) -> p j t e", e=NE), bc(tv(wm[:, :]).unsqueeze(1), [TP, 3, T, NE]),
                                bc(cand[:, :, :].bitcast(F32).unsqueeze(2), [TP, 3, T, NE]), ALU.is_ge).then_inc(over_ready, 1)
                dve.wait_ge(over_out, n + 1)
                link(v.tensor_reduce(n_over[:], bank[0][0:TP, 0:3 * T * NE].rearrange("p (j t e) -> p j e t", j=3, t=T), AX_X, ALU.add))
                link(v.scalar_tensor_tensor(out=grown[:], in0=n_over[:], scalar=CAP - 0.5, in1=bc(bits[:, 0:1, :], [TP, 3, NE]),
                                            op0=ALU.is_ge, op1=ALU.mult))
                with nc.allow_low_precision(reason="up to three times a power of two: exact as an integer"):
                    link(v.tensor_reduce(more[:], grown[:, :, :].rearrange("p j e -> p e j"), AX_X, ALU.add))
                v.tensor_scalar(bits[:], bits[:], 2, None, ALU.logical_shift_right)
                link(v.tensor_tensor(thr[:], thr[:], more[:], ALU.bitwise_or))
                link(v.tensor_tensor(cand[:], bits[:], bc(thr[:, :].unsqueeze(1), [TP, 3, NE]), ALU.bitwise_or))

            thr_b = bc(thr[:, :].bitcast(F32).unsqueeze(1), shp)
            v.tensor_tensor(tv(above[:, :]), tv(wm[:, :]), thr_b, ALU.is_gt).then_inc(mask_ready, 1)
            v.tensor_tensor(tv(tied[:, :]), tv(wm[:, :]), thr_b, ALU.is_equal).then_inc(mask_ready, 1)
            dve.wait_ge(rank_out, 1)
            st(v.tensor_reduce(room[:, 0, :], bank[1][0:TP, 0:T * NE].rearrange("p (t e) -> p e t", t=T), AX_X, ALU.add))
            st(v.tensor_scalar(room[:, 1, :], room[:, 0, :], -1.0, float(CAP), ALU.mult, ALU.add))
            dve.wait_ge(rank_out, 2)
            st(v.tensor_tensor(tv(fits[:, 0, :]), tv(bank[2][0:TP, 0:T * NE]), bc(room[:, 1, :].unsqueeze(1), shp), ALU.is_lt))
            st(v.tensor_tensor(fits[:, 1, :], fits[:, 0, :], tied[:], ALU.mult))
            v.tensor_tensor(sel[:], fits[:, 1, :], above[:], ALU.add).then_inc(mask_ready, 1)
            dve.wait_ge(mask_ready, 3)
            v.tensor_tensor(p_sel[:], prf, sel[:], ALU.mult)
            dve.wait_ge(rank_out, 3)
            st(v.tensor_tensor(slot[:, 0, :], bank[3][0:TP, 0:T * NE], first_row[:], ALU.add))
            st(v.tensor_tensor(slot[:, 1, :], slot[:, 0, :], sel[:], ALU.mult))
            kf = [TP, TOPK, T * NE]
            v.tensor_tensor(pick[:, 0], is_k[:], bc(slot[:, 1:2, :], kf), ALU.mult)
            v.tensor_tensor(pick[:, 1], is_k[:], bc(sel[:, :].unsqueeze(1), kf), ALU.mult)
            st(v.tensor_tensor(pick[:, 2], is_k[:], bc(p_sel[:, :].unsqueeze(1), kf), ALU.mult))
            pk = lambda i: pick[:, i].rearrange("p k (t e) -> p (k t) e", e=NE)
            v.tensor_reduce(slot_k[:], pk(0), AX_X, ALU.add)
            v.tensor_reduce(comb_w[:], pk(2), AX_X, ALU.add)
            st(v.tensor_reduce(sel_k[:, 0, :], pk(1), AX_X, ALU.add))
            v.tensor_copy(gath_idx[:], slot_k[:])
            st(v.tensor_scalar(sel_k[:, 1, :], sel_k[:, 0, :], -1.0, 1.0, ALU.mult, ALU.add))
            st(v.tensor_tensor(scat_f[:, 0, :], sel_k[:, 1, :], trash[:], ALU.mult))
            st(v.tensor_tensor(scat_f[:, 1, :], scat_f[:, 0, :], slot_k[:], ALU.add))
            v.tensor_copy(scat_idx[:], scat_f[:, 1, :]).then_inc(idx_ready, 1)

            PH, PO = (bank[0], bank[1]), bank[4:8]

            def expert(e):
                dve.wait_ge(piece_out, e * NCH + NCH)
                for d in range(KD):
                    last = v.tensor_scalar(yT[:, d, :], PO[d][:, 0:SLOTS], b2T[:, ds(e * KD + d, 1)], None, ALU.add)
                last.then_inc(yT_ready, 1)
                dve.wait_ge(y_out, e * 2 + 2)
                dve.wait_ge(y_stored, (e + 1) * 16)
                v.tensor_copy(y[:, 1, :], PH[1][0:SB2, :]).then_inc(y_ready, 1)

            with dve.Fori(0, NE) as e:
                expert(e)

            for t in range(T):
                dve.wait_ge(got_in[t % 4], 32 * (t // 4 + 1))
                if t >= 4:
                    dve.wait_ge(stored[t % 4], 16 * (t // 4))
                v.scalar_tensor_tensor(out=part[:, t % 4, :], in0=got[:, t % 4, 0, :], scalar=comb_w[:, t:t + 1], in1=X[:, t, :],
                                       op0=ALU.mult, op1=ALU.add).then_inc(part_ready, 1)
                dve.wait_ge(part_ready, t + 1)
                v.scalar_tensor_tensor(out=res[:, t % 4, :], in0=got[:, t % 4, 1, :], scalar=comb_w[:, T + t:T + t + 1],
                                       in1=part[:, t % 4, :], op0=ALU.mult, op1=ALU.add).then_inc(res_ready, 1)


_INS = ['x', 'src', 'dst', 'edge_weight', 'L0_gnn_W', 'L0_gnn_alpha', 'L0_mix_W_qkv', 'L0_mix_random_matrix',
        'L0_mix_W_out', 'L0_mix_b_out', 'L0_ffn_gate_w', 'L0_ffn_gate_b', 'L0_ffn_w1', 'L0_ffn_b1', 'L0_ffn_w2',
        'L0_ffn_b2']
_OUTS = [((1250, 512), 'float32')]


def kernel(**inputs):
    import numpy as _np
    import concourse.bacc as _bacc
    from concourse import mybir as _mybir
    from concourse.bass_utils import run_bass_kernel_spmd as _run

    nc = _bacc.Bacc("TRN2", target_bir_lowering=False, num_devices=1)
    arrays, args = {}, []
    for name in _INS:
        a = _np.ascontiguousarray(inputs[name])
        if a.ndim == 0:
            a = a.reshape(1)
        arrays[f"in_{name}_dram"] = a
        args.append(nc.dram_tensor(f"in_{name}_dram", a.shape, _mybir.dt.from_np(a.dtype), kind="ExternalInput").ap())
    for i, (shape, dtype) in enumerate(_OUTS):
        dt = _mybir.dt.from_np(_np.dtype(dtype))
        args.append(nc.dram_tensor(f"out_{i}_dram", shape, dt, kind="ExternalOutput").ap())
    gps_layer(nc, *args)
    r = _run(nc, [arrays], core_ids=[0])
    got = tuple(r.results[0][f"out_{i}_dram"] for i in range(len(_OUTS)))
    return got[0]
```

```python
from contextlib import ExitStack

import concourse.bass as bass
from concourse import mybir

ALU = mybir.AluOpType
ACT = mybir.ActivationFunctionType
AX_X = mybir.AxisListType.X
F32 = mybir.dt.float32
F32R = mybir.dt.float32r
BF16 = mybir.dt.bfloat16
I32 = mybir.dt.int32
U32 = mybir.dt.uint32
P = 128


class Chain:

    def __init__(self, eng, sem):
        self.eng, self.sem, self.n = eng, sem, 0

    def __call__(self, ins):
        ins.then_inc(self.sem, 1)
        self.n += 1
        self.eng.wait_ge(self.sem, self.n)


class Region:

    def __init__(self, nc, start):
        self.nc, self.at = nc, -(-start // 32) * 32

    def __call__(self, name, shape, dt=F32):
        t = self.nc.alloc_sbuf_tensor_at(name, shape, dt, offset=self.at)
        size = mybir.dt.size(dt)
        for n in shape[1:]:
            size *= n
        self.at += -(-size // 32) * 32
        assert self.at <= self.nc.sbuf_usable_end, (name, self.at, self.nc.sbuf_usable_end)
        return t


def ds(start, size):
    return bass.ds(start, size)


def gps_layer(nc, x, src, dst, edge_weight, gnn_W, gnn_alpha, W_qkv, R_feat, W_out, b_out,
              gate_w, gate_b, w1, b1, w2, b2, out):
    N, D = x.shape
    E = src.shape[0]
    HD, FD = R_feat.shape
    NH = D // HD
    NE, _, HID = w1.shape
    TOPK = 2
    CAP = int(1.2 * N / NE)
    EPS = 1e-5

    TP = 125
    T = N // TP
    KD = D // P
    NF = NH * FD
    assert T * TP == N and TOPK == 2

    GC, WIN = 5, 26
    GE = GC * P
    FULL = E // GE
    TAIL = E - FULL * GE
    KEYS = T * WIN
    RING = 2
    PSR = 3
    GPI = 6
    TURNS = -(-E // (GE * GPI))
    G = TURNS * GPI
    assert GPI % RING == 0 and GPI % PSR == 0 and TURNS == T + 1 and 0 < TAIL and FULL < G
    NWIN = -(-N // WIN)
    AW = max(NWIN * WIN, N + WIN)

    SLOTS = 188
    SB = 96
    BLOCKS = (slice(0, SB), slice(SB, SLOTS))
    ROWS = 2 * SB
    TRASH = TOPK * N
    HT = HID // P
    CH = 4
    NCH = HT // CH
    NP = 2 * NCH
    WR = 4
    LEAD = WR - 1
    assert SLOTS >= CAP and CH == KD and WR == NCH

    xg_rows = nc.dram_tensor("xg_rows", (TRASH + NE * ROWS, D), F32, kind="Internal").ap()
    y_rows = nc.dram_tensor("y_rows", (NE * ROWS, D), F32, kind="Internal").ap()


    ctx = ExitStack()
    with ctx:
        def sem(name):
            return ctx.enter_context(nc.semaphore(name))

        bank = [ctx.enter_context(nc.psum_tensor(f"bank{i}", [P, 512], F32)) for i in range(8)]

        keep = Region(nc, nc.sbuf_base)
        X = keep("X", [TP, T + 1, D])
        ident = keep("ident", [P, P])
        ones_f = keep("ones_f", [P, 1])
        ones_b = keep("ones_b", [TP, TP], BF16)
        tri_b = keep("tri_b", [TP, TP], BF16)
        b1T = keep("b1T", [P, NE * HT])
        b2T = keep("b2T", [P, NE * KD])
        gwT = keep("gwT", [P, KD, NE])
        gate_b_all = keep("gate_b_all", [TP, NE])
        stats = keep("stats", [TP, T, 6])
        sd2 = keep("sd2", [TP, 1])
        rstd2 = keep("rstd2", [TP, 1])
        mv = keep("mv", [TP, T + 1, 2])
        sd = keep("sd", [TP, T])
        rstd = keep("rstd", [TP, T + 1])
        zero_c = keep("zero_c", [P, 1])
        lg = keep("lg", [TP, T, NE])
        eps_c = keep("eps_c", [TP, 1])
        scat_idx = keep("scat_idx", [TP, TOPK * T], U32)
        gath_idx = keep("gath_idx", [TP, TOPK * T], U32)
        comb_w = keep("comb_w", [TP, TOPK * T])

        graph = Region(nc, keep.at)
        A = graph("A", [TP, T, AW])
        Mq = graph("Mq", [P, KD, NF])
        Wo_lo = Region(nc, graph.at)("Wo_lo", [P, KD, D], F32R)
        Wo = graph("Wo", [P, KD, D])
        alpha_neg = graph("alpha_neg", [TP, 1])
        bo_all = graph("bo_all", [TP, D])
        iota_r = graph("iota_r", [P, P])
        iota_k = graph("iota_k", [P, KEYS])
        col_r = graph("col_r", [P, G, GC])
        col_key = graph("col_key", [P, G, GC])
        col_w = graph("col_w", [P, G, GC, 2])
        col_blk = graph("col_blk", [P, G, GC])
        col_dst = graph("col_dst", [P, G, GC])
        first_dst = graph("first_dst", [1, G], I32)
        flag = graph("flag", [1, 1], I32)
        KV = graph("KV", [P, 2, 260])

        shared = graph.at
        H_hi = graph("H_hi", [TP, T, D], F32R)
        QT = graph("QT", [P, 2, N])
        Wo_hi = Region(nc, graph.at)("Wo_hi", [P, KD, D], F32R)
        xnT = graph("xnT", [P, KD, TP])
        V = graph("V", [TP, D])
        Kf = graph("Kf", [TP, NF])
        k_min = graph("k_min", [TP, NF])
        k_exp = graph("k_exp", [TP, NF])
        q_min = graph("q_min", [P, 2 * TP])
        q_exp = graph("q_exp", [P, 2 * TP])
        graph = Region(nc, max(graph.at, shared + 4 * (KD * 2 * D * 2 + KD * D)))
        wcat_at = graph.at
        Wcat = graph("Wcat", [P, KD, 2 * D + NF])
        late = graph.at
        gen = Region(nc, graph.at)
        win_lo = gen("win_lo", [P, 1])
        gen_rel = gen("gen_rel", [P, GC])
        gen_in = gen("gen_in", [P, GC])
        gen_key = gen("gen_key", [P, GC])
        xn = graph("xn", [TP, D])
        src_w = graph("src_w", [P, RING, GC, 2 * P], F32R)
        key1h = graph("key1h", [P, RING, GC, KEYS], F32R)
        away = graph("away", [P, RING, GC, KEYS], BF16)
        h_lo_at = graph.at
        H_lo = graph("H_lo", [TP, T, D], F32R)

        first = Region(nc, shared)
        raw_qk = first("raw_qk", [P, KD, 2 * D])
        qkT = first("qkT", [P, 2 * KD, D])
        raw_g = first("raw_g", [P, KD, D])
        assert first.at <= wcat_at
        first = Region(nc, late)
        row_src = first("row_src", [G, GE], I32)
        row_dst = first("row_dst", [G, GE], I32)
        row_w = first("row_w", [G, GE])
        valid = first("valid", [G, GE])
        src_f = first("src_f", [G, GE])
        dst_f = first("dst_f", [G, GE])
        blk_i = first("blk_i", [G, GE], I32)
        blk_f = first("blk_f", [G, GE])
        r_f = first("r_f", [G, GE])
        rel = first("rel", [G, GE])
        inside = first("inside", [G, GE])
        key_f = first("key_f", [G, GE])
        w_hi = first("w_hi", [G, GE], F32R)
        w_lo = first("w_lo", [G, GE])
        n_in = first("n_in", [G, 1])
        gw_row = first("gw_row", [NE, D])
        Rbd = first("Rbd", [P, 2 * FD])
        b1_row = first("b1_row", [NE * HT, P])
        b2_row = first("b2_row", [NE * KD, P])
        zero_rows = first("zero_rows", [SB, D])

        second = Region(nc, late)
        Qt = second("Qt", [P, 2, TP])
        At = second("At", [TP, 2, T, TP], F32R)
        zn = second("zn", [TP, D])
        zrec = second("zrec", [TP, 2, NH])
        znT = second("znT", [P, 2, KD, TP], F32R)
        agg_pos = second("agg_pos", [TP, D])
        agg_neg = second("agg_neg", [TP, D])
        xn2_t = second("xn2_t", [TP, D])
        xn2T = second("xn2T", [P, KD, TP])
        assert second.at <= h_lo_at
        moe = Region(nc, keep.at)
        raw = moe("raw", [P, WR, CH, 512])
        parts = moe("parts", [P, WR, 2, CH, 512], F32R)
        over_ = moe.at
        shp = [TP, T, NE]
        flat = [TP, T * NE]
        mx = moe("mx", [TP, T])
        ex = moe("ex", shp)
        sm = moe("sm", [TP, 2, T])
        pr = moe("pr", shp)
        cmp_gt = moe("cmp_gt", [TP, T * NE, NE])
        cmp_eq = moe("cmp_eq", [TP, T * NE, NE])
        lower_e = moe("lower_e", [TP, NE, NE])
        rank = moe("rank", flat)
        counts = moe("counts", [TP, 3, T, 4 + NE])
        earlier = moe("earlier", shp)
        is_k = moe("is_k", [TP, TOPK, T * NE])
        routed = moe("routed", flat)
        wm = moe("wm", flat)
        bits = moe("bits", [TP, 3, NE], I32)
        thr = moe("thr", [TP, NE], I32)
        next_bits = moe("next_bits", [TP, 3, NE], I32)
        cand = moe("cand", [TP, 3, NE], I32)
        next_cand = moe("next_cand", [TP, 3, NE], I32)
        over = moe("over", [TP, 3, T * NE], BF16)
        n_over = moe("n_over", [TP, 3, NE])
        grown = moe("grown", [TP, 3, NE])
        more = moe("more", [TP, NE], I32)
        above = moe("above", flat, BF16)
        tied = moe("tied", flat, BF16)
        room = moe("room", [TP, 2, NE])
        fits = moe("fits", [TP, 2, T * NE])
        sel = moe("sel", flat, BF16)
        first_row = moe("first_row", [TP, 2, T * NE])
        slot_back = moe("slot_back", flat)
        slot = moe("slot", [TP, 2, T * NE])
        p_sel = moe("p_sel", flat)
        trash = moe("trash", [TP, TOPK * T])
        pick = moe("pick", [TP, 3, TOPK, T * NE])
        sel_k = moe("sel_k", [TP, 2, TOPK * T])
        slot_k = moe("slot_k", [TP, TOPK * T])
        scat_f = moe("scat_f", [TP, 2, TOPK * T])
        assert moe.at <= wcat_at
        rows2 = Region(nc, wcat_at)
        xn2 = rows2("xn2", [TP, T, D])
        em = Region(nc, over_)
        xgT = em("xgT", [P, KD, 2 * SLOTS], F32R)
        yT = em("yT", [P, KD, SLOTS])
        y_cross = em("y_cross", [P, KD, SLOTS])
        y = em("y", [SB, 2, D])
        pre = em("pre", [P, 4, SLOTS])
        assert em.at <= wcat_at
        got_low = Region(nc, wcat_at)("got_low", [TP, T, D])
        em = Region(nc, rows2.at)
        hid = em("hid", [P, HT, 2 * SLOTS], F32R)
        gel = em("gel", [P, 4, SLOTS])
        xg = em("xg", [SB, 2, D])
        cm = Region(nc, keep.at)
        got = cm("got", [TP, T, D])
        res = cm("res", [TP, T, D])
        assert cm.at <= over_

        rows_zeroed = sem("rows_zeroed"); edges_in = sem("edges_in"); x_in = sem("x_in")
        qk_in = sem("qk_in"); r_in = sem("r_in"); g_in = sem("g_in"); v_in = sem("v_in")
        small_in = sem("small_in"); wo_in = sem("wo_in"); bo_in = sem("bo_in")
        ident_made = sem("ident_made"); consts_made = sem("consts_made"); A_step = sem("A_step")
        xg_zeroed = sem("xg_zeroed")
        edge_step = sem("edge_step"); ln_step = sem("ln_step"); std_done = sem("std_done")
        pe_setup = sem("pe_setup"); act_setup = sem("act_setup")
        xn_ready = sem("xn_ready"); xnT_out = sem("xnT_out"); xnT_ready = sem("xnT_ready")
        h_out = sem("h_out"); h_ready = sem("h_ready"); v_out = sem("v_out"); v_ready = sem("v_ready")
        k_out = sem("k_out"); kmin_ready = sem("kmin_ready"); kexp_ready = sem("kexp_ready")
        kf_ready = sem("kf_ready"); q_out = sem("q_out"); qmin_ready = sem("qmin_ready")
        qexp_ready = sem("qexp_ready"); qt_ready = sem("qt_ready"); kv_out = sem("kv_out")
        away_ready = sem("away_ready"); square_ready = sem("square_ready")
        key_ready = sem("key_ready"); src_ready = sem("src_ready"); grp_out = sem("grp_out")
        gen_step = sem("gen_step"); gen_w = sem("gen_w"); waited_apart = sem("waited_apart"); gen_out = sem("gen_out"); A_final = sem("A_final")
        kv_ready = sem("kv_ready")
        wo_hi_ready = sem("wo_hi_ready"); wo_ready = sem("wo_ready"); h_lo_ready = sem("h_lo_ready")
        qt_c = sem("qt_c"); at_hi_ready = sem("at_hi_ready"); at_lo_ready = sem("at_lo_ready"); z_out = sem("z_out")
        zrec_step = sem("zrec_step"); zn_ready = sem("zn_ready"); znT_out = sem("znT_out")
        znT_hi_ready = sem("znT_hi_ready"); znT_ready = sem("znT_ready")
        agg_out = sem("agg_out"); agg_parts = sem("agg_parts"); mix_out = sem("mix_out"); x2_step = sem("x2_step")
        x2_ready = sem("x2_ready")
        std2_done = sem("std2_done"); rstd2_ready = sem("rstd2_ready"); xn2_ready = sem("xn2_ready"); xn2_kept = sem("xn2_kept")
        xn2T_out = sem("xn2T_out"); xn2T_ready = sem("xn2T_ready"); gate_out = sem("gate_out"); lg_ready = sem("lg_ready")
        route_consts = sem("route_consts"); route_step = sem("route_step"); exp_ready = sem("exp_ready")
        over_ready = sem("over_ready"); over_out = sem("over_out"); srch_step = sem("srch_step")
        mask_ready = sem("mask_ready"); rank_out = sem("rank_out"); idx_ready = sem("idx_ready")
        pads_zeroed = sem("pads_zeroed"); routed_ready = sem("routed_ready"); count_step = sem("count_step"); is_k_ready = sem("is_k_ready")
        gath_ready = sem("gath_ready"); scattered_low = sem("scattered_low"); scattered_high = sem("scattered_high")
        raw_in = [sem(f"raw_in{i}") for i in range(WR)]
        w_hi_ready = sem("w_hi_ready"); w_lo_ready = sem("w_lo_ready"); w_end_hi = sem("w_end_hi"); w_end_ready = sem("w_end_ready"); piece_out = sem("piece_out")
        xg_in = sem("xg_in"); xgT_out = sem("xgT_out"); x_hi_ready = sem("x_hi_ready"); x_lo_ready = sem("x_lo_ready")
        hid_out = sem("hid_out"); pre_ready = sem("pre_ready"); hid_hi_ready = sem("hid_hi_ready")
        hid_lo_ready = sem("hid_lo_ready"); gelu_done = sem("gelu_done"); y_cross_ready = sem("y_cross_ready"); yT_ready = sem("yT_ready")
        y_out = sem("y_out"); y_ready = sem("y_ready"); y_stored = sem("y_stored")
        got_low_in = [sem(f"got_low_in{i}") for i in range(2)]
        got_in = [sem(f"got_in{i}") for i in range(T)]
        part_ready = sem("part_ready"); res_ready = sem("res_ready")
        stored = sem("stored")

        EDGE_STEPS, EXP_AT, GEN_STEPS, SRCH, ROUNDS, ROUNDS_TURN = 8, 2, 8, 8, 15, 5
        S_QKT, S_EDGE = 0, 2 * KD
        S_MAP = S_EDGE + 7
        S_GT = S_MAP + 4
        S_SMALL = S_GT + KD
        N_SETUP = S_SMALL + 1
        block = ctx.enter_context(nc.Block())

        def bc(ap, shape):
            return ap.to_broadcast(shape)

        def row3(t):
            return t[:, :].rearrange("g (c p) -> g c p", c=GC)

        @block.sync
        def _(sp):
            sp.wait_ge(rows_zeroed, 1)
            for row, vec in ((row_src, src), (row_dst, dst), (row_w, edge_weight)):
                sp.dma_start(row[0:FULL, :], vec[0:FULL * GE].rearrange("(g e) -> g e", e=GE)).then_inc(edges_in, 16)
                sp.dma_start(row[FULL:FULL + 1, 0:TAIL], vec[FULL * GE:E].rearrange("(a e) -> a e", a=1)).then_inc(edges_in, 16)
            sp.dma_start(raw_qk[:], W_qkv[:, 0:2 * D].rearrange("(k p) n -> p k n", p=P)).then_inc(qk_in, 16)
            sp.wait_ge(consts_made, 1)
            for j in range(2):
                sp.dma_start(Rbd[j * HD:(j + 1) * HD, j * FD:(j + 1) * FD], R_feat).then_inc(r_in, 16)
            for p in (slice(0, 112), slice(112, TP)):
                sp.dma_start(X[p, 0:T, :], x.rearrange("(t p) d -> p t d", p=TP)[p]).then_inc(x_in, 16)
            sp.dma_start(raw_g[:], gnn_W.rearrange("(k p) n -> p k n", p=P)).then_inc(g_in, 16)
            sp.dma_start(Wcat[:, :, D:2 * D], W_qkv[:, 2 * D:3 * D].rearrange("(k p) n -> p k n", p=P)).then_inc(v_in, 16)
            sp.dma_start(Wo[:], W_out.rearrange("(k p) n -> p k n", p=P)).then_inc(wo_in, 16)
            sp.dma_start(bo_all[:], b_out.partition_broadcast(TP)).then_inc(bo_in, 16)
            sp.dma_start(xg_rows[TRASH:, :].rearrange("(b p) d -> p b d", p=SB),
                         bc(zero_rows[:, :].unsqueeze(1), [SB, NE * ROWS // SB, D])).then_inc(xg_zeroed, 16)
            sp.wait_ge(x2_ready, T)

            def load_piece(e, c):
                if c < NCH:
                    part = w1[ds(e, 1), :, c * 512:(c + 1) * 512].rearrange("e (k p) h -> p (e k) h", p=P)
                else:
                    part = w2[ds(e, 1), (c - NCH) * 512:(c - NCH + 1) * 512, :].rearrange("e (j p) d -> p (e j) d", p=P)
                sp.dma_start(raw[:, c % WR], part).then_inc(raw_in[c % WR], 16)

            def load_xg(e):
                sp.dma_start(xg[:], xg_rows[ds(e * -ROWS + (TRASH + (NE - 1) * ROWS), ROWS), :].rearrange("(c p) d -> p c d", p=SB)).then_inc(xg_in, 16)

            def store_y(e):
                sp.wait_ge(y_ready, 2 * e + 4)
                sp.dma_start(y_rows[ds(e * ROWS, ROWS), :].rearrange("(c p) d -> p c d", p=SB), y[:]).then_inc(y_stored, 16)

            def expert(e, first, last_one):
                if not last_one:
                    sp.wait_ge(xgT_out, e * 2 + 2)
                    load_xg(e + 1)
                for c in range(NP):
                    ahead = c + LEAD + WR
                    if not last_one or ahead < NP:
                        sp.wait_ge(w_lo_ready, e * NP + (c + LEAD + 1))
                        sp.wait_ge(w_end_ready, e * NP + (c + LEAD + 1))
                        load_piece(e + ahead // NP, ahead % NP)
                    if c == 1 and not first:
                        store_y(e - 1)

            for c in range(WR):
                load_piece(0, c)
            def load_next(c):
                sp.wait_ge(w_lo_ready, c + 1)
                sp.wait_ge(w_end_ready, c + 1)
                load_piece(0, WR + c)

            load_next(0)
            sp.wait_ge(xg_zeroed, 16)
            sp.wait_ge(scattered_low, 16 * T)
            load_xg(0)
            for c in range(1, LEAD):
                load_next(c)
            sp.wait_ge(scattered_high, 16 * T)
            expert(0, True, False)
            with sp.Fori(1, NE - 1) as e:
                expert(e, False, False)
            expert(NE - 1, False, True)
            store_y(NE - 1)
            for t in range(T):
                sp.wait_ge(res_ready, t + 1)
                sp.dma_start(out[t * TP:(t + 1) * TP, :], res[:, t, :]).then_inc(stored, 16)
            sp.wait_ge(stored, 16 * T)

        @block.gpsimd
        def _(pool):
            g = nc.gpsimd
            for row in (row_src, row_dst, row_w):
                last = g.memset(row[:], 0)
            last.then_inc(rows_zeroed, 1)
            g.memset(ident[:], 0.0).then_inc(ident_made, 1)
            g.memset(valid[:], 1.0)
            g.memset(zero_rows[:], 0.0)
            g.memset(ones_f[:], 1.0)
            g.memset(Rbd[:], 0.0).then_inc(consts_made, 1)
            pool.wait_ge(consts_made, 1)
            g.affine_select(out=ident[:], in_=ident[:], compare_op=ALU.not_equal, fill=1.0, base=0,
                            pattern=[[-1, P]], channel_multiplier=1).then_inc(ident_made, 1)
            g.affine_select(out=valid[:], in_=valid[:], compare_op=ALU.is_gt, fill=0.0, base=E,
                            pattern=[[-1, GE]], channel_multiplier=-GE).then_inc(consts_made, 1)
            g.iota(iota_r[:], [[1, P]], base=0, channel_multiplier=0, allow_small_or_imprecise_dtypes=True)
            g.iota(iota_k[:], [[1, KEYS]], base=0, channel_multiplier=0, allow_small_or_imprecise_dtypes=True)
            g.memset(eps_c[:], EPS)
            g.memset(zero_c[:], 0.0)
            g.memset(X[:, T, :], 0.0)
            g.memset(mv[:, T, :], 0.0)
            g.memset(rstd[:, T:T + 1], 0.0)
            g.memset(KV[:], 0.0)
            g.memset(ones_b[:], 1.0)
            g.memset(tri_b[:], 1.0).then_inc(consts_made, 1)
            pool.wait_ge(consts_made, 3)
            g.affine_select(out=tri_b[:], in_=tri_b[:], compare_op=ALU.is_gt, fill=0.0, base=0,
                            pattern=[[1, TP]], channel_multiplier=-1).then_inc(consts_made, 1)
            g.memset(A[:], 0.0).then_inc(A_step, 1)

            def distances(gi, s):
                g.tensor_tensor(away[:, s], bc(iota_k[:, :].unsqueeze(1), [P, GC, KEYS]),
                                bc(col_key[:, ds(gi, 1), :].rearrange("p a c -> p (a c)").unsqueeze(2), [P, GC, KEYS]),
                                ALU.subtract).then_inc(away_ready, 1)

            pool.wait_ge(act_setup, S_MAP)
            for s in range(RING):
                distances(s, s)
            with pool.Fori(1, G // RING) as n:
                for s in range(RING):
                    pool.wait_ge(key_ready, n * RING + (s + 1 - RING))
                    distances(n * RING + s, s)

            pool.wait_ge(x2_ready, T)
            g.memset(lower_e[:], 1.0).then_inc(route_consts, 1)
            pool.wait_ge(route_consts, 1)
            g.affine_select(out=lower_e[:], in_=lower_e[:], compare_op=ALU.is_gt, fill=0.0, base=0,
                            pattern=[[1, NE], [-1, NE]], channel_multiplier=0).then_inc(route_consts, 1)
            g.iota(first_row[:, 0, :], [[0, T], [-ROWS, NE]], base=TRASH + (NE - 1) * ROWS, channel_multiplier=0,
                   allow_small_or_imprecise_dtypes=True)
            g.iota(first_row[:, 1, :], [[0, T], [ROWS, NE]], base=0, channel_multiplier=0, allow_small_or_imprecise_dtypes=True)
            g.iota(trash[:], [[N, TOPK], [TP, T]], base=0, channel_multiplier=1,
                   allow_small_or_imprecise_dtypes=True).then_inc(route_consts, 1)
            g.memset(counts[:], 0.0).then_inc(pads_zeroed, 1)
            pool.wait_ge(pads_zeroed, 1)
            pool.wait_ge(routed_ready, 1)
            rt = routed[:, :].rearrange("p (t e) -> p t e", e=NE)
            zeros = bc(zero_c[0:TP, :].unsqueeze(2), shp)
            st = Chain(pool, count_step)
            st(g.tensor_tensor(counts[:, 0, :, 4:], rt, zeros, ALU.add))
            st(g.tensor_tensor(counts[:, 1, :, 4:], counts[:, 0, :, 4:], counts[:, 0, :, 3:3 + NE], ALU.add))
            st(g.tensor_tensor(counts[:, 2, :, 4:], counts[:, 1, :, 4:], counts[:, 1, :, 2:2 + NE], ALU.add))
            st(g.tensor_tensor(earlier[:], counts[:, 2, :, 4:], counts[:, 2, :, 0:NE], ALU.add))
            st(g.tensor_tensor(earlier[:], earlier[:], rt, ALU.subtract))
            k3 = lambda k: is_k[:, k, :].rearrange("p (t e) -> p t e", e=NE)
            st(g.tensor_tensor(k3(1), earlier[:], rt, ALU.mult))
            g.tensor_tensor(k3(0), rt, k3(1), ALU.subtract).then_inc(is_k_ready, 1)

            pool.wait_ge(idx_ready, 1)
            pool.wait_ge(xn2_kept, T)
            pool.wait_ge(xg_zeroed, 16)
            for k, done in enumerate((scattered_low, scattered_high)):
                rows = xg_rows if k == 0 else xg_rows[0:TRASH + (NE - 1) * ROWS, :]
                for t in range(T):
                    g.indirect_dma_start(out=rows, out_offset=bass.IndirectOffsetOnAxis(ap=scat_idx[:, k * T + t:k * T + t + 1], axis=0),
                                         in_=xn2[:, t, :], in_offset=None).then_inc(done, 16)

            def split_end(n, c):
                pool.wait_ge(w_hi_ready, (n * WR + c) * (CH - 1) + 1)
                g.tensor_tensor(parts[:, c, 0, CH - 1, :], raw[:, c, CH - 1, :], bc(zero_c[:, 0:1], [P, 512]), ALU.add).then_inc(w_end_hi, 1)
                pool.wait_ge(w_hi_ready, (n * WR + c) * (CH - 1) + (CH - 1))
                g.tensor_tensor(parts[:, c, 1, CH - 2, :], raw[:, c, CH - 2, :], parts[:, c, 0, CH - 2, :].bitcast(F32), ALU.subtract)
                pool.wait_ge(w_end_hi, n * WR + (c + 1))
                g.tensor_tensor(parts[:, c, 1, CH - 1, :], raw[:, c, CH - 1, :], parts[:, c, 0, CH - 1, :].bitcast(F32),
                                ALU.subtract).then_inc(w_end_ready, 1)

            split_end(0, LEAD)
            with pool.Fori(1, NE * NP // WR) as n:
                for c in range(WR):
                    split_end(n, c)

            pool.wait_ge(gath_ready, 1)

            def gather(to, k, t, rows):
                return g.indirect_dma_start(out=to, out_offset=None, in_=rows,
                                            in_offset=bass.IndirectOffsetOnAxis(ap=gath_idx[:, k * T + t:k * T + t + 1], axis=0))

            pool.wait_ge(y_stored, 16 * NE)
            for t in range(T):
                gather(got_low[:, t, :], 0, t, y_rows[0:(NE - 1) * ROWS, :]).then_inc(got_low_in[2 * t // T], 16)
            pool.wait_ge(y_stored, 16 * (NE + 1))
            for t in range(T):
                gather(got[:, t, :], 1, t, y_rows).then_inc(got_in[t], 16)

        @block.tensor
        def _(pe):
            mm, tr = nc.tensor.matmul, nc.tensor.transpose

            def begin(k):
                if k >= 8:
                    pe.wait_ge(act_setup, k - 7)
                return bank[k % 8]

            pe.wait_ge(ident_made, 2)
            pe.wait_ge(consts_made, 1)
            pe.wait_ge(qk_in, 16)
            for s in range(2 * KD):
                ps = begin(S_QKT + s)
                for d in range(KD):
                    last = tr(ps[:, d * P:(d + 1) * P], raw_qk[:, d, s * P:(s + 1) * P], ident[:])
                last.then_inc(pe_setup, 1)
            pe.wait_ge(edge_step, EDGE_STEPS)
            for k, row in enumerate((r_f, key_f, w_hi, w_lo, blk_f, dst_f)):
                ps = begin(S_EDGE + k)
                for j in range(GC):
                    part = row[:, j * P:(j + 1) * P]
                    last = tr(ps[:, j * G:(j + 1) * G], part.bitcast(F32) if row is w_hi else part, ident[0:G, 0:G])
                last.then_inc(pe_setup, 1)
            ps = begin(S_EDGE + 6)
            tr(ps[0:1, 0:G], dst_f[:, 0:1], ident[0:G, 0:G])
            mm(ps[0:1, 128:129], n_in[:], ones_f[0:G, :], start=True, stop=True).then_inc(pe_setup, 1)
            pe.wait_ge(r_in, 32)
            for s in range(4):
                ps = begin(S_MAP + s)
                pe.wait_ge(act_setup, S_MAP)
                for d in range(2):
                    for f in range(KD):
                        row = (s % 2) * 2 + d
                        last = mm(ps[:, d * NF + f * 2 * FD:d * NF + (f + 1) * 2 * FD],
                                  qkT[:, (s // 2) * KD + f, row * P:(row + 1) * P], Rbd[:], start=True, stop=True)
                last.then_inc(pe_setup, 1)
            pe.wait_ge(g_in, 16)
            for s in range(KD):
                ps = begin(S_GT + s)
                for o in range(KD):
                    last = tr(ps[:, o * P:(o + 1) * P], raw_g[:, o, s * P:(s + 1) * P], ident[:])
                last.then_inc(pe_setup, 1)
            pe.wait_ge(small_in, 80)
            ps = begin(S_SMALL)
            tr(ps[:, 0:NE * HT], b1_row[:], ident[:])
            tr(ps[:, 128:128 + NE * KD], b2_row[:], ident[0:NE * KD, 0:NE * KD])
            for k in range(KD):
                last = tr(ps[:, 160 + k * NE:160 + (k + 1) * NE], gw_row[:, k * P:(k + 1) * P], ident[0:NE, 0:NE])
            last.then_inc(pe_setup, 1)
            pe.wait_ge(act_setup, N_SETUP)
            pe.wait_ge(v_in, 16)

            PT, PA, PB, PKV, PKS = bank[3], bank[4], bank[5], bank[6], bank[7]

            def products(ps, slot):
                for j in range(GC):
                    for part in range(2):
                        last = mm(ps[:, 0:KEYS], src_w[:, slot, j, part * P:(part + 1) * P], key1h[:, slot, j, :],
                                  start=(j == 0 and part == 0), stop=(j == GC - 1 and part == 1))
                return last

            def group(gi, s):
                pe.wait_ge(src_ready, gi + 1)
                pe.wait_ge(key_ready, gi + 1)
                products(bank[s % PSR], s % RING).then_inc(grp_out, 1)

            def tile_work(i, first):
                G_ = lambda s: group(i * GPI + s, s)
                pe.wait_ge(xn_ready, i + 1)
                for k in range(KD):
                    last = tr(PT[:, k * TP:(k + 1) * TP], xn[:, k * P:(k + 1) * P], ident[0:TP, 0:TP])
                last.then_inc(xnT_out, 1)
                G_(0)
                pe.wait_ge(xnT_ready, i + 1)

                def project(ps, cols, ks):
                    for k in ks:
                        last = mm(ps, xnT[:, k, :], Wcat[:, k, cols], start=(k == 0), stop=(k == KD - 1))
                    return last

                project(PA[0:TP, :], slice(0, D), (0, 1))
                G_(1)
                project(PA[0:TP, :], slice(0, D), (2, 3)).then_inc(h_out, 1)
                project(PB[0:TP, :], slice(D, 2 * D), (0,))
                G_(2)
                project(PB[0:TP, :], slice(D, 2 * D), (1, 2))
                G_(3)
                project(PB[0:TP, :], slice(D, 2 * D), (3,)).then_inc(v_out, 1)
                pe.wait_ge(h_lo_ready, i + 1)
                project(PA[0:TP, 0:NF], slice(2 * D, 2 * D + NF), range(KD)).then_inc(k_out, 1)
                G_(4)
                pe.wait_ge(v_ready, i + 1)
                for m in range(2):
                    for k in range(KD):
                        last = mm(PB[:, m * TP:(m + 1) * TP], Mq[:, k, m * P:(m + 1) * P], xnT[:, k, :],
                                  start=(k == 0), stop=(k == KD - 1))
                last.then_inc(q_out, 1)
                G_(5)
                pe.wait_ge(kf_ready, i + 1)
                for m in range(2):
                    mm(PKV[:, m * 256:(m + 1) * 256], Kf[:, m * P:(m + 1) * P], V[:, m * 256:(m + 1) * 256],
                       start=(first and m == 0), stop=False, skip_group_check=True)
                    last = mm(PKS[:, m:m + 1], Kf[:, m * P:(m + 1) * P], ones_f[0:TP, :],
                              start=(first and m == 0), stop=False, skip_group_check=True)
                last.then_inc(kv_out, 1)

            pe.nop().then_inc(grp_out, 1)
            tile_work(0, True)
            with pe.Fori(1, T) as i:
                tile_work(i, False)
            with pe.Fori(T, TURNS) as i:
                for s in range(GPI):
                    group(i * GPI + s, s)

            some = pe.value_load(flag[0:1, 0:1], min_val=0, max_val=G * GE)
            with pe.If(some):
                pe.nop().then_inc(gen_out, 1)
                with pe.Fori(0, NWIN * G) as n:
                    pe.wait_ge(gen_step, n * GEN_STEPS + 7)
                    products(bank[0], 0).then_inc(gen_out, 1)

            PZ, PN, PG, PM, PX, PL = bank[4], bank[5], bank[0], bank[1], bank[2], bank[7]
            SPLIT = ((0, 0), (0, 1), (1, 0))

            def gate(t):
                for k in range(KD):
                    last = mm(PL[0:TP, 0:NE], xn2T[:, k, :], gwT[:, k, :], start=(k == 0), stop=(k == KD - 1))
                last.then_inc(gate_out, 1)

            def turn_xn2(t):
                pe.wait_ge(xn2_ready, t + 1)
                for k in range(KD):
                    last = tr(PX[:, k * TP:(k + 1) * TP], xn2_t[:, k * P:(k + 1) * P], ident[0:TP, 0:TP])
                last.then_inc(xn2T_out, 1)

            def mix_tile(t, first):
                pe.wait_ge(qt_c, t + 1)
                for m in range(2):
                    mm(PZ[0:TP, m * 256:(m + 1) * 256], Qt[:, m, :], KV[:, m, 0:256], start=True, stop=True)
                    last = mm(PN[0:TP, m * 4:(m + 1) * 4], Qt[:, m, :], KV[:, m, 256:260], start=True, stop=True)
                last.then_inc(z_out, 1)
                if not first:
                    pe.wait_ge(agg_parts, t)
                for half in range(2):
                    pe.wait_ge(at_lo_ready, t * 2 + (half + 1))
                    for b in range(half * T // 2, (half + 1) * T // 2):
                        for n, (a, h) in enumerate(SPLIT):
                            last = mm(PG[0:TP, :], At[:, a, b, :], (H_hi, H_lo)[h][:, b, :], start=(b == 0 and n == 0),
                                      stop=(b == T - 1 and n == 2))
                    last.then_inc(agg_out, 1)
                    if half == 0:
                        pe.wait_ge(zn_ready, t + 1)
                        for k in range(KD):
                            last = tr(PT[:, k * TP:(k + 1) * TP], zn[:, k * P:(k + 1) * P], ident[0:TP, 0:TP])
                        last.then_inc(znT_out, 1)
                        if not first:
                            turn_xn2(t - 1)
                if not first:
                    pe.wait_ge(xn2T_ready, t)
                    gate(t - 1)
                pe.wait_ge(znT_ready, t + 1)
                if first:
                    pe.wait_ge(wo_ready, 1)
                for k in range(KD):
                    for n, (a, w) in enumerate(SPLIT):
                        last = mm(PM[0:TP, :], znT[:, a, k, :], (Wo_hi, Wo_lo)[w][:, k, :], start=(k == 0 and n == 0),
                                  stop=(k == KD - 1 and n == 2))
                last.then_inc(mix_out, 1)

            pe.wait_ge(kv_ready, 1)
            pe.wait_ge(A_final, 1)
            mix_tile(0, True)
            with pe.Fori(1, T) as t:
                mix_tile(t, False)
            turn_xn2(T - 1)
            pe.wait_ge(xn2T_ready, T)
            gate(T - 1)

            pe.wait_ge(consts_made, 4)
            with pe.Fori(0, ROUNDS) as n:
                pe.wait_ge(over_ready, n + 1)
                mm(bank[0][0:TP, 0:3 * T * NE], ones_b[:], over[:, :, :].rearrange("p j f -> p (j f)"),
                   start=True, stop=True).then_inc(over_out, 1)

            def ranks(ps, mask):
                mm(ps[0:TP, 0:T * NE], tri_b[:], mask[:], start=True, stop=False, skip_group_check=True)
                for s in range(1, T):
                    last = mm(ps[0:TP, s * NE:T * NE], ones_b[:], mask[:, 0:(T - s) * NE], start=False,
                              stop=(s == T - 1), skip_group_check=True)
                last.then_inc(rank_out, 1)

            pe.wait_ge(mask_ready, 2)
            mm(bank[1][0:TP, 0:T * NE], ones_b[:], above[:], start=True, stop=True).then_inc(rank_out, 1)
            ranks(bank[2], tied)
            pe.wait_ge(mask_ready, 3)
            ranks(bank[3], sel)

            PH, PX, PO = (bank[0], bank[1], bank[4]), (bank[2], bank[3]), (*bank[5:8], bank[4])
            WIDE = max(SLOTS, 256)

            def turn_in(e):
                pe.wait_ge(xg_in, (e + 1) * 16)
                for h in range(2):
                    for k in range(2):
                        for c in range(2):
                            n = BLOCKS[c].stop - BLOCKS[c].start
                            o = k * SLOTS + c * SB
                            last = tr(PX[h][:, o:o + n], xg[0:n, c, (2 * h + k) * P:(2 * h + k + 1) * P], ident[0:n, 0:n])
                    last.then_inc(xgT_out, 1)

            def turn_out(e):
                pe.wait_ge(yT_ready, e + 1)
                for c in range(2):
                    for d in range(KD):
                        last = tr(PX[c][0:BLOCKS[c].stop - BLOCKS[c].start, d * P:(d + 1) * P], yT[:, d, BLOCKS[c]], ident[:])
                    last.then_inc(y_out, 1)

            def split_product(ps, slot, row, col, moving, start, stop):
                cols = slice(col * P, (col + 1) * P)
                mm(ps[:, 0:2 * SLOTS], parts[:, slot, 0, row, cols], moving, start=start, stop=False, skip_group_check=True)
                return mm(ps[:, 0:WIDE], parts[:, slot, 1, row, cols], moving[:, 0:WIDE], start=False, stop=stop,
                          skip_group_check=True)

            def expert(e, first, last_one):
                for c in range(NP):
                    pe.wait_ge(w_lo_ready, e * NP + (c + 1))
                    pe.wait_ge(w_end_ready, e * NP + (c + 1))
                    if c == 0:
                        pe.wait_ge(x_hi_ready, e * 2 + 2)
                        pe.wait_ge(x_lo_ready, e * 2 + 2)
                    if c == NP - 1 and not last_one:
                        pe.wait_ge(y_ready, e * 2 + 2)
                        turn_in(e + 1)
                    for j in range(CH):
                        if c < NCH:
                            q = CH * c + j
                            pe.wait_ge(pre_ready, e * HT + (q + 1))
                            if q == 2 and not first:
                                pe.wait_ge(yT_ready, e)
                            for k in range(KD):
                                last = split_product(PH[q % 3], c % WR, k, j, xgT[:, k, :], k == 0, k == KD - 1)
                            last.then_inc(hid_out, 1)
                        else:
                            q = CH * (c - NCH) + j
                            if q % 2 == 0:
                                pe.wait_ge(hid_lo_ready, e * (HT // 2) + (q // 2 + 1))
                            for d in range(KD):
                                if q == 0 and d == KD - 1:
                                    pe.wait_ge(pre_ready, e * HT + (HT + 2))
                                last = split_product(PO[d], c % WR, j, d, hid[:, q, :], q == 0, q == HT - 1)
                    if c >= NCH:
                        last.then_inc(piece_out, 1)
                    if c == 0 and not first:
                        turn_out(e - 1)

            turn_in(0)
            expert(0, True, False)
            with pe.Fori(1, NE - 1) as e:
                expert(e, False, False)
            expert(NE - 1, False, True)
            turn_out(NE - 1)

        @block.scalar
        def _(act):
            av = nc.scalar.activation

            act.dma_start(b1_row[:], b1.rearrange("e (j p) -> (e j) p", p=P)).then_inc(small_in, 16)
            act.dma_start(b2_row[:], b2.rearrange("e (j p) -> (e j) p", p=P)).then_inc(small_in, 16)
            act.dma_start(gw_row[:], gate_w).then_inc(small_in, 16)
            act.dma_start(gate_b_all[:], gate_b.partition_broadcast(TP)).then_inc(small_in, 16)
            act.dma_start(alpha_neg[:], gnn_alpha.partition_broadcast(TP)).then_inc(small_in, 16)

            def take(k):
                act.wait_ge(pe_setup, k + 1)
                return bank[k % 8]

            def square(gi, s):
                act.wait_ge(away_ready, gi + 1)
                av(away[:, s % RING], away[:, s % RING], ACT.Square).then_inc(square_ready, 1)

            def one_hot(gi, s, free=None):
                act.wait_ge(square_ready, gi + 1)
                if free is not None:
                    act.wait_ge(grp_out, free)
                av(key1h[:, s % RING], away[:, s % RING], ACT.Relu, bias=1.0, scale=-1.0).then_inc(key_ready, 1)

            for s in range(2 * KD):
                ps = take(S_QKT + s)
                av(qkT[:, s, :], ps[:], ACT.Copy).then_inc(act_setup, 1)
            for k, col in enumerate((col_r[:], col_key[:], col_w[:, :, :, 0], col_w[:, :, :, 1], col_blk[:], col_dst[:])):
                ps = take(S_EDGE + k)
                av(col, ps[:, 0:GC * G].rearrange("p (c g) -> p g c", c=GC), ACT.Copy).then_inc(act_setup, 1)
            ps = take(S_EDGE + 6)
            av(first_dst[:], ps[0:1, 0:G], ACT.Copy)
            av(flag[:], ps[0:1, 128:129], ACT.Relu, bias=float(G * GE), scale=-1.0).then_inc(act_setup, 1)
            for s in range(4):
                ps = take(S_MAP + s)
                half = slice((s % 2) * 2, (s % 2) * 2 + 2)
                to = Mq[:, half, :] if s < 2 else Wcat[:, half, 2 * D:]
                av(to, ps[:].rearrange("p (d n) -> p d n", d=2), ACT.Copy).then_inc(act_setup, 1)
                if s < RING:
                    square(s, s)
                elif s == RING:
                    act.wait_ge(ln_step, 2)
                    act.wait_ge(consts_made, 3)
                    av(sd[:], mv[:, 0:T, 1], ACT.Sqrt, bias=eps_c[:]).then_inc(std_done, 1)
                    av(sd2[:], eps_c[:], ACT.Exp)
            one_hot(0, 0)
            for s in range(KD):
                ps = take(S_GT + s)
                av(Wcat[:, s, 0:D], ps[:], ACT.Copy).then_inc(act_setup, 1)
            ps = take(S_SMALL)
            av(b1T[:], ps[:, 0:NE * HT], ACT.Copy)
            av(b2T[:], ps[:, 128:128 + NE * KD], ACT.Copy)
            av(gwT[:, :, :], ps[:, 160:160 + KD * NE].rearrange("p (k e) -> p k e", k=KD), ACT.Copy).then_inc(act_setup, 1)

            PT, PA, PB, PKV, PKS = bank[3], bank[4], bank[5], bank[6], bank[7]

            def ahead(i, s, last_turn=False):
                gi = i * GPI
                if not last_turn or s + 1 < GPI:
                    one_hot(gi + (s + 1), s + 1, gi + (s + 1))
                if not last_turn or s + 2 < GPI:
                    square(gi + (s + 2), s + 2)

            with act.Fori(0, T) as i:
                act.wait_ge(xnT_out, i + 1)
                av(xnT[:], PT[:, 0:KD * TP].rearrange("p (k t) -> p k t", k=KD), ACT.Copy).then_inc(xnT_ready, 1)
                ahead(i, 0)
                ahead(i, 1)
                act.wait_ge(h_out, i + 1)
                av(H_hi[:, ds(i, 1), :].rearrange("p a d -> p (a d)"), PA[0:TP, :], ACT.Copy).then_inc(h_ready, 1)
                ahead(i, 2)
                ahead(i, 3)
                act.wait_ge(v_out, i + 1)
                av(V[:], PB[0:TP, :], ACT.Copy).then_inc(v_ready, 1)
                one_hot(i * GPI + (GPI - 1), GPI - 1, i * GPI + (GPI - 1))
                act.wait_ge(kmin_ready, i + 1)
                av(k_exp[:], k_min[:], ACT.Exp).then_inc(kexp_ready, 1)
                square(i * GPI + GPI, 0)
                one_hot((i + 1) * GPI, 0, (i + 1) * GPI)
                act.wait_ge(qmin_ready, i + 1)
                av(q_exp[:], q_min[:], ACT.Exp).then_inc(qexp_ready, 1)
                square((i + 1) * GPI + 1, 1)
            for s in range(GPI):
                ahead(TURNS - 1, s, last_turn=True)

            act.wait_ge(kv_out, T)
            for m in range(2):
                for h in range(4):
                    p = slice(h * FD, (h + 1) * FD)
                    av(KV[p, m, h * HD:(h + 1) * HD], PKV[p, m * 256 + h * HD:m * 256 + (h + 1) * HD], ACT.Copy)
                    last = av(KV[p, m, 256 + h:257 + h], PKS[p, m:m + 1], ACT.Copy)
            last.then_inc(kv_ready, 1)

            PG, PX = bank[0], bank[2]
            act.wait_ge(wo_in, 16)
            act.wait_ge(qt_ready, T)
            av(Wo_hi[:], Wo[:], ACT.Copy).then_inc(wo_hi_ready, 1)
            act.wait_ge(A_final, 1)

            def at_hi(t, half):
                tiles = slice(half * T // 2, (half + 1) * T // 2)
                av(At[:, 0, tiles, :], A[:, tiles, ds(t * TP, TP)], ACT.Copy).then_inc(at_hi_ready, 1)

            def std2(t):
                act.wait_ge(x2_ready, t + 1)
                av(sd2[:], stats[:, 1, 1:2], ACT.Sqrt, bias=eps_c[:]).then_inc(std2_done, 1)

            def take_xn2(t):
                act.wait_ge(xn2_ready, t + 1)
                av(xn2[:, ds(t, 1), :].rearrange("p a d -> p (a d)"), xn2_t[:], ACT.Copy).then_inc(xn2_kept, 1)
                act.wait_ge(xn2T_out, t + 1)
                av(xn2T[:], PX[:, 0:KD * TP].rearrange("p (k t) -> p k t", k=KD), ACT.Copy).then_inc(xn2T_ready, 1)

            def mix_tile(t, first, last_one):
                if not first:
                    std2(t - 1)
                act.wait_ge(znT_out, t + 1)
                av(znT[:, 0], PT[:, 0:KD * TP].rearrange("p (k t) -> p k t", k=KD), ACT.Copy).then_inc(znT_hi_ready, 1)
                if not last_one:
                    act.wait_ge(agg_out, t * 2 + 1)
                    at_hi(t + 1, 0)
                if not first:
                    take_xn2(t - 1)
                if not last_one:
                    act.wait_ge(z_out, t + 1)
                    av(Qt[:], QT[:, :, ds((t + 1) * TP, TP)], ACT.Copy).then_inc(qt_c, 1)
                act.wait_ge(agg_out, t * 2 + 2)
                if not last_one:
                    at_hi(t + 1, 1)
                av(agg_pos[:], PG[0:TP, :], ACT.Relu)
                av(agg_neg[:], PG[0:TP, :], ACT.Relu, scale=-1.0).then_inc(agg_parts, 1)

            av(Qt[:], QT[:, :, 0:TP], ACT.Copy).then_inc(qt_c, 1)
            at_hi(0, 0)
            at_hi(0, 1)
            av(sd2[:], eps_c[:], ACT.Sqrt)
            mix_tile(0, True, False)
            with act.Fori(1, T - 1) as t:
                mix_tile(t, False, False)
            mix_tile(T - 1, False, True)
            std2(T - 1)
            take_xn2(T - 1)
            act.wait_ge(route_step, EXP_AT)
            av(ex[:], lg[:], ACT.Exp).then_inc(exp_ready, 1)

            PH, PX, PO = (bank[0], bank[1], bank[4]), (bank[2], bank[3]), (*bank[5:8], bank[4])

            def split_hi(e, c, j):
                if j == CH - 1:
                    return
                if j == 0:
                    act.wait_ge(raw_in[c % WR], (e * (NP // WR) + (c // WR + 1)) * 16)
                    if c < NCH:
                        act.wait_ge(piece_out, e * NCH + (c + 1))
                    else:
                        act.wait_ge(hid_out, e * HT + CH * (c - NCH + 1))
                av(parts[:, c % WR, 0, j, :], raw[:, c % WR, j, :], ACT.Copy).then_inc(w_hi_ready, 1)

            def x_hi(e):
                for h in range(2):
                    act.wait_ge(xgT_out, e * 2 + (h + 1))
                    av(xgT[:, 2 * h:2 * h + 2, 0:SLOTS], PX[h][:, 0:2 * SLOTS].rearrange("p (k c) -> p k c", k=2), ACT.Copy).then_inc(x_hi_ready, 1)

            def cross_y(e):
                act.wait_ge(piece_out, e * NCH + 2 * NCH)
                for d in range(KD):
                    av(y_cross[:, d, :], PO[d][:, SLOTS:2 * SLOTS], ACT.Identity, bias=b2T[:, ds(e * KD + d, 1)]).then_inc(y_cross_ready, 1)

            def take_y(e):
                act.wait_ge(y_out, e * 2 + 1)
                act.wait_ge(y_stored, (e + 1) * 16)
                av(y[:, 0, :], PX[0][0:SB, :], ACT.Copy).then_inc(y_ready, 1)

            def expert(e, first, last_one):
                if not first:
                    cross_y(e - 1)
                for c in range(NP):
                    for j in range(CH):
                        q = CH * c + j
                        if not last_one or c + LEAD < NP:
                            split_hi(e + (c + LEAD) // NP, (c + LEAD) % NP, j)
                        if c < NCH and j % 2 == 1:
                            two = slice(q % 4 - 1, q % 4 + 1)
                            for b in (q - 1, q):
                                act.wait_ge(pre_ready, e * HT + (b + 4))
                                gelu = av(gel[:, b % 4, :], pre[:, b % 4, :], ACT.Gelu, bias=b1T[:, ds(e * HT + b, 1)])
                            gelu.then_inc(gelu_done, 1)
                            act.wait_ge(gelu_done, e * (HT // 2) + (q // 2 + 1))
                            av(hid[:, q - 1:q + 1, 0:SLOTS], gel[:, two, :], ACT.Copy).then_inc(hid_hi_ready, 1)
                    if c == 1 and not first:
                        take_y(e - 1)
                    if c == NP - 1 and not last_one:
                        x_hi(e + 1)

            act.nop().then_inc(pre_ready, 3)
            act.nop().then_inc(y_ready, 2)
            act.nop().then_inc(y_stored, 16)
            act.nop().then_inc(piece_out, NCH)
            for c in range(LEAD):
                for j in range(CH):
                    split_hi(0, c, j)
                av(parts[:, c, 0, CH - 1, :], raw[:, c, CH - 1, :], ACT.Copy).then_inc(w_end_hi, 1)
            act.wait_ge(gath_ready, 1)
            x_hi(0)
            expert(0, True, False)
            with act.Fori(1, NE - 1) as e:
                expert(e, False, False)
            expert(NE - 1, False, True)
            cross_y(NE - 1)
            take_y(NE - 1)

        @block.vector
        def _(dve):
            v = nc.vector

            step = Chain(dve, edge_step)
            dve.wait_ge(edges_in, 96)
            v.tensor_copy(w_hi[:], row_w[:])
            v.tensor_copy(src_f[:], row_src[:])
            step(v.tensor_copy(dst_f[:], row_dst[:]))
            v.tensor_tensor(w_lo[:], row_w[:], w_hi[:].bitcast(F32), ALU.subtract)
            v.tensor_scalar(blk_i[:], src_f[:], 1.0 / TP, -((TP - 1) / 2) / TP, ALU.mult, ALU.add)
            step(v.tensor_scalar(rel[:], dst_f[:], dst_f[:, 0:1], None, ALU.subtract))
            dve.wait_ge(consts_made, 2)
            v.tensor_copy(blk_f[:], blk_i[:])
            step(v.tensor_tensor(rel[:], rel[:], valid[:], ALU.mult))
            v.scalar_tensor_tensor(out=r_f[:], in0=blk_f[:], scalar=-float(TP), in1=src_f[:], op0=ALU.mult, op1=ALU.add)
            step(v.tensor_scalar(inside[:], rel[:], 0.0, None, ALU.is_ge))
            step(v.scalar_tensor_tensor(out=inside[:], in0=rel[:], scalar=float(WIN), in1=inside[:], op0=ALU.is_lt, op1=ALU.mult))
            v.tensor_reduce(n_in[:], inside[:], AX_X, ALU.add)
            step(v.scalar_tensor_tensor(out=key_f[:], in0=blk_f[:], scalar=float(WIN), in1=rel[:], op0=ALU.mult, op1=ALU.add))
            step(v.scalar_tensor_tensor(out=key_f[:], in0=key_f[:], scalar=1.0, in1=inside[:], op0=ALU.add, op1=ALU.mult))
            step(v.tensor_scalar(key_f[:], key_f[:], -1.0, None, ALU.add))
            assert step.n == EDGE_STEPS

            ln = Chain(dve, ln_step)
            dve.wait_ge(x_in, 32)
            for t in range(T):
                last = v.bn_stats(stats[:, t, :], X[:, t, :])
            ln(last)
            for t in range(T):
                last = v.bn_aggr(mv[:, t, :], stats[:, t, :])
            ln(last)
            dve.wait_ge(std_done, 1)
            dve.wait_ge(consts_made, 3)
            ln(v.reciprocal(rstd[:, 0:T], sd[:]))

            PT, PA, PB = bank[3], bank[4], bank[5]

            def wait_apart(sem, value):
                dve.wait_ge(sem, value)
                dve.sem_inc(waited_apart, 1)

            def sources(gi, slot):
                for j in range(GC):
                    last = v.scalar_tensor_tensor(
                        out=src_w[:, slot, j, :].rearrange("p (a k) -> p a k", a=2),
                        in0=bc(iota_r[:, :].unsqueeze(1), [P, 2, P]),
                        scalar=col_r[:, ds(gi, 1), j],
                        in1=bc(col_w[:, ds(gi, 1), j, :].rearrange("p a w -> p (a w)").unsqueeze(2), [P, 2, P]),
                        op0=ALU.is_equal, op1=ALU.mult)
                return last

            def add_group(gi, s):
                at = dve.value_load(first_dst[0:1, ds(gi, 1)], min_val=0, max_val=N - 1)
                dve.wait_ge(grp_out, gi + 2)
                dve.wait_ge(A_step, gi + 1)
                win = A[:, :, ds(at, WIN)]
                v.tensor_tensor(win, win, bank[s % PSR][0:TP, 0:KEYS].rearrange("p (b w) -> p b w", b=T), ALU.add).then_inc(A_step, 1)

            dve.wait_ge(act_setup, S_MAP)
            dve.wait_ge(edge_step, EDGE_STEPS)

            def norm_tile(i):
                v.tensor_scalar(xn[:], X[:, ds(i, 1), :].rearrange("p a d -> p (a d)"), mv[:, ds(i, 1), 0], rstd[:, ds(i, 1)],
                                ALU.subtract, ALU.mult).then_inc(xn_ready, 1)

            norm_tile(0)
            sources(0, 0).then_inc(src_ready, 1)
            dve.wait_ge(small_in, 80)
            ln(v.tensor_scalar(alpha_neg[:], alpha_neg[:], -1.0, None, ALU.mult))
            dve.wait_ge(xg_zeroed, 16)
            with dve.Fori(0, T) as i:
                for s in range(GPI):
                    if s == 5:
                        dve.wait_ge(kexp_ready, i + 1)
                        v.scalar_tensor_tensor(out=Kf[:], in0=PA[0:TP, 0:NF], scalar=0.0, in1=k_exp[:],
                                               op0=ALU.max, op1=ALU.add).then_inc(kf_ready, 1)
                    sources(i * GPI + (s + 1), (s + 1) % RING).then_inc(src_ready, 1)
                    if s == 2:
                        dve.wait_ge(h_ready, i + 1)
                        at_i = (slice(None), ds(i, 1), slice(None))
                        v.tensor_tensor(H_lo[at_i].rearrange("p a d -> p (a d)"), PA[0:TP, :],
                                        H_hi[at_i].rearrange("p a d -> p (a d)").bitcast(F32), ALU.subtract).then_inc(h_lo_ready, 1)
                    if s == 4:
                        dve.wait_ge(k_out, i + 1)
                        v.tensor_scalar(k_min[:], PA[0:TP, 0:NF], 0.0, None, ALU.min).then_inc(kmin_ready, 1)
                    if s == 5:
                        norm_tile(i + 1)
                        dve.wait_ge(q_out, i + 1)
                        v.tensor_scalar(q_min[:], PB[:, 0:2 * TP], 0.0, None, ALU.min).then_inc(qmin_ready, 1)
                    add_group(i * GPI + s, s)
                dve.wait_ge(qexp_ready, i + 1)
                v.scalar_tensor_tensor(out=QT[:, :, ds(i * TP, TP)], in0=PB[:, 0:2 * TP].rearrange("p (m t) -> p m t", m=2),
                                       scalar=0.0, in1=q_exp[:].rearrange("p (m t) -> p m t", m=2),
                                       op0=ALU.max, op1=ALU.add).then_inc(qt_ready, 1)
            for s in range(GPI):
                if s + 1 < GPI:
                    sources((TURNS - 1) * GPI + s + 1, (s + 1) % RING).then_inc(src_ready, 1)
                add_group((TURNS - 1) * GPI + s, s)
            dve.wait_ge(A_step, G + 1)

            some = dve.value_load(flag[0:1, 0:1], min_val=0, max_val=G * GE)
            with dve.If(some):
                v.memset(A[:], 0.0)
                v.memset(win_lo[:], -float(WIN)).then_inc(gen_w, 1)
                with dve.Fori(0, NWIN) as w:
                    dve.wait_ge(gen_w, w + 1)
                    v.tensor_scalar(win_lo[:], win_lo[:], float(WIN), None, ALU.add).then_inc(gen_w, 1)
                    wait_apart(gen_w, w + 2)
                    with dve.Fori(0, G) as gi:
                        n = w * G + gi
                        k = [0]

                        def link(ins):
                            k[0] += 1
                            ins.then_inc(gen_step, 1)
                            dve.wait_ge(gen_step, n * GEN_STEPS + k[0])

                        dcol = col_dst[:, ds(gi, 1), :].rearrange("p a c -> p (a c)")
                        bcol = col_blk[:, ds(gi, 1), :].rearrange("p a c -> p (a c)")
                        link(v.tensor_scalar(gen_rel[:], dcol, win_lo[:, 0:1], None, ALU.subtract))
                        link(v.tensor_scalar(gen_in[:], gen_rel[:], 0.0, None, ALU.is_ge))
                        link(v.scalar_tensor_tensor(out=gen_in[:], in0=gen_rel[:], scalar=float(WIN), in1=gen_in[:], op0=ALU.is_lt, op1=ALU.mult))
                        link(v.scalar_tensor_tensor(out=gen_key[:], in0=bcol, scalar=float(WIN), in1=gen_rel[:], op0=ALU.mult, op1=ALU.add))
                        link(v.scalar_tensor_tensor(out=gen_key[:], in0=gen_key[:], scalar=1.0, in1=gen_in[:], op0=ALU.add, op1=ALU.mult))
                        link(v.tensor_scalar(gen_key[:], gen_key[:], -1.0, None, ALU.add))
                        dve.wait_ge(gen_out, n + 1)
                        sources(gi, 0)
                        v.tensor_tensor(key1h[:, 0], bc(iota_k[:, :].unsqueeze(1), [P, GC, KEYS]),
                                        bc(gen_key[:, :].unsqueeze(2), [P, GC, KEYS]), ALU.is_equal).then_inc(gen_step, 1)
                        dve.wait_ge(gen_out, n + 2)
                        win = A[:, :, ds(w * WIN, WIN)]
                        v.tensor_tensor(win, win, bank[0][0:TP, 0:KEYS].rearrange("p (b w) -> p b w", b=T), ALU.add).then_inc(gen_step, 1)
                        dve.wait_ge(gen_step, n * GEN_STEPS + 8)
            v.nop().then_inc(A_final, 1)

            PZ, PN, PM, PL = bank[4], bank[5], bank[1], bank[7]
            dve.wait_ge(wo_hi_ready, 1)
            v.tensor_tensor(Wo_lo[:], Wo[:], Wo_hi[:].bitcast(F32), ALU.subtract).then_inc(wo_ready, 1)
            dve.wait_ge(bo_in, 16)

            def at_lo(t, half):
                dve.wait_ge(at_hi_ready, t * 2 + (half + 1))
                tiles = slice(half * T // 2, (half + 1) * T // 2)
                v.tensor_tensor(At[:, 1, tiles, :], A[:, tiles, ds(t * TP, TP)], At[:, 0, tiles, :].bitcast(F32),
                                ALU.subtract).then_inc(at_lo_ready, 1)

            def norm2(t):
                dve.wait_ge(std2_done, t + 1)
                v.reciprocal(rstd2[:], sd2[:]).then_inc(rstd2_ready, 1)
                dve.wait_ge(rstd2_ready, t + 1)
                v.tensor_scalar(xn2_t[:], X[:, ds(t, 1), :].rearrange("p a d -> p (a d)"), stats[:, 1, 0:1], rstd2[:],
                                ALU.subtract, ALU.mult).then_inc(xn2_ready, 1)

            def logits(t):
                dve.wait_ge(gate_out, t + 1)
                v.tensor_tensor(lg[:, ds(t, 1), :].rearrange("p a e -> p (a e)"), PL[0:TP, 0:NE], gate_b_all[:], ALU.add).then_inc(lg_ready, 1)

            def mix_tile(t, first, last_one):
                xt = X[:, ds(t, 1), :].rearrange("p a d -> p (a d)")
                dve.wait_ge(z_out, t + 1)
                v.tensor_scalar(zrec[:, 0, :], PN[0:TP, 0:NH], 1e-6, None, ALU.add).then_inc(zrec_step, 1)
                dve.wait_ge(zrec_step, t * 2 + 1)
                v.reciprocal(zrec[:, 1, :], zrec[:, 0, :]).then_inc(zrec_step, 1)
                dve.wait_ge(zrec_step, t * 2 + 2)
                v.tensor_tensor(zn[:, :].rearrange("p (h f) -> p h f", h=NH), PZ[0:TP, :].rearrange("p (h f) -> p h f", h=NH),
                                bc(zrec[:, 1, :].unsqueeze(2), [TP, NH, HD]), ALU.mult).then_inc(zn_ready, 1)
                if not first:
                    norm2(t - 1)
                v.tensor_tensor(xt, xt, bo_all[:], ALU.add).then_inc(x2_step, 1)
                dve.wait_ge(znT_hi_ready, t + 1)
                v.tensor_tensor(znT[:, 1], PT[:, 0:KD * TP].rearrange("p (k t) -> p k t", k=KD), znT[:, 0].bitcast(F32),
                                ALU.subtract).then_inc(znT_ready, 1)
                if not last_one:
                    at_lo(t + 1, 0)
                    at_lo(t + 1, 1)
                if not first:
                    logits(t - 1)
                dve.wait_ge(agg_parts, t + 1)
                dve.wait_ge(x2_step, t * 5 + 1)
                v.scalar_tensor_tensor(out=xt, in0=agg_neg[:], scalar=alpha_neg[:, 0:1], in1=xt, op0=ALU.mult, op1=ALU.add).then_inc(x2_step, 1)
                dve.wait_ge(x2_step, t * 5 + 2)
                v.tensor_tensor(xt, xt, agg_pos[:], ALU.add).then_inc(x2_step, 1)
                dve.wait_ge(x2_step, t * 5 + 3)
                dve.wait_ge(mix_out, t + 1)
                v.tensor_tensor(xt, xt, PM[0:TP, :], ALU.add).then_inc(x2_step, 1)
                wait_apart(x2_step, t * 5 + 4)
                v.bn_stats(stats[:, 0, :], xt).then_inc(x2_step, 1)
                wait_apart(x2_step, t * 5 + 5)
                v.bn_aggr(stats[:, 1, 0:2], stats[:, 0, :]).then_inc(x2_ready, 1)

            at_lo(0, 0)
            at_lo(0, 1)
            mix_tile(0, True, False)
            with dve.Fori(1, T - 1) as t:
                mix_tile(t, False, False)
            mix_tile(T - 1, False, True)
            norm2(T - 1)
            logits(T - 1)

            st = Chain(dve, route_step)

            def tv(ap):
                return ap.rearrange("p (t e) -> p t e", e=NE)

            dve.wait_ge(lg_ready, T)
            st(v.tensor_reduce(mx[:], lg[:], AX_X, ALU.max))
            st(v.tensor_tensor(lg[:], lg[:], bc(mx[:, :].unsqueeze(2), shp), ALU.subtract))
            assert st.n == EXP_AT
            dve.wait_ge(exp_ready, 1)
            st(v.tensor_reduce(sm[:, 0, :], ex[:], AX_X, ALU.add))
            st(v.reciprocal(sm[:, 1, :], sm[:, 0, :]))
            st(v.tensor_tensor(pr[:], ex[:], bc(sm[:, 1, :].unsqueeze(2), shp), ALU.mult))
            prf = pr[:, :, :].rearrange("p t e -> p (t e)")
            others = bc(pr[:, :, :].unsqueeze(2), [TP, T, NE, NE])
            mine = bc(pr[:, :, :].unsqueeze(3), [TP, T, NE, NE])
            c4 = lambda m: m[:, :, :].rearrange("p (t e) f -> p t e f", e=NE)
            v.tensor_tensor(c4(cmp_gt), others, mine, ALU.is_gt)
            st(v.tensor_tensor(c4(cmp_eq), others, mine, ALU.is_equal))
            dve.wait_ge(route_consts, 3)
            st(v.tensor_tensor(c4(cmp_eq), c4(cmp_eq), bc(lower_e[:, :, :].unsqueeze(1), [TP, T, NE, NE]), ALU.mult))
            st(v.tensor_tensor(cmp_gt[:], cmp_gt[:], cmp_eq[:], ALU.add))
            st(v.tensor_reduce(rank[:], cmp_gt[:], AX_X, ALU.add))
            v.tensor_scalar(routed[:], rank[:], float(TOPK), None, ALU.is_lt).then_inc(routed_ready, 1)
            dve.wait_ge(routed_ready, 1)
            st(v.tensor_tensor(wm[:], routed[:], prf, ALU.mult))
            st(v.scalar_tensor_tensor(out=wm[:], in0=routed[:], scalar=-1.0, in1=wm[:], op0=ALU.add, op1=ALU.add))

            v.memset(thr[:], 0)
            v.memset(more[:], 0)
            for j in range(3):
                top = (j + 1) << (2 * ROUNDS)
                v.memset(bits[:, j, :], top - (1 << 32) if top >= 1 << 31 else top)
                last = v.memset(cand[:, j, :], (j + 1) << (2 * ROUNDS - 2))
            st(last)
            with dve.Fori(0, ROUNDS // ROUNDS_TURN) as n:
                for r in range(ROUNDS_TURN):
                    k = [0]

                    def link(ins, wait=True):
                        k[0] += 1
                        ins.then_inc(srch_step, 1)
                        if wait:
                            dve.wait_ge(srch_step, n * (SRCH * ROUNDS_TURN) + (SRCH * r + k[0]))

                    v.tensor_tensor(over[:, :, :].rearrange("p j (t e) -> p j t e", e=NE), bc(tv(wm[:, :]).unsqueeze(1), [TP, 3, T, NE]),
                                    bc(cand[:, :, :].bitcast(F32).unsqueeze(2), [TP, 3, T, NE]), ALU.is_ge).then_inc(over_ready, 1)
                    link(v.tensor_tensor(thr[:], thr[:], more[:], ALU.bitwise_or), wait=False)
                    link(v.tensor_scalar(bits[:], bits[:], 2, None, ALU.logical_shift_right))
                    link(v.tensor_scalar(next_bits[:], bits[:], 2, None, ALU.logical_shift_right))
                    link(v.tensor_tensor(next_cand[:], next_bits[:], bc(thr[:, :].unsqueeze(1), [TP, 3, NE]), ALU.bitwise_or), wait=False)
                    dve.wait_ge(over_out, n * ROUNDS_TURN + (r + 1))
                    link(v.tensor_reduce(n_over[:], bank[0][0:TP, 0:3 * T * NE].rearrange("p (j t e) -> p j e t", j=3, t=T), AX_X, ALU.add))
                    link(v.scalar_tensor_tensor(out=grown[:], in0=n_over[:], scalar=CAP - 0.5, in1=bc(bits[:, 0:1, :], [TP, 3, NE]),
                                                op0=ALU.is_ge, op1=ALU.mult))
                    with nc.allow_low_precision(reason="up to three times a power of two: exact as an integer"):
                        link(v.tensor_reduce(more[:], grown[:, :, :].rearrange("p j e -> p e j"), AX_X, ALU.add))
                    link(v.tensor_tensor(cand[:], next_cand[:], bc(more[:, :].unsqueeze(1), [TP, 3, NE]), ALU.bitwise_or))
            st(v.tensor_tensor(thr[:], thr[:], more[:], ALU.bitwise_or))

            thr_b = bc(thr[:, :].bitcast(F32).unsqueeze(1), shp)
            v.tensor_tensor(tv(above[:, :]), tv(wm[:, :]), thr_b, ALU.is_gt).then_inc(mask_ready, 1)
            v.tensor_tensor(tv(tied[:, :]), tv(wm[:, :]), thr_b, ALU.is_equal).then_inc(mask_ready, 1)
            dve.wait_ge(rank_out, 1)
            st(v.tensor_reduce(room[:, 0, :], bank[1][0:TP, 0:T * NE].rearrange("p (t e) -> p e t", t=T), AX_X, ALU.add))
            st(v.tensor_scalar(room[:, 1, :], room[:, 0, :], -1.0, float(CAP), ALU.mult, ALU.add))
            dve.wait_ge(rank_out, 2)
            st(v.tensor_tensor(tv(fits[:, 0, :]), tv(bank[2][0:TP, 0:T * NE]), bc(room[:, 1, :].unsqueeze(1), shp), ALU.is_lt))
            st(v.tensor_tensor(fits[:, 1, :], fits[:, 0, :], tied[:], ALU.mult))
            v.tensor_tensor(sel[:], fits[:, 1, :], above[:], ALU.add).then_inc(mask_ready, 1)
            dve.wait_ge(mask_ready, 3)
            dve.wait_ge(rank_out, 3)
            st(v.tensor_tensor(slot[:, 0, :], bank[3][0:TP, 0:T * NE], first_row[:, 0, :], ALU.add))
            v.tensor_tensor(slot_back[:], bank[3][0:TP, 0:T * NE], first_row[:, 1, :], ALU.add)
            st(v.tensor_tensor(slot[:, 1, :], slot[:, 0, :], sel[:], ALU.mult))
            kf = [TP, TOPK, T * NE]
            dve.wait_ge(is_k_ready, 1)
            v.tensor_tensor(pick[:, 0], is_k[:], bc(slot[:, 1:2, :], kf), ALU.mult)
            st(v.tensor_tensor(pick[:, 1], is_k[:], bc(sel[:, :].unsqueeze(1), kf), ALU.mult))
            pk = lambda i: pick[:, i].rearrange("p k (t e) -> p (k t) e", e=NE)
            v.tensor_reduce(slot_k[:], pk(0), AX_X, ALU.add)
            st(v.tensor_reduce(sel_k[:, 0, :], pk(1), AX_X, ALU.add))
            st(v.tensor_scalar(sel_k[:, 1, :], sel_k[:, 0, :], -1.0, 1.0, ALU.mult, ALU.add))
            st(v.tensor_tensor(scat_f[:, 0, :], sel_k[:, 1, :], trash[:], ALU.mult))
            st(v.tensor_tensor(scat_f[:, 1, :], scat_f[:, 0, :], slot_k[:], ALU.add))
            v.tensor_copy(scat_idx[:], scat_f[:, 1, :]).then_inc(idx_ready, 1)

            PH, PX, PO = (bank[0], bank[1], bank[4]), (bank[2], bank[3]), (*bank[5:8], bank[4])

            def split_lo(e, c, j):
                if j < CH - 2:
                    dve.wait_ge(w_hi_ready, (e * NP + c) * (CH - 1) + (j + 1))
                    low = v.tensor_tensor(parts[:, c % WR, 1, j, :], raw[:, c % WR, j, :], parts[:, c % WR, 0, j, :].bitcast(F32), ALU.subtract)
                    if j == CH - 3:
                        low.then_inc(w_lo_ready, 1)

            def x_lo(e):
                for h in range(2):
                    dve.wait_ge(x_hi_ready, e * 2 + (h + 1))
                    k = slice(2 * h, 2 * h + 2)
                    v.tensor_tensor(xgT[:, k, SLOTS:], PX[h][:, 0:2 * SLOTS].rearrange("p (k c) -> p k c", k=2),
                                    xgT[:, k, 0:SLOTS].bitcast(F32), ALU.subtract).then_inc(x_lo_ready, 1)

            def hid_lo(e, q):
                dve.wait_ge(hid_hi_ready, e * (HT // 2) + (q // 2 + 1))
                v.tensor_tensor(hid[:, q:q + 2, SLOTS:], gel[:, q % 4:q % 4 + 2, :], hid[:, q:q + 2, 0:SLOTS].bitcast(F32),
                                ALU.subtract).then_inc(hid_lo_ready, 1)

            def add_y(e):
                dve.wait_ge(piece_out, e * NCH + 2 * NCH)
                for d in range(KD):
                    dve.wait_ge(y_cross_ready, e * KD + (d + 1))
                    last = v.tensor_tensor(yT[:, d, :], PO[d][:, 0:SLOTS], y_cross[:, d, :], ALU.add)
                last.then_inc(yT_ready, 1)

            def take_y(e):
                dve.wait_ge(y_out, e * 2 + 2)
                dve.wait_ge(y_stored, (e + 1) * 16)
                v.tensor_copy(y[0:SLOTS - SB, 1, :], PX[1][0:SLOTS - SB, :]).then_inc(y_ready, 1)

            def expert(e, first, last_one):
                if not first:
                    add_y(e - 1)
                for c in range(NP):
                    for j in range(CH):
                        q = CH * c + j
                        if c < NCH:
                            dve.wait_ge(hid_out, e * HT + (q + 1))
                            v.tensor_reduce(pre[:, q % 4, :], PH[q % 3][:, 0:2 * SLOTS].rearrange("p (a s) -> p s a", a=2),
                                            AX_X, ALU.add).then_inc(pre_ready, 1)
                        if c < NCH and j == 3:
                            hid_lo(e, q - 3)
                        if 0 < c <= NCH and j == 0:
                            hid_lo(e, q - 2)
                        if j > 0 and (not last_one or c + LEAD < NP):
                            split_lo(e + (c + LEAD) // NP, (c + LEAD) % NP, j - 1)
                    if c == 1 and not first:
                        take_y(e - 1)
                    if c == NP - 1 and not last_one:
                        x_lo(e + 1)

            for c in range(LEAD):
                for j in range(CH):
                    split_lo(0, c, j)
                for j in (CH - 2, CH - 1):
                    dve.wait_ge(*((w_hi_ready, (c + 1) * (CH - 1)) if j == CH - 2 else (w_end_hi, c + 1)))
                    low = v.tensor_tensor(parts[:, c, 1, j, :], raw[:, c, j, :], parts[:, c, 0, j, :].bitcast(F32), ALU.subtract)
                low.then_inc(w_end_ready, 1)

            v.tensor_tensor(p_sel[:], prf, sel[:], ALU.mult)
            st(v.tensor_tensor(slot[:, 1, :], slot_back[:], sel[:], ALU.mult))
            v.tensor_tensor(pick[:, 0], is_k[:], bc(slot[:, 1:2, :], kf), ALU.mult)
            st(v.tensor_tensor(pick[:, 2], is_k[:], bc(p_sel[:, :].unsqueeze(1), kf), ALU.mult))
            v.tensor_reduce(comb_w[:], pk(2), AX_X, ALU.add)
            st(v.tensor_reduce(slot_k[:], pk(0), AX_X, ALU.add))
            v.tensor_copy(gath_idx[:], slot_k[:]).then_inc(gath_ready, 1)
            x_lo(0)
            v.memset(y[:], 0.0)
            expert(0, True, False)
            with dve.Fori(1, NE - 1) as e:
                expert(e, False, False)
            expert(NE - 1, False, True)

            def add_low(half):
                dve.wait_ge(got_low_in[half], 16 * T // 2)
                for t in range(half * T // 2, (half + 1) * T // 2):
                    last = v.scalar_tensor_tensor(out=X[:, t, :], in0=got_low[:, t, :], scalar=comb_w[:, t:t + 1], in1=X[:, t, :],
                                                  op0=ALU.mult, op1=ALU.add)
                last.then_inc(part_ready, 1)

            add_low(0)
            add_y(NE - 1)
            take_y(NE - 1)
            add_low(1)
            dve.wait_ge(part_ready, 2)

            for t in range(T):
                dve.wait_ge(got_in[t], 16)
                v.scalar_tensor_tensor(out=res[:, t, :], in0=got[:, t, :], scalar=comb_w[:, T + t:T + t + 1],
                                       in1=X[:, t, :], op0=ALU.mult, op1=ALU.add).then_inc(res_ready, 1)


_INS = ['x', 'src', 'dst', 'edge_weight', 'L0_gnn_W', 'L0_gnn_alpha', 'L0_mix_W_qkv', 'L0_mix_random_matrix',
        'L0_mix_W_out', 'L0_mix_b_out', 'L0_ffn_gate_w', 'L0_ffn_gate_b', 'L0_ffn_w1', 'L0_ffn_b1', 'L0_ffn_w2',
        'L0_ffn_b2']
_OUTS = [((1250, 512), 'float32')]


def kernel(**inputs):
    import numpy as _np
    import concourse.bacc as _bacc
    from concourse import mybir as _mybir
    from concourse.bass_utils import run_bass_kernel_spmd as _run

    nc = _bacc.Bacc("TRN2", target_bir_lowering=False, num_devices=1)
    arrays, args = {}, []
    for name in _INS:
        a = _np.ascontiguousarray(inputs[name])
        if a.ndim == 0:
            a = a.reshape(1)
        arrays[f"in_{name}_dram"] = a
        args.append(nc.dram_tensor(f"in_{name}_dram", a.shape, _mybir.dt.from_np(a.dtype), kind="ExternalInput").ap())
    for i, (shape, dtype) in enumerate(_OUTS):
        dt = _mybir.dt.from_np(_np.dtype(dtype))
        args.append(nc.dram_tensor(f"out_{i}_dram", shape, dt, kind="ExternalOutput").ap())
    gps_layer(nc, *args)
    r = _run(nc, [arrays], core_ids=[0])
    got = tuple(r.results[0][f"out_{i}_dram"] for i in range(len(_OUTS)))
    return got[0]
```
